# Optimizing a Trainium2 kernel written in Bass

```python
import numpy as np
import jax
import jax.numpy as jnp

def _softmax(x, axis=-1):
    return jax.nn.softmax(x, axis=axis)

def _gelu(x):
    return jax.nn.gelu(x, approximate=True)

def _silu(x):
    return jax.nn.silu(x)

def _sigmoid(x):
    return jax.nn.sigmoid(x)

def _layernorm(x, axis=-1, eps=1e-05):
    m = jnp.mean(x, axis=axis, keepdims=True)
    v = jnp.var(x, axis=axis, keepdims=True)
    return (x - m) / jnp.sqrt(v + eps)

def _scatter_add(tgt, idx, src, axis=0):
    return tgt.at[idx].add(src)

def _segment_sum(src, seg, n):
    return jax.ops.segment_sum(src, seg, n)
kernel_name = 'mk_seq_postln_d1_jaxref_r4_9fe9e4'

def setup_inputs(seed: int=0):
    np.random.seed(seed)
    _w = jnp.asarray

    def _L0_attn_setup():
        import jax, jax.numpy as jnp
        import numpy as np
        D_MODEL = 256
        NUM_HEADS = 16
        D_HEAD = D_MODEL // NUM_HEADS
        LAMBDA_INIT = 0.8
        EPS = 1e-05
        B, N = (4, 256)
        key = jax.random.key(seed)
        ks = jax.random.split(key, 10)
        w_scale = 1.0 / np.sqrt(D_MODEL)
        d2 = 2 * D_HEAD * NUM_HEADS
        return {'X': jax.random.normal(ks[0], (B, N, D_MODEL), jnp.float32), 'Wq': jax.random.normal(ks[1], (d2, D_MODEL), jnp.float32) * w_scale, 'Wk': jax.random.normal(ks[2], (d2, D_MODEL), jnp.float32) * w_scale, 'Wv': jax.random.normal(ks[3], (d2, D_MODEL), jnp.float32) * w_scale, 'Wo': jax.random.normal(ks[4], (D_MODEL, d2), jnp.float32) * w_scale, 'lq1': jax.random.normal(ks[5], (NUM_HEADS, D_HEAD), jnp.float32), 'lk1': jax.random.normal(ks[6], (NUM_HEADS, D_HEAD), jnp.float32), 'lq2': jax.random.normal(ks[7], (NUM_HEADS, D_HEAD), jnp.float32), 'lk2': jax.random.normal(ks[8], (NUM_HEADS, D_HEAD), jnp.float32), 'rms_scale': jnp.ones((2 * D_HEAD,), jnp.float32)}
    _L0_attn_in = _L0_attn_setup()

    def _L0_ffn_setup():
        import jax, jax.numpy as jnp
        import numpy as np
        B, SEQ, DIM = (2, 1024, 256)
        E, S = (8, 128)
        HID = 4 * DIM
        SCALE = DIM ** 0.5

        def rmsnorm(x, gamma):
            n = jnp.linalg.norm(x, axis=-1, keepdims=True)
            return x / jnp.maximum(n, 1e-12) * SCALE * gamma
        key = jax.random.key(seed)
        ks = jax.random.split(key, 4)
        w_init = lambda k, shape: jax.random.normal(k, shape, dtype=jnp.float32) * 0.02
        return {'x': jax.random.normal(ks[0], (B, SEQ, DIM), dtype=jnp.float32), 'norm_gamma': jnp.ones((DIM,), jnp.float32), 'slot_norm_gamma': jnp.ones((DIM,), jnp.float32), 'slot_embeds': jax.random.normal(ks[1], (E, S, DIM), dtype=jnp.float32), 'w1': w_init(ks[2], (E, DIM, HID)), 'b1': jnp.zeros((E, HID), jnp.float32), 'w2': w_init(ks[3], (E, HID, DIM)), 'b2': jnp.zeros((E, DIM), jnp.float32)}
    _L0_ffn_in = _L0_ffn_setup()
    _d = {'L0_attn_X': _L0_attn_in['X'], 'L0_attn_Wq': _L0_attn_in['Wq'], 'L0_attn_Wk': _L0_attn_in['Wk'], 'L0_attn_Wv': _L0_attn_in['Wv'], 'L0_attn_Wo': _L0_attn_in['Wo'], 'L0_attn_lq1': _L0_attn_in['lq1'], 'L0_attn_lk1': _L0_attn_in['lk1'], 'L0_attn_lq2': _L0_attn_in['lq2'], 'L0_attn_lk2': _L0_attn_in['lk2'], 'L0_attn_rms_scale': _L0_attn_in['rms_scale'], 'L0_ffn_norm_gamma': _L0_ffn_in['norm_gamma'], 'L0_ffn_slot_norm_gamma': _L0_ffn_in['slot_norm_gamma'], 'L0_ffn_slot_embeds': _L0_ffn_in['slot_embeds'], 'L0_ffn_w1': _L0_ffn_in['w1'], 'L0_ffn_b1': _L0_ffn_in['b1'], 'L0_ffn_w2': _L0_ffn_in['w2'], 'L0_ffn_b2': _L0_ffn_in['b2']}
    _x0 = _d['L0_attn_X']
    _d['L0_attn_X'] = jax.random.normal(jax.random.fold_in(jax.random.key(seed), 1), (8, 512, 256), dtype=_x0.dtype)
    del _x0
    return _d

def reference(L0_attn_X, L0_attn_Wq, L0_attn_Wk, L0_attn_Wv, L0_attn_Wo, L0_attn_lq1, L0_attn_lk1, L0_attn_lq2, L0_attn_lk2, L0_attn_rms_scale, L0_ffn_norm_gamma, L0_ffn_slot_norm_gamma, L0_ffn_slot_embeds, L0_ffn_w1, L0_ffn_b1, L0_ffn_w2, L0_ffn_b2):

    def _L0_attn_ref(X, Wq, Wk, Wv, Wo, lq1, lk1, lq2, lk2, rms_scale):
        import jax, jax.numpy as jnp
        import numpy as np
        D_MODEL = 256
        NUM_HEADS = 16
        D_HEAD = D_MODEL // NUM_HEADS
        LAMBDA_INIT = 0.8
        EPS = 1e-05
        B, N = (4, 256)
        b, n, _ = X.shape
        H, dh = (NUM_HEADS, D_HEAD)

        def proj(W):
            return (X @ W.T).reshape(b, n, H, 2 * dh).transpose(0, 2, 1, 3)
        Q, K, V = (proj(Wq), proj(Wk), proj(Wv))
        Q1, Q2 = jnp.split(Q, 2, axis=-1)
        K1, K2 = jnp.split(K, 2, axis=-1)
        lam = jnp.exp(jnp.sum(lq1 * lk1, axis=-1)) - jnp.exp(jnp.sum(lq2 * lk2, axis=-1)) + LAMBDA_INIT
        lam = lam[None, :, None, None]
        scaling = 1.0 / np.sqrt(dh)
        causal = jnp.tril(jnp.ones((n, n), bool))
        A1 = jnp.where(causal, jnp.einsum('bhnd,bhmd->bhnm', Q1, K1) * scaling, -jnp.inf)
        A2 = jnp.where(causal, jnp.einsum('bhnd,bhmd->bhnm', Q2, K2) * scaling, -jnp.inf)
        attn = jax.nn.softmax(A1, axis=-1) - lam * jax.nn.softmax(A2, axis=-1)
        O = jnp.einsum('bhnm,bhmd->bhnd', attn, V)
        rms = jnp.sqrt(jnp.mean(O * O, axis=-1, keepdims=True) + EPS)
        O = O / rms * rms_scale * (1.0 - LAMBDA_INIT)
        Oc = O.transpose(0, 2, 1, 3).reshape(b, n, H * 2 * dh)
        return Oc @ Wo.T

    def _L0_ffn_ref(x, norm_gamma, slot_norm_gamma, slot_embeds, w1, b1, w2, b2):
        import jax, jax.numpy as jnp
        import numpy as np
        B, SEQ, DIM = (2, 1024, 256)
        E, S = (8, 128)
        HID = 4 * DIM
        SCALE = DIM ** 0.5

        def rmsnorm(x, gamma):
            n = jnp.linalg.norm(x, axis=-1, keepdims=True)
            return x / jnp.maximum(n, 1e-12) * SCALE * gamma
        xn = rmsnorm(x, norm_gamma)
        sn = rmsnorm(slot_embeds, slot_norm_gamma)
        logits = jnp.einsum('bnd,esd->bnes', xn, sn)
        dispatch = jax.nn.softmax(logits, axis=1)
        b, n, e, s = logits.shape
        combine = jax.nn.softmax(logits.reshape(b, n, e * s), axis=-1)
        slots = jnp.einsum('bnd,bnes->besd', xn, dispatch)
        h = jnp.einsum('besd,edh->besh', slots, w1) + b1[None, :, None, :]
        h = jax.nn.gelu(h, approximate=False)
        eo = jnp.einsum('besh,ehd->besd', h, w2) + b2[None, :, None, :]
        eo = eo.reshape(b, e * s, DIM)
        out = jnp.einsum('bmd,bnm->bnd', eo, combine)
        return out
    x = L0_attn_X
    x = _layernorm(x + _L0_attn_ref(x, L0_attn_Wq, L0_attn_Wk, L0_attn_Wv, L0_attn_Wo, L0_attn_lq1, L0_attn_lk1, L0_attn_lq2, L0_attn_lk2, L0_attn_rms_scale), axis=-1)
    x = _layernorm(x + _L0_ffn_ref(x, L0_ffn_norm_gamma, L0_ffn_slot_norm_gamma, L0_ffn_slot_embeds, L0_ffn_w1, L0_ffn_b1, L0_ffn_w2, L0_ffn_b2), axis=-1)
    return x

_drawn_inputs = setup_inputs


def setup_inputs(seed=0):
    import zlib

    import numpy as np

    out = dict(_drawn_inputs(seed))
    spreads = {'L0_attn_rms_scale': (1.0, 0.2),
     'L0_ffn_norm_gamma': (1.0, 0.2),
     'L0_ffn_slot_norm_gamma': (1.0, 0.2),
     'L0_ffn_b1': (0.0, 0.1),
     'L0_ffn_b2': (0.0, 0.1)}
    factors = {}
    for name, (base, spread) in spreads.items():
        noise = np.random.default_rng([zlib.crc32(name.encode()), seed]).standard_normal(out[name].shape)
        drawn = base * np.exp(spread * noise) if base else spread * noise
        out[name] = jnp.asarray(drawn.astype(out[name].dtype))
    for name, factor in factors.items():
        out[name] = (out[name] * factor).astype(out[name].dtype)
    return out
```

```python
import numpy as np
import concourse.bass as bass
from concourse import mybir
from contextlib import ExitStack

F32 = mybir.dt.float32
F32R = mybir.dt.float32r
ALU = mybir.AluOpType
ACT = mybir.ActivationFunctionType
AX = mybir.AxisListType

DBG = None
NB, N, D = 8, 512, 256
H, DH, DV = 16, 16, 32
E, S, HID = 8, 128, 1024
M = E * S
HD = H * DV
P = 128
NT, DC, HG = N // P, D // P, HD // P
STEPS = 2 * HG
HC = HID // P
LAMBDA_INIT = 0.8
EPS = 1e-5
NEG = -1e30
START = 1
PARTS = ((0, 0), (0, 1), (1, 0))


def phase1_schedule():
    out = [("XT", 0, 0)] + [("QK", k, 0) for k in range(8)] + [("VP", t, 0) for t in range(NT)]
    out += [("A", 0, u) for u in range(10)] + [("A", 1, u) for u in range(10)] + [("T", 0, 0)]
    for s in range(STEPS):
        b = [("B", s, u) for u in range(5)]
        a = [("A", s + 2, u) for u in range(10)] if s + 2 < STEPS else []
        t = [("T", s + 1, 0)] if s + 1 < STEPS else []
        pv = [(k, s - 1, j) for k in ("PVS", "PVV") for j in range(NT)] if s else []
        order = "BaBpaBpaBTpaBpaapapapapa" if a else "BBpBpBTpBpppp" 
        for c in order:
            src = {"B": b, "a": a, "p": pv, "T": t}[c]
            if src:
                out.append(src.pop(0))
        out += pv + a + b + t
    out += [(k, STEPS - 1, j) for k in ("PVS", "PVV") for j in range(NT)]
    out += [("MS", 0, 0), ("MS", 1, 0), ("WO", 0, 0), ("WO", 1, 0), ("XNT", 0, 0), ("XNT", 1, 0)]
    out += [("L2", 0, 0), ("L2", 1, 0), ("L1", 0, 0), ("TD", 0, 0), ("TD", 1, 0), ("L2", 2, 0),
            ("TD", 2, 0), ("TD", 3, 0), ("SL", 0, 0), ("SL", 0, 1), ("L2", 3, 0), ("L1", 1, 0),
            ("TD", 4, 0), ("TD", 5, 0), ("L1", 2, 0), ("TD", 6, 0), ("TD", 7, 0), ("SL", 1, 0),
            ("SL", 1, 1), ("L1", 3, 0)]
    return out


SCHEDULE = phase1_schedule()
W_READER = {"QK": "dve", "VP": "act", "A": "dve", "T": "act", "WO": "dve", "XNT": "dve", "TD": "dve"}
W_UNITS = [x for x in SCHEDULE if x[0] in W_READER]
S_UNITS = [x for x in SCHEDULE if x[0] in ("B", "MS", "L2", "L1")]
U_READER = {"PVS": "dve", "PVV": "dve", "SL": "act"}
U_UNITS = [x for x in SCHEDULE if x[0] in U_READER and (x[0] == "SL" or x[2] == NT - 1)]
NW, NS, NU = len(W_UNITS), len(S_UNITS), len(U_UNITS)
assert NW % 2 == 0 and NS % 2 == 0 and NU % 2 == 0


def read_by(units, reader, who, upto):
    return sum(reader[x[0]] == who for x in units[:upto])


W_DVE, W_ACT = (read_by(W_UNITS, W_READER, w, NW) for w in ("dve", "act"))
U_DVE, U_ACT = (read_by(U_UNITS, U_READER, w, NU) for w in ("dve", "act"))


def p_piece(a, j):
    return {0: (a, 512), 1: (a, 0), 3: (a, 384), 2: (4, 256 * a)}[j]


A_PIECES = []
for _a in range(4):
    A_PIECES += [[(_a, 3, 0)], [(_a, 2, 0), (_a, 0, 384)]]
A_PIECES += [[(0, 1, 0), (1, 1, 256)], [(2, 1, 0), (3, 1, 256)]]


def layer(nc, t, out, stop_after=3):
    ctx = ExitStack()
    with ctx:
        nsem = [0]

        def sem(name):
            return ctx.enter_context(nc.semaphore(name))

        top = [(nc.sbuf_base + 63) // 64 * 64]

        def place(name, shape, dt, at):
            size = 4 * int(np.prod(shape[1:]))
            return nc.alloc_sbuf_tensor_at(name, shape, dt, offset=at), at + (size + 31) // 32 * 32

        def keep(name, shape, dt=F32):
            tensor, top[0] = place(name, shape, dt, top[0])
            return tensor

        ident = keep("ident", [P, P])
        powers = keep("powers", [P, 8])
        eps_col = keep("eps_col", [P, 1])
        base = top[0]
        ones = keep("ones", [P, DV])
        mask_a = keep("mask_a", [P, N])
        block32 = keep("block32", [P, P])
        neg_lam = keep("neg_lam", [P, HG])
        w_qk = [keep(f"w_qk{hl}", [P, 2, DC, HD], F32R) for hl in range(2)]
        w_v = [keep(f"w_v{hl}", [P, DC, HD], F32R) for hl in range(2)]
        w_o = [keep(f"w_o{hl}", [P, HG, D], F32R) for hl in range(2)]
        sn_t = [keep(f"sn_t{hl}", [P, DC, M], F32R) for hl in range(2)]
        gamma = keep("gamma", [P, D])
        q_stack = keep("q_stack", [P, H, N], F32R)
        k_stack = keep("k_stack", [P, H, N], F32R)
        v_sb = keep("v_sb", [P, NT, HD])
        x_t = [keep(f"x_t{hl}", [P, DC, N], F32R) for hl in range(2)]
        x_res = keep("x_res", [P, NT, D])
        m_col = keep("m_col", [P, STEPS, 16])
        m_row = keep("m_row", [16, STEPS, P], F32R)
        stat = keep("stat", [P, NT, 6])
        aggr = keep("aggr", [P, NT, 2])
        small = keep("small", [P, 64])
        sumsq = keep("sumsq", [P, NT])
        p_at = top[0]
        p_sb = [keep(f"p_sb{k}", [P, 5, 1024]) for k in range(2)]
        d_at = p_at
        disp = []
        for hl in range(2):
            tensor, d_at = place(f"disp{hl}", [P, NT, M], F32R, d_at)
            disp.append(tensor)
        r_at = top[0]
        x_raw, a1 = place("x_raw", [P, DC, N], F32, r_at)
        stage = []
        for k in range(3):
            tensor, a1 = place(f"stage{k}", [P, 2, N], F32R, a1)
            stage.append(tensor)
        o_sb, a2 = place("o_sb", [P, HG, N], F32, r_at)
        o_tmp, a2 = place("o_tmp", [P, 2, N], F32, a2)
        o_sq, a2 = place("o_sq", [P, HG, N], F32, a2)
        xn_f, a3 = place("xn_f", [P, NT, D], F32, r_at)
        xn = []
        for hl in range(2):
            tensor, a3 = place(f"xn{hl}", [P, NT, D], F32R, a3)
            xn.append(tensor)
        ed_t, a3 = place("ed_t", [P, 4, N], F32, a3)
        slots, a3 = place("slots", [P, DC, 512], F32, a3)
        on_at = max(a1, a2, a3)
        on_at = p_at
        on = []
        for hl in range(2):
            tensor, on_at = place(f"on{hl}", [P, HG, N], F32R, on_at)
            on.append(tensor)
        ec_at = d_at
        e_c = []
        for k in range(2):
            tensor, ec_at = place(f"e_c{k}", [P, M], F32, ec_at)
            e_c.append(tensor)
        assert max(a1, a2, a3) <= nc.sbuf_usable_end
        raw_at = p_at
        w_qk_raw, raw_at = place("w_qk_raw", [P, 2, DC, HD], F32, raw_at)
        w_v_raw, raw_at = place("w_v_raw", [P, DC, HD], F32, raw_at)
        w_o_raw, raw_at = place("w_o_raw", [P, HG, D], F32, raw_at)
        slot_raw, raw_at = place("slot_raw", [P, E, D], F32, raw_at)
        slot_n, raw_at = place("slot_n", [P, E, D], F32, raw_at)
        slot_gamma, raw_at = place("slot_gamma", [P, D], F32, raw_at)
        rms_col, raw_at = place("rms_col", [P, 1], F32, raw_at)
        lam_in, raw_at = place("lam_in", [P, 4, HG, DH], F32, raw_at)
        lam_sum, raw_at = place("lam_sum", [P, 2, HG], F32, raw_at)
        assert raw_at <= r_at

        psum = ctx.enter_context(nc.psum_tensor("psum", [P, 8, 512], F32))
        W, SR, U = psum[:, 0:2, :], psum[:, 2:6, :], psum[:, 6:8, :]

        qk_scr = nc.dram_tensor("qk_scr", [2, 2, HD, N], F32, **({"kind": DBG} if DBG else {})).ap()
        x_scr = nc.dram_tensor("x_scr", [NB, P, NT, D], F32, **({"kind": DBG} if DBG else {})).ap()
        ec_scr = nc.dram_tensor("ec_scr", [NB, NT, P, M], F32, **({"kind": DBG} if DBG else {})).ap()
        sl_scr = nc.dram_tensor("sl_scr", [E, DC, P, NB, S], F32, **({"kind": DBG} if DBG else {})).ap()
        eo_scr = nc.dram_tensor("eo_scr", [NB, S, E, D], F32, **({"kind": DBG} if DBG else {})).ap()
        start_scr = nc.dram_tensor("start_scr", [2, 16, 16], F32).ap()

        def lo_part(eng, lo, src, hi):
            return eng.tensor_tensor(lo, src, hi.bitcast(F32), ALU.subtract)

        const_in, pro_dve, pro_pool, pro_act, pro_pe = (
            sem(x) for x in ("const_in", "pro_dve", "pro_pool", "pro_act", "pro_pe"))
        loads = [(ident, t["ident"]), (mask_a, t["mask_a"]), (block32, t["block32"]), (gamma, t["gamma"]),
                 (w_qk_raw, t["w_qk"]), (w_v_raw, t["w_v"]), (w_o_raw, t["w_o"]), (slot_raw, t["slot"]),
                 (slot_gamma, t["slot_gamma"]), (rms_col, t["rms_col"]), (lam_in, t["lam_in"])]
        SN_UNITS = [(c, g) for c in range(DC) for g in range(2)]

        def sn_bank(n):
            return psum[:, n, :]

        slot_ready, squares_ready = 12, 9

        with nc.Block() as block:

            @block.sync
            def _(sp):
                for dst, src in loads:
                    sp.dma_start(dst[:], src).then_inc(const_in, 16)
                sp.wait_ge(pro_dve, 1)
                sp.wait_ge(const_in, 16 * len(loads))

            @block.vector
            def _(dve):
                v = nc.vector
                n = [0]

                def link(ins):
                    n[0] += 1
                    ins.then_inc(pro_dve, 1)
                    dve.wait_ge(pro_dve, n[0])

                link(v.memset(k_stack[:].bitcast(F32), -1.0))
                v.memset(ones[:], 1.0)
                dve.wait_ge(const_in, 16 * len(loads))
                link(v.tensor_tensor(lam_in[:, 0:2], lam_in[:, 0:2], lam_in[:, 2:4], ALU.mult))
                link(v.reduce_sum(lam_sum[:], lam_in[:, 0:2], AX.X))
                v.tensor_copy(w_qk[0][:], w_qk_raw[:])
                link(v.tensor_copy(w_v[0][:], w_v_raw[:]))
                lo_part(v, w_qk[1][:], w_qk_raw[:], w_qk[0][:])
                lo_part(v, w_v[1][:], w_v_raw[:], w_v[0][:])
                link(v.tensor_scalar(w_o_raw[:], w_o_raw[:], rms_col[:, 0:1], 1.0 - LAMBDA_INIT,
                                     ALU.mult, ALU.mult))
                link(v.tensor_copy(w_o[0][:], w_o_raw[:]))
                lo_part(v, w_o[1][:], w_o_raw[:], w_o[0][:])
                dve.wait_ge(pro_act, 1)
                link(v.tensor_tensor(neg_lam[:], lam_sum[:, 1, :], lam_sum[:, 0, :], ALU.subtract))
                link(v.tensor_scalar(neg_lam[:], neg_lam[:], -LAMBDA_INIT, None, ALU.add))
                for e in range(E):
                    ins = v.tensor_tensor_reduce(
                        out=slot_n[:, e], in0=slot_raw[:, e], in1=slot_raw[:, e], scale=1.0, scalar=0.0,
                        op0=ALU.mult, op1=ALU.add, accum_out=small[:, e:e + 1])
                link(ins)
                assert n[0] == squares_ready
                dve.wait_ge(pro_pool, 2)
                link(v.tensor_scalar(small[:, 8:16], small[:, 8:16], 1e-12, float(D) ** -0.5,
                                     ALU.max, ALU.mult))
                link(v.reciprocal(small[:, 16:24], small[:, 8:16]))
                for e in range(E):
                    ins = v.scalar_tensor_tensor(slot_n[:, e], slot_raw[:, e], small[:, 16 + e:17 + e],
                                                 slot_gamma[:], ALU.mult, ALU.mult)
                link(ins)
                assert n[0] == slot_ready
                for k, (c, g) in enumerate(SN_UNITS):
                    dve.wait_ge(pro_act, 2 + k)
                    lo_part(v, sn_t[1][:, c, 512 * g:512 * g + 512], sn_bank(k),
                            sn_t[0][:, c, 512 * g:512 * g + 512])

            @block.gpsimd
            def _(pool):
                nc.gpsimd.memset(eps_col[:], EPS)
                nc.gpsimd.memset(powers[:, 0:4], -0.5)
                nc.gpsimd.memset(powers[:, 4:8], 0.5)
                nc.gpsimd.memset(small[:, 40:48], 0.5).then_inc(pro_pool, 1)
                pool.wait_ge(pro_pool, 1)
                pool.wait_ge(pro_dve, squares_ready)
                nc.gpsimd.tensor_tensor(small[:, 8:16], small[:, 0:8], small[:, 40:48], ALU.pow)\
                    .then_inc(pro_pool, 1)

            @block.scalar
            def _(act):
                act.wait_ge(pro_dve, 3)
                nc.scalar.activation(lam_sum[:], lam_sum[:], ACT.Exp).then_inc(pro_act, 1)
                for k, (c, g) in enumerate(SN_UNITS):
                    act.wait_ge(pro_pe, k + 1)
                    nc.scalar.activation(sn_t[0][:, c, 512 * g:512 * g + 512], sn_bank(k), ACT.Copy)\
                        .then_inc(pro_act, 1)

            @block.tensor
            def _(pe):
                pe.wait_ge(pro_dve, slot_ready)
                for k, (c, g) in enumerate(SN_UNITS):
                    for e in range(4):
                        last = nc.tensor.transpose(sn_bank(k)[:, P * e:P * e + P],
                                                   slot_n[:, 4 * g + e, P * c:P * c + P], ident[:])
                    last.then_inc(pro_pe, 1)

        (w_ready, w_dve, w_act, s_ready, s_done, u_ready, u_dve, u_act, xt_in, xt_split, qk_hi, stack_in,
         xres_in, masked, o_ready, o_squared, on_ready, stats_ready, rstd_ready, x_ready,
         sq_ready, norm_ready, xn_ready, xnt_hi, gneg_ready, ed_ready, td_hi, cneg_ready,
         ec_ready, x_out, chain_d, chain_p) = (sem(x) for x in (
             "w_ready w_dve w_act s_ready s_done u_ready u_dve u_act xt_in xt_split qk_hi stack_in "
             "xres_in masked o_ready o_squared on_ready stats_ready rstd_ready x_ready "
             "sq_ready norm_ready xn_ready xnt_hi gneg_ready ed_ready td_hi cneg_ready "
             "ec_ready x_out chain_d chain_p").split())
        stage_out = [sem(f"stage_out{k}") for k in range(3)]
        m_row_in = [sem(f"m_row_in{k}") for k in range(2)]
        slots_out = [sem(f"slots_out{k}") for k in range(DC)]
        ec_out = [sem(f"ec_out{k}") for k in range(2)]
        STAGE_USES = [len(range(k, 8, 3)) for k in range(3)]
        stacks = (q_stack, k_stack)
        STACK_PARTS = ((0, 0, 1), (0, 1, 0))

        def w_seq(kind, a, b=0):
            return W_UNITS.index((kind, a, b))

        def s_seq(kind, a, b=0):
            return S_UNITS.index((kind, a, b))

        def u_seq(kind, a, b):
            return U_UNITS.index((kind, a, b))

        def w_bank(n):
            return W[:, n % 2, :]

        def s_unit(n):
            return SR[:, 2 * (n % 2):2 * (n % 2) + 2, :]

        def u_bank(n):
            return U[:, n % 2, :]

        def w_by_dve(i, n):
            return w_dve, i * W_DVE + read_by(W_UNITS, W_READER, "dve", n) + START

        def w_by_act(i, n):
            return w_act, i * W_ACT + read_by(W_UNITS, W_READER, "act", n) + START

        def w_free(i, n):
            by = w_by_dve if W_READER[W_UNITS[(n - 2) % NW][0]] == "dve" else w_by_act
            return by(i, max(n - 1, 0))

        def u_by_dve(i, n):
            return u_dve, i * U_DVE + read_by(U_UNITS, U_READER, "dve", n) + START

        def u_by_act(i, n):
            return u_act, i * U_ACT + read_by(U_UNITS, U_READER, "act", n) + START

        def u_free(i, n):
            by = u_by_dve if U_READER[U_UNITS[(n - 2) % NU][0]] == "dve" else u_by_act
            return by(i, max(n - 1, 0))

        def s_by_act(i, n):
            return s_done, i * NS + n + START

        def s_free(i, n):
            return s_by_act(i, max(n - 1, 0))

        with nc.Block() as block:

            @block.tensor
            def _(pe):
                mm = nc.tensor.matmul

                def products(out, pairs):
                    for k, (stationary, moving) in enumerate(pairs):
                        last = mm(out, stationary, moving, start=k == 0, stop=k == len(pairs) - 1)
                    return last

                with pe.Fori(0, NB) as i:
                    for kind, a, b in SCHEDULE:
                        if kind == "QK":
                            qk, hg = a // HG, a % HG
                            if a == 0:
                                pe.wait_ge(xt_split, 2 * i + 2)
                            n = w_seq(kind, a)
                            pe.wait_ge(*w_free(i, n))
                            products(w_bank(n), [
                                (w_qk[x][:, qk, c, P * hg:P * hg + P], x_t[y][:, c, :])
                                for c in range(DC) for x, y in PARTS]).then_inc(w_ready, 1)
                        elif kind == "VP":
                            n = w_seq(kind, a)
                            pe.wait_ge(*w_free(i, n))
                            products(w_bank(n), [
                                (x_t[x][:, c, P * a:P * a + P], w_v[y][:, c, :])
                                for c in range(DC) for x, y in PARTS]).then_inc(w_ready, 1)
                        elif kind == "A":
                            if (a, b) == (0, 0):
                                pe.wait_ge(stack_in, 192 * i + 192)
                            n = w_seq(kind, a, b)
                            pe.wait_ge(*w_free(i, n))
                            r, hg = 64 * (a % 2), a // 2
                            for h, qt, col in A_PIECES[b]:
                                keys = P * (qt + 1)
                                last = mm(w_bank(n)[:, col:col + keys],
                                          q_stack[r:r + 48, 4 * hg + h, P * qt:P * qt + P],
                                          k_stack[r:r + 48, 4 * hg + h, 0:keys], start=True, stop=True)
                            last.then_inc(w_ready, 1)
                        elif kind == "T":
                            n = w_seq(kind, a)
                            pe.wait_ge(*w_free(i, n))
                            pe.wait_ge(*w_by_dve(i, w_seq("A", a, 9) + 1))
                            nc.tensor.transpose(w_bank(n)[0:16, 0:P], m_col[:, a, :], ident[:])\
                                .then_inc(w_ready, 1)
                        elif kind == "B":
                            if b == 0:
                                pe.wait_ge(m_row_in[a % 2], 64 * i + 16 * (a // 2 + 1))
                            n = s_seq(kind, a, b)
                            pe.wait_ge(*s_free(i, n))
                            r, hg = 64 * (a % 2), a // 2
                            unit = s_unit(n)
                            pieces = ([(b, 1, 0, 0), (b, 3, 0, 384), (b, 0, 1, 0)] if b < 4 else
                                      [(h, 2, h // 2, 256 * (h % 2)) for h in range(4)])
                            for h, j, bank, col in pieces:
                                q0 = P * j
                                last = mm(unit[:, bank, col:col + N - q0],
                                          k_stack[r:r + 49, 4 * hg + h, q0:q0 + P],
                                          q_stack[r:r + 49, 4 * hg + h, q0:N], start=True, stop=True)
                            last.then_inc(s_ready, 1)
                        elif kind in ("PVS", "PVV"):
                            n = u_seq(kind, a, NT - 1)
                            if b == 0:
                                pe.wait_ge(masked, i * 5 * STEPS + 5 * (a + 1))
                                pe.wait_ge(*u_free(i, n))
                            hg = a // 2
                            for h in range(4):
                                unit, col = p_piece(h, b)
                                q0 = P * b
                                stationary = (ones[:] if kind == "PVS" else
                                              v_sb[:, b, DV * (4 * hg + h):DV * (4 * hg + h) + DV])
                                last = mm(u_bank(n)[DV * h:DV * h + DV, q0:N], stationary,
                                          p_sb[a % 2][:, unit, col:col + N - q0],
                                          start=b == 0, stop=b == NT - 1, skip_group_check=True)
                            if b == NT - 1:
                                last.then_inc(u_ready, 1)
                        elif kind == "MS":
                            n = s_seq(kind, a)
                            pe.wait_ge(*s_free(i, n))
                            pe.wait_ge(o_squared, i * HG + 2 * a + 2)
                            for k in range(2):
                                last = mm(s_unit(n)[:, k, :], block32[:], o_sq[:, 2 * a + k, :],
                                          start=True, stop=True)
                            last.then_inc(s_ready, 1)
                        elif kind == "WO":
                            n = w_seq(kind, a)
                            pe.wait_ge(*w_free(i, n))
                            if a == 0:
                                pe.wait_ge(on_ready, i + 1)
                            for k in range(2):
                                qt = 2 * a + k
                                last = products(w_bank(n)[:, D * k:D * k + D], [
                                    (on[x][:, hg, P * qt:P * qt + P], w_o[y][:, hg, :])
                                    for hg in range(HG) for x, y in PARTS])
                            last.then_inc(w_ready, 1)
                        elif kind == "XNT":
                            n = w_seq(kind, a)
                            pe.wait_ge(*w_free(i, n))
                            pe.wait_ge(xn_ready, 2 * i + 1)
                            for k in range(NT):
                                last = nc.tensor.transpose(w_bank(n)[:, P * k:P * k + P],
                                                           xn_f[:, k, P * a:P * a + P], ident[:])
                            last.then_inc(w_ready, 1)
                        elif kind == "L2":
                            n = s_seq(kind, a)
                            pe.wait_ge(*s_free(i, n))
                            if a == 0:
                                pe.wait_ge(*w_by_dve(i, w_seq("XNT", 1) + 1))
                            for k in range(2):
                                mt = 2 * a + k
                                last = products(s_unit(n)[:, k, :], [
                                    (sn_t[x][:, c, P * mt:P * mt + P], x_t[y][:, c, :])
                                    for c in range(DC) for x, y in PARTS])
                            last.then_inc(s_ready, 1)
                        elif kind == "L1":
                            n = s_seq(kind, a)
                            pe.wait_ge(*s_free(i, n))
                            for k in range(2):
                                last = products(s_unit(n)[:, k, :], [
                                    (x_t[x][:, c, P * a:P * a + P], sn_t[y][:, c, 512 * k:512 * k + 512])
                                    for c in range(DC) for x, y in PARTS])
                            last.then_inc(s_ready, 1)
                        elif kind == "TD":
                            n = w_seq(kind, a)
                            pe.wait_ge(*w_free(i, n))
                            pe.wait_ge(ed_ready, i * E + a + 1)
                            for k in range(NT):
                                last = nc.tensor.transpose(w_bank(n)[:, P * k:P * k + P],
                                                           ed_t[:, a % 4, P * k:P * k + P], ident[:])
                            last.then_inc(w_ready, 1)
                        elif kind == "SL":
                            n = u_seq(kind, a, b)
                            pe.wait_ge(*u_free(i, n))
                            if b == 0:
                                pe.wait_ge(*w_by_dve(i, w_seq("TD", 4 * a + 3) + 1))
                            if (a, b) == (0, 0):
                                pe.wait_ge(xn_ready, 2 * i + 2)
                            products(u_bank(n), [
                                (xn[x][:, k, P * b:P * b + P], disp[y][:, k, 512 * a:512 * a + 512])
                                for k in range(NT) for x, y in PARTS]).then_inc(u_ready, 1)

            @block.sync
            def _(sp):
                with sp.Fori(0, NB) as i:
                    for kind, a, b in SCHEDULE:
                        if kind == "XT":
                            sp.dma_start(x_raw[:], t["x_t"][bass.ds(i, 1)].rearrange(
                                "o (c p) n -> p (o c) n", p=P)).then_inc(xt_in, 16)
                            sp.dma_start(x_res[:], t["x"][bass.ds(i, 1)].rearrange(
                                "o (k p) d -> p (o k) d", p=P)).then_inc(xres_in, 16)
                        elif kind == "QK":
                            sp.wait_ge(*w_by_dve(i, a + 1))
                            qk, hg = a // HG, a % HG
                            sp.dma_start(qk_scr[qk, :, P * hg:P * hg + P, :].rearrange("l p n -> p l n"),
                                         stage[a % 3][:].bitcast(F32)).then_inc(stage_out[a % 3], 16)
                            if a % HG == HG - 1:
                                for k in range(3):
                                    sp.wait_ge(stage_out[k], 16 * (i * STAGE_USES[k]
                                                                   + len(range(k, a + 1, 3))))
                                view = qk_scr[qk].rearrange("l (h m r) n -> l m r h n", m=2, r=DH)
                                for m in range(2):
                                    for k, part in enumerate(STACK_PARTS[qk]):
                                        r = 64 * m + DH * k
                                        sp.dma_start(stacks[qk][r:r + DH, :, :].bitcast(F32),
                                                     view[part, m]).then_inc(stack_in, 16)
                        elif kind == "T":
                            n = w_seq(kind, a)
                            sp.wait_ge(*w_by_act(i, n + 1))
                            r = 64 * (a % 2) + 48
                            sp.dma_start(q_stack[r:r + 1, 4 * (a // 2):4 * (a // 2) + 4, :].bitcast(F32)
                                         .rearrange("p h (k n) -> p (h k) n", n=P),
                                         m_row[:, a, :].bitcast(F32)).then_inc(m_row_in[a % 2], 16)
                        elif kind == "XNT" and a == 0:
                            sp.wait_ge(x_ready, i + 1)
                            sp.nop(nofuse=True)
                            sp.dma_start(x_scr[bass.ds(i, 1)].rearrange("o p k d -> p (o k) d"), x_res[:])\
                                .then_inc(x_out, 16)
                        elif kind == "SL":
                            sp.wait_ge(*u_by_act(i, u_seq(kind, a, b) + 1))
                            sp.nop(nofuse=True)
                            sp.dma_start(
                                sl_scr[4 * a:4 * a + 4, b, :, bass.ds(i, 1), :]
                                .rearrange("e p o s -> p (e o) s"),
                                slots[:, b, :].rearrange("p (e s) -> p e s", e=4)).then_inc(slots_out[b], 16)
                        elif kind == "L1":
                            sp.wait_ge(ec_ready, i * NT + a + 1)
                            sp.nop(nofuse=True)
                            sp.dma_start(ec_scr[bass.ds(i, 1), a].rearrange("o p m -> (o p) m"),
                                         e_c[a % 2][:]).then_inc(ec_out[a % 2], 16)
                    sp.wait_ge(s_ready, i * NS + NS)
                    sp.nop(nofuse=True)
                    for c in range(DC):
                        sp.wait_ge(slots_out[c], 32 * i + 32)
                        sp.nop(nofuse=True)
                    for k in range(2):
                        sp.wait_ge(ec_out[k], 32 * i + 32)
                        sp.nop(nofuse=True)
                    sp.wait_ge(x_out, 16 * i + 16)
                    sp.nop(nofuse=True)

            @block.scalar
            def _(act):
                ac = nc.scalar.activation
                for x in (w_act, s_done, u_act):
                    act.sem_inc(x, START)
                with act.Fori(0, NB) as i:
                    for kind, a, b in SCHEDULE:
                        if (kind, a, b) in W_UNITS:
                            n = w_seq(kind, a, b)
                        if kind == "QK":
                            if a >= 3:
                                act.wait_ge(stage_out[a % 3], 16 * (i * STAGE_USES[a % 3] + a // 3))
                            act.wait_ge(w_ready, i * NW + n + 1)
                            ac(stage[a % 3][:, 0, :], w_bank(n), ACT.Copy).then_inc(qk_hi, 1)
                        elif kind == "VP":
                            act.wait_ge(w_ready, i * NW + n + 1)
                            ac(v_sb[:, a, :], w_bank(n), ACT.Copy).then_inc(w_act, 1)
                        elif kind == "T":
                            act.wait_ge(w_ready, i * NW + n + 1)
                            ac(m_row[:, a, :], w_bank(n)[0:16, 0:P], ACT.Copy).then_inc(w_act, 1)
                        elif kind == "B":
                            n = s_seq(kind, a, b)
                            if b == 0 and a >= 2:
                                act.wait_ge(u_ready, i * NU + 2 * (a - 1))
                            act.wait_ge(s_ready, i * NS + n + 1)
                            ac(p_sb[a % 2][:, b, :], s_unit(n).rearrange("p k n -> p (k n)"), ACT.Exp,
                               scale=float(DH) ** -0.5).then_inc(s_done, 1)
                        elif kind == "MS":
                            n = s_seq(kind, a)
                            act.wait_ge(s_ready, i * NS + n + 1)
                            ac(o_sq[:, 2 * a:2 * a + 2, :], s_unit(n), ACT.Sqrt, bias=eps_col[:, 0:1])\
                                .then_inc(s_done, 1)
                        elif kind == "XNT":
                            act.wait_ge(w_ready, i * NW + n + 1)
                            ac(x_t[0][:, a, :], w_bank(n), ACT.Copy).then_inc(xnt_hi, 1)
                        elif kind == "L2":
                            n = s_seq(kind, a)
                            act.wait_ge(gneg_ready, i * 4 + a + 1)
                            for k in range(2):
                                mt = 2 * a + k
                                if mt >= 4:
                                    act.wait_ge(w_ready, i * NW + w_seq("TD", mt - 4) + 1)
                                last = ac(ed_t[:, mt % 4, :], s_unit(n)[:, k, :], ACT.Exp,
                                          bias=small[:, 16 + mt:17 + mt],
                                          accum_out=small[:, 24 + mt:25 + mt])
                            last.then_inc(s_done, 1)
                        elif kind == "L1":
                            n = s_seq(kind, a)
                            act.wait_ge(cneg_ready, i * NT + a + 1)
                            if a >= 2:
                                act.wait_ge(ec_out[a % 2], 32 * i + 16)
                            ac(e_c[a % 2][:], s_unit(n).rearrange("p k n -> p (k n)"), ACT.Exp,
                               bias=small[:, 44 + a:45 + a],
                               accum_out=small[:, 48 + a:49 + a]).then_inc(s_done, 1)
                        elif kind == "TD":
                            act.wait_ge(w_ready, i * NW + n + 1)
                            ac(disp[0][:, :, P * a:P * a + P], w_bank(n).rearrange("p (k m) -> p k m", m=P),
                               ACT.Copy).then_inc(td_hi, 1)
                        elif kind == "SL":
                            n = u_seq(kind, a, b)
                            if a:
                                act.wait_ge(slots_out[b], 32 * i + 16)
                            act.wait_ge(u_ready, i * NU + n + 1)
                            ac(slots[:, b, :], u_bank(n), ACT.Copy).then_inc(u_act, 1)

            @block.gpsimd
            def _(pool):
                g = nc.gpsimd
                with pool.Fori(0, NB) as i:
                    for kind, a, b in SCHEDULE:
                        if kind == "B":
                            pool.wait_ge(*s_by_act(i, s_seq(kind, a, b) + 1))
                            pool.nop(nofuse=True)
                            unit = p_sb[a % 2][:, b, :]
                            if b < 4:
                                tiles = [unit[:, 0:P].rearrange("p (k n) -> p k n", n=P),
                                         unit[:, 384:384 + 2 * P].rearrange("p (k n) -> p k n", n=P)]
                            else:
                                tiles = [unit.rearrange("p (k n) -> p k n", k=4)[:, :, 0:P]]
                            for x in tiles:
                                last = g.affine_select(out=x, in_=x, compare_op=ALU.is_ge, fill=0.0, base=0,
                                                       pattern=[[0, x.shape[1]], [1, P]],
                                                       channel_multiplier=-1)
                            last.then_inc(masked, 1)
                        elif kind == "PVV" and a % 2 and b == NT - 1:
                            hg = a // 2
                            pool.wait_ge(o_ready, i * HG + hg + 1 + START)
                            g.tensor_tensor(o_sq[:, hg, :], o_sb[:, hg, :], o_sb[:, hg, :], ALU.mult)\
                                .then_inc(o_squared, 1)
                        elif kind == "WO" and a == 1:
                            pool.wait_ge(stats_ready, i + 1)
                            pool.nop(nofuse=True)
                            g.tensor_scalar(small[:, 0:4], aggr[:, :, 1], EPS, None, ALU.add)\
                                .then_inc(chain_p, 1)
                            pool.wait_ge(chain_p, i + 1)
                            g.tensor_tensor(small[:, 4:8], small[:, 0:4], powers[:, 0:4], ALU.pow)\
                                .then_inc(rstd_ready, 1)
                            pool.wait_ge(sq_ready, i + 1)
                            g.tensor_tensor(small[:, 56:60], sumsq[:], powers[:, 4:8], ALU.pow)\
                                .then_inc(norm_ready, 1)

            @block.vector
            def _(dve):
                v = nc.vector
                LINKS = 26
                for x in (w_dve, u_dve, o_ready):
                    dve.sem_inc(x, START)
                with dve.Fori(0, NB) as i:
                    n_links = [0]

                    def link(ins):
                        n_links[0] += 1
                        ins.then_inc(chain_d, 1)
                        dve.wait_ge(chain_d, i * LINKS + n_links[0])

                    for kind, a, b in SCHEDULE:
                        if (kind, a, b) in W_UNITS:
                            n = w_seq(kind, a, b)
                        if kind == "XT":
                            dve.wait_ge(xt_in, 16 * i + 16)
                            v.tensor_copy(x_t[0][:], x_raw[:]).then_inc(xt_split, 1)
                            dve.wait_ge(xt_split, 2 * i + 1)
                            lo_part(v, x_t[1][:], x_raw[:], x_t[0][:]).then_inc(xt_split, 1)
                        elif kind == "QK":
                            dve.wait_ge(qk_hi, 8 * i + a + 1)
                            lo_part(v, stage[a % 3][:, 1, :], w_bank(n), stage[a % 3][:, 0, :])\
                                .then_inc(w_dve, 1)
                        elif kind == "A":
                            dve.wait_ge(w_ready, i * NW + n + 1)
                            dve.nop(nofuse=True)
                            for h, qt, col in A_PIECES[b]:
                                keys = P * (qt + 1)
                                last = v.tensor_tensor_reduce(
                                    out=w_bank(n)[:, col:col + keys], in0=w_bank(n)[:, col:col + keys],
                                    in1=mask_a[:, N - keys:N], scale=1.0, scalar=-3e38, op0=ALU.add,
                                    op1=ALU.max, accum_out=m_col[:, a, 4 * h + qt:4 * h + qt + 1])
                            last.then_inc(w_dve, 1)
                        elif kind == "PVS" and b == NT - 1:
                            n = u_seq(kind, a, b)
                            if a % 2 == 0:
                                dve.wait_ge(o_ready, i * HG + a // 2 + START)
                            else:
                                dve.wait_ge(*u_by_dve(i, n))
                            dve.wait_ge(u_ready, i * NU + n + 1)
                            v.reciprocal(o_tmp[:, 0, :], u_bank(n)).then_inc(u_dve, 1)
                        elif kind == "PVV" and b == NT - 1:
                            n = u_seq(kind, a, b)
                            dve.wait_ge(*u_by_dve(i, n))
                            dve.wait_ge(u_ready, i * NU + n + 1)
                            dst = o_tmp[:, 1, :] if a % 2 == 0 else o_tmp[:, 0, :]
                            v.tensor_tensor(dst, u_bank(n), o_tmp[:, 0, :], ALU.mult).then_inc(u_dve, 1)
                            if a % 2:
                                dve.wait_ge(*u_by_dve(i, n + 1))
                                hg = a // 2
                                v.scalar_tensor_tensor(o_sb[:, hg, :], o_tmp[:, 0, :], neg_lam[:, hg:hg + 1],
                                                       o_tmp[:, 1, :], ALU.mult, ALU.add)\
                                    .then_inc(o_ready, 1)
                        elif kind == "MS":
                            rms, o = o_sq[:, 2 * a:2 * a + 2, :], o_sb[:, 2 * a:2 * a + 2, :]
                            hi, lo = (on[hl][:, 2 * a:2 * a + 2, :] for hl in range(2))
                            dve.wait_ge(*s_by_act(i, s_seq(kind, a) + 1))
                            link(v.reciprocal(rms, rms))
                            link(v.tensor_tensor(o, o, rms, ALU.mult))
                            link(v.tensor_copy(hi, o))
                            last = lo_part(v, lo, o, hi)
                            if a == 1:
                                last.then_inc(on_ready, 1)
                        elif kind == "WO":
                            if a == 0:
                                dve.wait_ge(xres_in, 16 * i + 16)
                            dve.wait_ge(w_ready, i * NW + n + 1)
                            x2 = x_res[:, 2 * a:2 * a + 2, :]
                            v.tensor_tensor(x2, x2, w_bank(n).rearrange("p (k d) -> p k d", d=D), ALU.add)\
                                .then_inc(w_dve, 1)
                            dve.wait_ge(*w_by_dve(i, n + 1))
                            for k in range(2 * a, 2 * a + 2):
                                last = v.bn_stats(stat[:, k, :], x_res[:, k, :])
                            if a == 1:
                                link(last)
                                dve.nop(nofuse=True)
                                for k in range(NT):
                                    last = v.bn_aggr(aggr[:, k, :], stat[:, k, :])
                                last.then_inc(stats_ready, 1)
                                dve.wait_ge(rstd_ready, i + 1)
                                for k in range(NT):
                                    last = v.tensor_scalar(x_res[:, k, :], x_res[:, k, :], aggr[:, k, 0:1],
                                                           small[:, 4 + k:5 + k], ALU.subtract, ALU.mult)
                                last.then_inc(x_ready, 1)
                                dve.wait_ge(x_ready, i + 1)
                                for k in range(NT):
                                    last = v.tensor_tensor_reduce(
                                        out=xn_f[:, k, :], in0=x_res[:, k, :], in1=x_res[:, k, :], scale=1.0,
                                        scalar=0.0, op0=ALU.mult, op1=ALU.add, accum_out=sumsq[:, k:k + 1])
                                last.then_inc(sq_ready, 1)
                                dve.wait_ge(norm_ready, i + 1)
                                link(v.tensor_scalar(small[:, 56:60], small[:, 56:60], 1e-12,
                                                     float(D) ** -0.5, ALU.max, ALU.mult))
                                link(v.reciprocal(small[:, 0:4], small[:, 56:60]))
                                for k in range(NT):
                                    last = v.scalar_tensor_tensor(xn_f[:, k, :], x_res[:, k, :],
                                                                  small[:, k:k + 1], gamma[:],
                                                                  ALU.mult, ALU.mult)
                                last.then_inc(xn_ready, 1)
                                dve.wait_ge(xn_ready, 2 * i + 1)
                                link(v.tensor_copy(xn[0][:], xn_f[:]))
                                lo_part(v, xn[1][:], xn_f[:], xn[0][:]).then_inc(xn_ready, 1)
                        elif kind == "XNT":
                            dve.wait_ge(xnt_hi, 2 * i + a + 1)
                            lo_part(v, x_t[1][:, a, :], w_bank(n), x_t[0][:, a, :]).then_inc(w_dve, 1)
                        elif kind == "L2":
                            n = s_seq(kind, a)
                            dve.wait_ge(s_ready, i * NS + n + 1)
                            link(v.reduce_max(small[:, 8 + 2 * a:10 + 2 * a], s_unit(n), AX.X))
                            v.tensor_scalar(small[:, 16 + 2 * a:18 + 2 * a], small[:, 8 + 2 * a:10 + 2 * a],
                                            -1.0, None, ALU.mult).then_inc(gneg_ready, 1)
                            dve.wait_ge(*s_by_act(i, n + 1))
                            link(v.reciprocal(small[:, 32 + 2 * a:34 + 2 * a],
                                              small[:, 24 + 2 * a:26 + 2 * a]))
                            for mt in (2 * a, 2 * a + 1):
                                v.tensor_scalar(ed_t[:, mt % 4, :], ed_t[:, mt % 4, :],
                                                small[:, 32 + mt:33 + mt], None, ALU.mult)\
                                    .then_inc(ed_ready, 1)
                        elif kind == "L1":
                            n = s_seq(kind, a)
                            dve.wait_ge(s_ready, i * NS + n + 1)
                            link(v.reduce_max(small[:, 40 + a:41 + a],
                                              s_unit(n).rearrange("p k n -> p (k n)"), AX.X))
                            v.tensor_scalar(small[:, 44 + a:45 + a], small[:, 40 + a:41 + a],
                                            -1.0, None, ALU.mult).then_inc(cneg_ready, 1)
                            dve.wait_ge(*s_by_act(i, n + 1))
                            link(v.reciprocal(small[:, 52 + a:53 + a], small[:, 48 + a:49 + a]))
                            v.tensor_scalar(e_c[a % 2][:], e_c[a % 2][:], small[:, 52 + a:53 + a], None,
                                            ALU.mult).then_inc(ec_ready, 1)
                        elif kind == "TD":
                            hi, lo = (disp[hl][:, :, P * a:P * a + P] for hl in range(2))
                            dve.wait_ge(td_hi, i * E + a + 1)
                            lo_part(v, lo, w_bank(n).rearrange("p (k m) -> p k m", m=P), hi)\
                                .then_inc(w_dve, 1)
                    assert n_links[0] == LINKS, n_links[0]

        if stop_after == 1:
            return

        at = base
        w1_raw, at = place("w1_raw", [P, DC, HID], F32, at)
        w2_raw, at = place("w2_raw", [P, HC, D], F32, at)
        sl_raw, at = place("sl_raw", [P, DC, NB * S], F32, at)
        w1_p, w2_p, sl_p, h_p, h_f, b1_sb, b2_sb, eo_sb = [[], []], [[], []], [[], []], [[], []], [], [], [], []
        for k in range(2):
            for hl in range(2):
                tensor, at = place(f"w1_p{k}{hl}", [P, DC, HID], F32R, at)
                w1_p[k].append(tensor)
                tensor, at = place(f"w2_p{k}{hl}", [P, HC, D], F32R, at)
                w2_p[k].append(tensor)
                tensor, at = place(f"sl_p{k}{hl}", [P, DC, NB * S], F32R, at)
                sl_p[k].append(tensor)
                tensor, at = place(f"h_p{k}{hl}", [P, HC, 512], F32R, at)
                h_p[k].append(tensor)
            tensor, at = place(f"h_f{k}", [P, 1024], F32, at)
            h_f.append(tensor)
            tensor, at = place(f"b1_sb{k}", [P, HC], F32, at)
            b1_sb.append(tensor)
            tensor, at = place(f"b2_sb{k}", [P, D], F32, at)
            b2_sb.append(tensor)
            tensor, at = place(f"eo_sb{k}", [P, 2, D], F32, at)
            eo_sb.append(tensor)
        assert at <= nc.sbuf_usable_end
        raw_in, raw_split, split_link, h_ready, h_done, h_hi, h_split, eo_ready, eo_done = (
            sem(x) for x in ("raw_in raw_split split_link h_ready h_done h_hi h_split eo_ready "
                             "eo_done").split())
        bias_in = [sem(f"bias_in{k}") for k in range(2)]
        eo_out = [sem(f"eo_out{k}") for k in range(2)]
        PAIRS = E // 2
        PAIR_ORDER = [(kind, k, hf, u) for k in range(2) for kind, us in (("H", 4), ("EO", 2))
                      for hf in range(2) for u in range(us)]
        H_UNITS = [x for x in PAIR_ORDER if x[0] == "H"]
        EO_UNITS = [x for x in PAIR_ORDER if x[0] == "EO"]
        NH, NE = len(H_UNITS), len(EO_UNITS)
        raws = [(w1_raw, w1_p), (w2_raw, w2_p), (sl_raw, sl_p)]

        with nc.Block() as block:

            @block.sync
            def _(sp):
                with sp.Fori(0, PAIRS) as i:
                    for k in range(2):
                        if k == 0:
                            sp.wait_ge(raw_split, 6 * i + START)
                            sp.nop(nofuse=True)
                            sp.wait_ge(eo_done, i * NE + START)
                            sp.nop(nofuse=True)
                        else:
                            sp.wait_ge(raw_split, 6 * i + 3 + START)
                            sp.nop(nofuse=True)
                        one = bass.ds(2 * i + k, 1)
                        sp.dma_start(w1_raw[:], t["w1"][one].rearrange("o (c p) h -> p (o c) h", p=P))\
                            .then_inc(raw_in, 16)
                        sp.dma_start(sl_raw[:], sl_scr[one].rearrange("o c p b s -> p (o c) (b s)"))\
                            .then_inc(raw_in, 16)
                        sp.dma_start(w2_raw[:], t["w2"][one].rearrange("o (c p) d -> p (o c) d", p=P))\
                            .then_inc(raw_in, 16)
                        sp.dma_start(b1_sb[k][:], t["b1"][one].rearrange("o p c -> (o p) c"))\
                            .then_inc(bias_in[k], 16)
                        sp.dma_start(b2_sb[k][:], t["b2"][one].rearrange("o p d -> (o p) d"))\
                            .then_inc(bias_in[k], 16)

            @block.gpsimd
            def _(pool):
                for k in range(2):
                    pool.dma_start(start_scr[k], ident[0:16, 0:16]).then_inc(eo_out[k], 16 * START)
                with pool.Fori(0, PAIRS) as i:
                    for n, (_, k, hf, u) in enumerate(EO_UNITS):
                        pool.wait_ge(eo_done, i * NE + n + 1 + START)
                        pool.nop(nofuse=True)
                        b0 = 4 * hf + 2 * u
                        pool.dma_start(eo_scr[b0:b0 + 2, :, bass.ds(2 * i + k, 1), :]
                                       .rearrange("b s e d -> s (b e) d"), eo_sb[n % 2][:])\
                            .then_inc(eo_out[n % 2], 16)
                for k in range(2):
                    pool.wait_ge(eo_out[k], 16 * START + 16 * PAIRS * NE // 2)

            @block.tensor
            def _(pe):
                mm = nc.tensor.matmul

                def products(out, pairs):
                    for q, (stationary, moving) in enumerate(pairs):
                        last = mm(out, stationary, moving, start=q == 0, stop=q == len(pairs) - 1)
                    return last

                with pe.Fori(0, PAIRS) as i:
                    for kind, k, hf, u in PAIR_ORDER:
                        if kind == "H":
                            n = H_UNITS.index((kind, k, hf, u))
                            if (hf, u) == (0, 0):
                                pe.wait_ge(raw_split, 6 * i + 3 * k + 3 + START)
                            pe.wait_ge(h_done, i * NH + max(n - 1, 0) + START)
                            for q in range(2):
                                hc = 2 * u + q
                                last = products(s_unit(n)[:, q, :], [
                                    (w1_p[k][x][:, c, P * hc:P * hc + P],
                                     sl_p[k][y][:, c, 512 * hf:512 * hf + 512])
                                    for c in range(DC) for x, y in PARTS])
                            last.then_inc(h_ready, 1)
                        else:
                            n = EO_UNITS.index((kind, k, hf, u))
                            pe.wait_ge(h_split, i * NH + 8 * k + 4 * hf + 4 + START)
                            pe.wait_ge(eo_done, i * NE + max(n - 1, 0) + START)
                            for q in range(2):
                                s0 = P * (2 * u + q)
                                last = products(w_bank(n)[:, D * q:D * q + D], [
                                    (h_p[hf][x][:, hc, s0:s0 + P], w2_p[k][y][:, hc, :])
                                    for hc in range(HC) for x, y in PARTS])
                            last.then_inc(eo_ready, 1)

            @block.scalar
            def _(act):
                act.sem_inc(h_done, START)
                with act.Fori(0, PAIRS) as i:
                    for n, (_, k, hf, u) in enumerate(H_UNITS):
                        if (hf, u) == (0, 0):
                            act.wait_ge(bias_in[k], 32 * i + 32)
                        act.wait_ge(h_split, i * NH + max(n - 1, 0) + START)
                        act.wait_ge(h_ready, i * NH + n + 1)
                        for q in range(2):
                            hc = 2 * u + q
                            last = nc.scalar.activation(h_f[n % 2][:, 512 * q:512 * q + 512],
                                                        s_unit(n)[:, q, :], ACT.Gelu,
                                                        bias=b1_sb[k][:, hc:hc + 1])
                        last.then_inc(h_done, 1)

            @block.vector
            def _(dve):
                v = nc.vector

                def split_raw(i, k):
                    for q, (raw, parts) in enumerate(raws):
                        v.tensor_copy(parts[k][0][:], raw[:]).then_inc(split_link, 1)
                        dve.wait_ge(split_link, 6 * i + 3 * k + q + 1)
                        lo_part(v, parts[k][1][:], raw[:], parts[k][0][:]).then_inc(raw_split, 1)

                for x in (raw_split, h_split, eo_done):
                    dve.sem_inc(x, START)
                with dve.Fori(0, PAIRS) as i:
                    for kind, k, hf, u in PAIR_ORDER:
                        if (kind, hf, u) == ("H", 0, 0):
                            dve.wait_ge(raw_in, 96 * i + 48 * k + 48)
                            split_raw(i, k)
                        if kind == "H":
                            n = H_UNITS.index((kind, k, hf, u))
                            hi, lo = (h_p[hf][hl][:, 2 * u:2 * u + 2, :] for hl in range(2))
                            src = h_f[n % 2][:].rearrange("p (c n) -> p c n", c=2)
                            dve.wait_ge(h_done, i * NH + n + 1 + START)
                            v.tensor_copy(hi, src).then_inc(h_hi, 1)
                            dve.wait_ge(h_hi, i * NH + n + 1)
                            lo_part(v, lo, src, hi).then_inc(h_split, 1)
                        else:
                            n = EO_UNITS.index((kind, k, hf, u))
                            dve.wait_ge(eo_out[n % 2], 16 * (i * (NE // 2) + n // 2 + START))
                            dve.wait_ge(eo_ready, i * NE + n + 1)
                            for q in range(2):
                                last = v.tensor_tensor(eo_sb[n % 2][:, q, :],
                                                       w_bank(n)[:, D * q:D * q + D], b2_sb[k][:], ALU.add)
                            last.then_inc(eo_done, 1)

        if stop_after == 2:
            return

        at = base
        ec_in, eo_in, x_in, ec_p, eo_p = [], [], [], [[], []], [[], []]
        for k in range(2):
            tensor, at = place(f"ec_in{k}", [P, NT, M], F32, at)
            ec_in.append(tensor)
            tensor, at = place(f"eo_in{k}", [P, E, D], F32, at)
            eo_in.append(tensor)
            tensor, at = place(f"x_in{k}", [P, NT, D], F32, at)
            x_in.append(tensor)
            for hl in range(2):
                tensor, at = place(f"ec_p{k}{hl}", [P, E, N], F32R, at)
                ec_p[k].append(tensor)
                tensor, at = place(f"eo_p{k}{hl}", [P, E, D], F32R, at)
                eo_p[k].append(tensor)
        stat3, at = place("stat3", [P, 2, NT, 6], F32, at)
        aggr3, at = place("aggr3", [P, 2, NT, 2], F32, at)
        var3, at = place("var3", [P, 2, NT], F32, at)
        rstd3, at = place("rstd3", [P, 2, NT], F32, at)
        assert at <= nc.sbuf_usable_end
        (te_ready, te_hi, te_done, eo_hi, eo_split, y_ready, y_done, chain3, stats3_ready, rstd3_ready,
         chain3_p, ln_done) = (sem(x) for x in (
             "te_ready te_hi te_done eo_hi eo_split y_ready y_done chain3 stats3_ready rstd3_ready "
             "chain3_p ln_done").split())
        ec_loaded = [sem(f"ec_loaded{k}") for k in range(2)]
        eo_loaded = [sem(f"eo_loaded{k}") for k in range(2)]
        x_loaded = [sem(f"x_loaded{k}") for k in range(2)]
        out_stored = [sem(f"out_stored{k}") for k in range(2)]
        ORDER3 = [("TE", 0, u) for u in range(E)]
        for u in range(NT):
            ORDER3 += [("Y", 0, u), ("TE", 1, 2 * u), ("TE", 1, 2 * u + 1)]
        ORDER3 += [("Y", 1, u) for u in range(NT)]

        with nc.Block() as block:

            @block.sync
            def _(sp):
                with sp.Fori(0, NB // 2) as i:
                    for k in range(2):
                        one = bass.ds(2 * i + k, 1)
                        sp.wait_ge(te_done, 16 * i + START)
                        sp.nop(nofuse=True)
                        sp.dma_start(ec_in[k][:], ec_scr[one].rearrange("o k p m -> p (o k) m"))\
                            .then_inc(ec_loaded[k], 16)
                        sp.wait_ge(eo_split, 2 * i + START)
                        sp.nop(nofuse=True)
                        sp.dma_start(eo_in[k][:], eo_scr[one].rearrange("o s e d -> (o s) e d"))\
                            .then_inc(eo_loaded[k], 16)
                        sp.wait_ge(out_stored[k], 16 * i + 16 * START)
                        sp.nop(nofuse=True)
                        sp.dma_start(x_in[k][:], x_scr[one].rearrange("o p k d -> p (o k) d"))\
                            .then_inc(x_loaded[k], 16)

            @block.gpsimd
            def _(pool):
                g = nc.gpsimd
                for k in range(2):
                    pool.dma_start(start_scr[k], ident[0:16, 0:16]).then_inc(out_stored[k], 16 * START)
                with pool.Fori(0, NB // 2) as i:
                    for k in range(2):
                        pool.wait_ge(stats3_ready, 2 * i + k + 1)
                        pool.nop(nofuse=True)
                        g.tensor_scalar(var3[:, k, :], aggr3[:, k, :, 1], EPS, None, ALU.add)\
                            .then_inc(chain3_p, 1)
                        pool.wait_ge(chain3_p, 2 * i + k + 1)
                        g.tensor_tensor(rstd3[:, k, :], var3[:, k, :], powers[:, 0:4], ALU.pow)\
                            .then_inc(rstd3_ready, 1)
                        pool.wait_ge(ln_done, 2 * i + k + 1)
                        pool.nop(nofuse=True)
                        pool.dma_start(out[bass.ds(2 * i + k, 1)].rearrange("o (k p) d -> p (o k) d", p=P),
                                       x_in[k][:]).then_inc(out_stored[k], 16)
                for k in range(2):
                    pool.wait_ge(out_stored[k], 16 * NB // 2 + 16 * START)

            @block.tensor
            def _(pe):
                mm = nc.tensor.matmul
                pe.sem_inc(y_ready, START)
                with pe.Fori(0, NB // 2) as i:
                    for kind, k, u in ORDER3:
                        if kind == "TE":
                            n = 8 * k + u
                            if u == 0:
                                pe.wait_ge(ec_loaded[k], 16 * i + 16)
                            pe.wait_ge(te_done, 16 * i + max(n - 1, 0) + START)
                            for q in range(NT):
                                last = nc.tensor.transpose(w_bank(n)[:, P * q:P * q + P],
                                                           ec_in[k][:, q, P * u:P * u + P], ident[:])
                            last.then_inc(te_ready, 1)
                        else:
                            n = 4 * k + u
                            if u == 0:
                                pe.wait_ge(te_done, 16 * i + 8 * k + 8 + START)
                                pe.wait_ge(eo_split, 2 * i + k + 1 + START)
                            pe.wait_ge(y_done, 8 * i + max(n - 1, 0) + START)
                            pairs = [(ec_p[k][x][:, j, P * u:P * u + P], eo_p[k][y][:, j, :])
                                     for j in range(E) for x, y in PARTS]
                            for q, (stationary, moving) in enumerate(pairs):
                                last = mm(u_bank(n)[:, 0:D], stationary, moving, start=q == 0,
                                          stop=q == len(pairs) - 1)
                            last.then_inc(y_ready, 1)

            @block.scalar
            def _(act):
                with act.Fori(0, NB // 2) as i:
                    for kind, k, u in ORDER3:
                        if kind == "TE":
                            n = 8 * k + u
                            if u == 0:
                                act.wait_ge(y_ready, 8 * i + START)
                            act.wait_ge(te_ready, 16 * i + n + 1)
                            nc.scalar.activation(ec_p[k][0][:, u, :], w_bank(n), ACT.Copy).then_inc(te_hi, 1)

            @block.vector
            def _(dve):
                v = nc.vector
                for x in (te_done, eo_split, y_done):
                    dve.sem_inc(x, START)
                with dve.Fori(0, NB // 2) as i:
                    for kind, k, u in ORDER3:
                        if (kind, u) == ("TE", 0):
                            dve.wait_ge(eo_loaded[k], 16 * i + 16)
                            v.tensor_copy(eo_p[k][0][:], eo_in[k][:]).then_inc(eo_hi, 1)
                            dve.wait_ge(eo_hi, 2 * i + k + 1)
                            lo_part(v, eo_p[k][1][:], eo_in[k][:], eo_p[k][0][:]).then_inc(eo_split, 1)
                        if kind == "TE":
                            n = 8 * k + u
                            dve.wait_ge(te_hi, 16 * i + n + 1)
                            lo_part(v, ec_p[k][1][:, u, :], w_bank(n), ec_p[k][0][:, u, :])\
                                .then_inc(te_done, 1)
                        else:
                            n = 4 * k + u
                            x = x_in[k][:, u, :]
                            if u == 0:
                                dve.wait_ge(x_loaded[k], 16 * i + 16)
                            dve.wait_ge(y_ready, 8 * i + n + 1 + START)
                            v.tensor_tensor(x, x, u_bank(n)[:, 0:D], ALU.add).then_inc(y_done, 1)
                            dve.wait_ge(y_done, 8 * i + n + 1 + START)
                            last = v.bn_stats(stat3[:, k, u, :], x)
                            if u == NT - 1:
                                last.then_inc(chain3, 1)
                                dve.wait_ge(chain3, 2 * i + k + 1)
                                dve.nop(nofuse=True)
                                for q in range(NT):
                                    last = v.bn_aggr(aggr3[:, k, q, :], stat3[:, k, q, :])
                                last.then_inc(stats3_ready, 1)
                                dve.wait_ge(rstd3_ready, 2 * i + k + 1)
                                for q in range(NT):
                                    last = v.tensor_scalar(x_in[k][:, q, :], x_in[k][:, q, :],
                                                           aggr3[:, k, q, 0:1], rstd3[:, k, q:q + 1],
                                                           ALU.subtract, ALU.mult)
                                last.then_inc(ln_done, 1)


def layouts(L0_attn_X, L0_attn_Wq, L0_attn_Wk, L0_attn_Wv, L0_attn_Wo, L0_attn_lq1, L0_attn_lk1,
            L0_attn_lq2, L0_attn_lk2, L0_attn_rms_scale, L0_ffn_norm_gamma, L0_ffn_slot_norm_gamma,
            L0_ffn_slot_embeds, L0_ffn_w1, L0_ffn_b1, L0_ffn_w2, L0_ffn_b2):
    def tiled(w):
        return w.reshape(-1, P, w.shape[1]).transpose(1, 0, 2)

    def per_head(x):
        return np.repeat(x.reshape(HG, 4, DH).transpose(1, 0, 2), DV, axis=0)

    rows = np.arange(P)
    arrays = {
        "x": L0_attn_X, "x_t": L0_attn_X.transpose(0, 2, 1),
        "w_qk": np.stack([tiled(L0_attn_Wq.T), tiled(L0_attn_Wk.T)], axis=1),
        "w_v": tiled(L0_attn_Wv.T), "w_o": tiled(L0_attn_Wo.T),
        "lam_in": np.stack([per_head(x) for x in (L0_attn_lq1, L0_attn_lq2, L0_attn_lk1, L0_attn_lk2)], 1),
        "rms_col": np.tile(L0_attn_rms_scale, 4)[:, None],
        "gamma": np.broadcast_to(L0_ffn_norm_gamma, (P, D)),
        "slot_gamma": np.broadcast_to(L0_ffn_slot_norm_gamma, (P, D)),
        "slot": L0_ffn_slot_embeds.transpose(1, 0, 2),
        "w1": L0_ffn_w1, "w2": L0_ffn_w2,
        "b1": L0_ffn_b1.reshape(E, HC, P).transpose(0, 2, 1),
        "b2": np.broadcast_to(L0_ffn_b2[:, None, :], (E, P, D)),
        "ident": np.eye(P, dtype=np.float32),
        "block32": np.kron(np.eye(4), np.full((DV, DV), 1 / DV)).astype(np.float32),
        "mask_a": np.concatenate([np.zeros((P, N - P)), np.where(rows[None] > rows[:, None], NEG, 0.0)],
                                 axis=1).astype(np.float32),
    }
    return {k: np.ascontiguousarray(v) for k, v in arrays.items()}


def kernel(**inputs):
    import concourse.bacc as bacc
    from concourse.bass_utils import run_bass_kernel_spmd

    nc = bacc.Bacc("TRN2", target_bir_lowering=False, num_devices=1)
    arrays = layouts(**{k: np.asarray(v) for k, v in inputs.items()})
    t = {k: nc.dram_tensor("in_" + k, v.shape, F32, kind="ExternalInput").ap() for k, v in arrays.items()}
    out = nc.dram_tensor("out", (NB, N, D), F32, kind="ExternalOutput").ap()
    layer(nc, t, out)
    result = run_bass_kernel_spmd(nc, [{"in_" + k: v for k, v in arrays.items()}], core_ids=[0])
    return result.results[0]["out"]
```

```python
import numpy as np
import concourse.bass as bass
from concourse import mybir
from contextlib import ExitStack

F32 = mybir.dt.float32
F32R = mybir.dt.float32r
ALU = mybir.AluOpType
ACT = mybir.ActivationFunctionType
AX = mybir.AxisListType

DBG = None
NB, N, D = 8, 512, 256
H, DH, DV = 16, 16, 32
E, S, HID = 8, 128, 1024
M = E * S
HD = H * DV
P = 128
NT, DC, HG = N // P, D // P, HD // P
STEPS = 2 * HG
HC = HID // P
LAMBDA_INIT = 0.8
EPS = 1e-5
NEG = -1e30
START = 1
PARTS = ((0, 0), (0, 1), (1, 0))


STEP_ORDER = "aBBaapaaBBTapBaSapapaapppp"
LAST_ORDER = ("pppppppBpXqqBqBBBppppppppqSqqmmqmmqmmvwwnvfffnfvxxfn2f1fv2DD"
              "2DD2ff1fDsfDff1sDffffDfffffsffff1sffff")


QK_ORDER = [k for hg in range(HG) for k in (hg, HG + hg)]


def woven(order, queues):
    queues = {letter: list(units) for letter, units in queues.items()}
    out = [queues[letter].pop(0) for letter in order if queues[letter]]
    assert not any(queues.values()), queues
    return out


def phase1_schedules():
    def score(s):
        return [("A", s, u) for u in range(10)]

    def exponentials(s):
        return [("B", s, u) for u in range(5)]

    def values(s):
        return [(kind, s, j) for kind in ("PVS", "PVV") for j in range(NT)] if s >= 0 else []

    def units(kind, count):
        return [(kind, k, 0) for k in range(count)]

    x_split, projections, v_units = [("XS", 0, 0)], [("QK", k, 0) for k in QK_ORDER], units("VP", NT)
    first = [("XL", 0, 0)] + x_split + projections + v_units + score(0) + score(1) + [("T", 0, 0)]
    turn = [("XL", 0, 0)]
    for s in range(STEPS - 1):
        turn += woven(STEP_ORDER, {
            "p": values(s - 1), "B": exponentials(s), "a": score(s + 2) if s + 2 < STEPS else [],
            "T": [("T", s + 1, 0)], "S": [("SQ", s // 2 - 1, 0)] if s and s % 2 == 0 else []})
    last = STEPS - 1
    turn += woven(LAST_ORDER, {
        "p": values(last - 1) + values(last), "B": exponentials(last), "S": [("SQ", HG - 1, 0)],
        "X": x_split, "q": projections, "v": v_units, "f": score(0) + score(1),
        "m": units("MS", 2) + units("MB", HG), "n": units("LN", 3), "w": units("WO", 2),
        "x": units("XNT", DC), "2": units("L2", 4), "1": units("L1", NT), "D": units("TD", E),
        "s": [("SL", a, b) for a in range(2) for b in range(DC)]})
    return first, turn + [("T", 0, 0)]


FIRST, TURN = phase1_schedules()
W_READER = {"QK": "dve", "VP": "act", "A": "dve", "T": "act", "MS": "act", "MB": "dve",
            "WO": "dve", "XNT": "dve", "TD": "dve"}
W_FIRST, W_UNITS = ([x for x in units if x[0] in W_READER] for units in (FIRST, TURN))
S_UNITS = [x for x in TURN if x[0] in ("B", "L2", "L1")]
U_UNITS = [x for x in TURN if x[0] == "SL" or (x[0] in ("PVS", "PVV") and x[2] == NT - 1)]
NW, NS, NU = len(W_UNITS), len(S_UNITS), len(U_UNITS)
assert NW % 2 == 0 and NS % 2 == 0 and NU % 2 == 0
assert W_FIRST[-2:] == W_UNITS[-2:]


def w_reader(unit):
    return W_READER[unit[0]]


def u_reader(unit):
    return "act" if unit[0] == "SL" or unit[1] % 2 == 0 else "dve"


def read_by(units, reader, who, upto):
    return sum(reader(x) == who for x in units[:upto])


W_DVE, W_ACT = (read_by(W_UNITS, w_reader, w, NW) for w in ("dve", "act"))
U_DVE, U_ACT = (read_by(U_UNITS, u_reader, w, NU) for w in ("dve", "act"))


def p_piece(a, j):
    return {0: (a, 512), 1: (a, 0), 3: (a, 384), 2: (4, 256 * a)}[j]


A_PIECES = []
for _a in range(4):
    A_PIECES += [[(_a, 3, 0)], [(_a, 2, 0), (_a, 0, 384)]]
A_PIECES += [[(0, 1, 0), (1, 1, 256)], [(2, 1, 0), (3, 1, 256)]]


def layer(nc, t, out, stop_after=3):
    ctx = ExitStack()
    with ctx:

        def sem(name):
            return ctx.enter_context(nc.semaphore(name))

        top = [(nc.sbuf_base + 63) // 64 * 64]

        def place(name, shape, dt, at):
            size = 4 * int(np.prod(shape[1:]))
            return nc.alloc_sbuf_tensor_at(name, shape, dt, offset=at), at + (size + 31) // 32 * 32

        def keep(name, shape, dt=F32):
            tensor, top[0] = place(name, shape, dt, top[0])
            return tensor

        ident = keep("ident", [P, P])
        powers = keep("powers", [P, 8])
        eps_col = keep("eps_col", [P, 1])
        base = top[0]
        ones = keep("ones", [P, DV])
        mask_a = keep("mask_a", [P, N])
        head_mean = keep("head_mean", [P, DV])
        head_rows = keep("head_rows", [P, P])
        neg_lam = keep("neg_lam", [P, HG])
        w_qk = [keep(f"w_qk{hl}", [P, 2, DC, HD], F32R) for hl in range(2)]
        w_v = [keep(f"w_v{hl}", [P, DC, HD], F32R) for hl in range(2)]
        w_o = [keep(f"w_o{hl}", [P, HG, D], F32R) for hl in range(2)]
        sn_t = [keep(f"sn_t{hl}", [P, DC, M], F32R) for hl in range(2)]
        gamma = keep("gamma", [P, D])
        q_stack = keep("q_stack", [P, H, N], F32R)
        k_stack = keep("k_stack", [P, H, N], F32R)
        v_sb = keep("v_sb", [P, NT, HD])
        xn_t = [keep(f"xn_t{hl}", [P, DC, N], F32R) for hl in range(2)]
        x_raw = keep("x_raw", [P, DC, N])
        x_res = keep("x_res", [P, NT, D])
        m_col = keep("m_col", [P, STEPS, 16])
        m_row = keep("m_row", [16, 2, P], F32R)
        stat = keep("stat", [P, NT, 6])
        aggr = keep("aggr", [P, NT, 2])
        small = keep("small", [P, 64])
        sumsq = keep("sumsq", [P, NT])
        p_at = top[0]
        p_sb = [keep(f"p_sb{k}", [P, 5, 1024]) for k in range(2)]
        at = p_at
        x_t, stage, on, disp, e_c, xn = [], [], [], [], [], []
        for hl in range(2):
            tensor, at = place(f"x_t{hl}", [P, DC, N], F32R, at)
            x_t.append(tensor)
        for k in range(3):
            tensor, at = place(f"stage{k}", [P, 2, N], F32R, at)
            stage.append(tensor)
        for hl in range(2):
            tensor, at = place(f"on{hl}", [P, HG, N], F32R, at)
            on.append(tensor)
        assert at <= top[0]
        at = p_at
        for hl in range(2):
            tensor, at = place(f"disp{hl}", [P, NT, M], F32R, at)
            disp.append(tensor)
        for k in range(2):
            tensor, at = place(f"e_c{k}", [P, M], F32, at)
            e_c.append(tensor)
        assert at <= top[0]
        r_at = top[0]
        o_sb, a2 = place("o_sb", [P, HG, N], F32, r_at)
        o_tmp, a2 = place("o_tmp", [P, 2, N], F32, a2)
        o_sq, a2 = place("o_sq", [P, HG, N], F32, a2)
        xn_f, a3 = place("xn_f", [P, NT, D], F32, r_at)
        slots = nc.alloc_sbuf_tensor_at("slots", [P, DC, 512], F32, offset=r_at)
        for hl in range(2):
            tensor, a3 = place(f"xn{hl}", [P, NT, D], F32R, a3)
            xn.append(tensor)
        ed_t, a3 = place("ed_t", [P, 4, N], F32, a3)
        assert max(a2, a3) <= nc.sbuf_usable_end, (max(a2, a3), nc.sbuf_usable_end)
        raw_at = p_at
        w_qk_raw, raw_at = place("w_qk_raw", [P, 2, DC, HD], F32, raw_at)
        w_v_raw, raw_at = place("w_v_raw", [P, DC, HD], F32, raw_at)
        w_o_raw, raw_at = place("w_o_raw", [P, HG, D], F32, raw_at)
        slot_raw, raw_at = place("slot_raw", [P, E, D], F32, raw_at)
        slot_n, raw_at = place("slot_n", [P, E, D], F32, raw_at)
        slot_gamma, raw_at = place("slot_gamma", [P, D], F32, raw_at)
        rms_col, raw_at = place("rms_col", [P, 1], F32, raw_at)
        lam_in, raw_at = place("lam_in", [P, 4, HG, DH], F32, raw_at)
        lam_sum, raw_at = place("lam_sum", [P, 2, HG], F32, raw_at)
        assert raw_at <= nc.sbuf_usable_end

        psum = ctx.enter_context(nc.psum_tensor("psum", [P, 8, 512], F32))
        W, SR, U = psum[:, 0:2, :], psum[:, 2:6, :], psum[:, 6:8, :]

        qk_scr = nc.dram_tensor("qk_scr", [2, 2, HD, N], F32, **({"kind": DBG} if DBG else {})).ap()
        x_scr = nc.dram_tensor("x_scr", [NB, P, NT, D], F32, **({"kind": DBG} if DBG else {})).ap()
        ec_scr = nc.dram_tensor("ec_scr", [NB, NT, P, M], F32, **({"kind": DBG} if DBG else {})).ap()
        sl_scr = nc.dram_tensor("sl_scr", [E, DC, P, NB, S], F32, **({"kind": DBG} if DBG else {})).ap()
        eo_scr = nc.dram_tensor("eo_scr", [NB, S, E, D], F32, **({"kind": DBG} if DBG else {})).ap()
        start_scr = nc.dram_tensor("start_scr", [2, 16, 16], F32).ap()

        def lo_part(eng, lo, src, hi):
            return eng.tensor_tensor(lo, src, hi.bitcast(F32), ALU.subtract)

        const_in, pro_dve, pro_pool, pro_act, pro_pe = (
            sem(x) for x in ("const_in", "pro_dve", "pro_pool", "pro_act", "pro_pe"))
        loads = [(ident, t["ident"]), (mask_a, t["mask_a"]), (head_mean, t["head_mean"]), (head_rows, t["head_rows"]), (gamma, t["gamma"]),
                 (w_qk_raw, t["w_qk"]), (w_v_raw, t["w_v"]), (w_o_raw, t["w_o"]), (slot_raw, t["slot"]),
                 (slot_gamma, t["slot_gamma"]), (rms_col, t["rms_col"]), (lam_in, t["lam_in"])]
        SN_UNITS = [(c, g) for c in range(DC) for g in range(2)]

        def sn_bank(n):
            return psum[:, n, :]

        slot_ready, squares_ready = 13, 10

        with nc.Block() as block:

            @block.sync
            def _(sp):
                for dst, src in loads:
                    sp.dma_start(dst[:], src).then_inc(const_in, 16)
                sp.wait_ge(pro_dve, 2)
                sp.wait_ge(const_in, 16 * len(loads))

            @block.vector
            def _(dve):
                v = nc.vector
                n = [0]

                def link(ins):
                    n[0] += 1
                    ins.then_inc(pro_dve, 1)
                    dve.wait_ge(pro_dve, n[0])

                link(v.memset(k_stack[:].bitcast(F32), -1.0))
                link(v.memset(q_stack[:].bitcast(F32), 0.0))
                v.memset(ones[:], 1.0)
                dve.wait_ge(const_in, 16 * len(loads))
                link(v.tensor_tensor(lam_in[:, 0:2], lam_in[:, 0:2], lam_in[:, 2:4], ALU.mult))
                link(v.reduce_sum(lam_sum[:], lam_in[:, 0:2], AX.X))
                v.tensor_copy(w_qk[0][:], w_qk_raw[:])
                link(v.tensor_copy(w_v[0][:], w_v_raw[:]))
                lo_part(v, w_qk[1][:], w_qk_raw[:], w_qk[0][:])
                lo_part(v, w_v[1][:], w_v_raw[:], w_v[0][:])
                link(v.tensor_scalar(w_o_raw[:], w_o_raw[:], rms_col[:, 0:1], 1.0 - LAMBDA_INIT,
                                     ALU.mult, ALU.mult))
                link(v.tensor_copy(w_o[0][:], w_o_raw[:]))
                lo_part(v, w_o[1][:], w_o_raw[:], w_o[0][:])
                dve.wait_ge(pro_act, 1)
                link(v.tensor_tensor(neg_lam[:], lam_sum[:, 1, :], lam_sum[:, 0, :], ALU.subtract))
                link(v.tensor_scalar(neg_lam[:], neg_lam[:], -LAMBDA_INIT, None, ALU.add))
                for e in range(E):
                    ins = v.tensor_tensor_reduce(
                        out=slot_n[:, e], in0=slot_raw[:, e], in1=slot_raw[:, e], scale=1.0, scalar=0.0,
                        op0=ALU.mult, op1=ALU.add, accum_out=small[:, e:e + 1])
                link(ins)
                assert n[0] == squares_ready
                dve.wait_ge(pro_pool, 2)
                link(v.tensor_scalar(small[:, 8:16], small[:, 8:16], 1e-12, float(D) ** -0.5,
                                     ALU.max, ALU.mult))
                link(v.reciprocal(small[:, 16:24], small[:, 8:16]))
                for e in range(E):
                    ins = v.scalar_tensor_tensor(slot_n[:, e], slot_raw[:, e], small[:, 16 + e:17 + e],
                                                 slot_gamma[:], ALU.mult, ALU.mult)
                link(ins)
                assert n[0] == slot_ready
                for k, (c, g) in enumerate(SN_UNITS):
                    dve.wait_ge(pro_act, 2 + k)
                    lo_part(v, sn_t[1][:, c, 512 * g:512 * g + 512], sn_bank(k),
                            sn_t[0][:, c, 512 * g:512 * g + 512])

            @block.gpsimd
            def _(pool):
                nc.gpsimd.memset(eps_col[:], EPS)
                nc.gpsimd.memset(powers[:, 0:4], -0.5)
                nc.gpsimd.memset(powers[:, 4:8], 0.5)
                nc.gpsimd.memset(small[:, 40:48], 0.5).then_inc(pro_pool, 1)
                pool.wait_ge(pro_pool, 1)
                pool.wait_ge(pro_dve, squares_ready)
                nc.gpsimd.tensor_tensor(small[:, 8:16], small[:, 0:8], small[:, 40:48], ALU.pow)\
                    .then_inc(pro_pool, 1)

            @block.scalar
            def _(act):
                act.wait_ge(pro_dve, 4)
                nc.scalar.activation(lam_sum[:], lam_sum[:], ACT.Exp).then_inc(pro_act, 1)
                for k, (c, g) in enumerate(SN_UNITS):
                    act.wait_ge(pro_pe, k + 1)
                    nc.scalar.activation(sn_t[0][:, c, 512 * g:512 * g + 512], sn_bank(k), ACT.Copy)\
                        .then_inc(pro_act, 1)

            @block.tensor
            def _(pe):
                pe.wait_ge(pro_dve, slot_ready)
                for k, (c, g) in enumerate(SN_UNITS):
                    for e in range(4):
                        last = nc.tensor.transpose(sn_bank(k)[:, P * e:P * e + P],
                                                   slot_n[:, 4 * g + e, P * c:P * c + P], ident[:])
                    last.then_inc(pro_pe, 1)

        (w_ready, w_dve, w_act, s_ready, s_done, u_ready, u_dve, u_act, xt_in, xt_split, qk_hi, stack_first, stack_rest,
         xres_in, masked, o_ready, squares, o_squared, r_ready, on_ready, stats_ready, rstd_ready, x_ready,
         sq_ready, norm_ready, xn_ready, xnt_hi, gneg_ready, ed_ready, td_hi, cneg_ready,
         ec_ready, x_out, chain_d, chain_p) = (sem(x) for x in (
             "w_ready w_dve w_act s_ready s_done u_ready u_dve u_act xt_in xt_split qk_hi stack_first stack_rest "
             "xres_in masked o_ready squares o_squared r_ready on_ready stats_ready rstd_ready x_ready "
             "sq_ready norm_ready xn_ready xnt_hi gneg_ready ed_ready td_hi cneg_ready "
             "ec_ready x_out chain_d chain_p").split())
        stage_out = [sem(f"stage_out{k}") for k in range(3)]
        m_row_in = [sem(f"m_row_in{k}") for k in range(2)]
        slots_out = [sem(f"slots_out{k}") for k in range(DC)]
        ec_out = [sem(f"ec_out{k}") for k in range(2)]
        STAGE_USES = [len(range(k, 8, 3)) for k in range(3)]
        stacks = (q_stack, k_stack)
        STACK_PARTS = ((0, 0, 1), (0, 1, 0))

        def ahead(i):
            return isinstance(i, int)

        def w_seq(i, kind, a, b=0):
            return (W_FIRST if ahead(i) else W_UNITS).index((kind, a, b))

        def s_seq(kind, a, b=0):
            return S_UNITS.index((kind, a, b))

        def u_seq(kind, a, b=NT - 1):
            return U_UNITS.index((kind, a, b))

        def w_bank(n):
            return W[:, n % 2, :]

        def w_unit(i, n):
            return w_bank(n if ahead(i) else n + len(W_FIRST))

        def s_unit(n):
            return SR[:, 2 * (n % 2):2 * (n % 2) + 2, :]

        def u_bank(n):
            return U[:, n % 2, :]

        def w_made(i, n):
            return w_ready, n + 1 if ahead(i) else len(W_FIRST) + i * NW + n + 1

        def w_by(i, n, who, done, per_turn):
            if ahead(i):
                return done, read_by(W_FIRST, w_reader, who, n)
            return done, (read_by(W_FIRST, w_reader, who, len(W_FIRST)) + i * per_turn
                          + read_by(W_UNITS, w_reader, who, n))

        def w_by_dve(i, n):
            return w_by(i, n, "dve", w_dve, W_DVE)

        def w_by_act(i, n):
            return w_by(i, n, "act", w_act, W_ACT)

        def w_reused(i, n):
            return n >= 2 or not ahead(i)

        def w_free(i, n):
            before = (W_FIRST if ahead(i) else W_UNITS)[n - 2]
            by = w_by_dve if w_reader(before) == "dve" else w_by_act
            return by(i, max(n - 1, 0))

        def u_by_dve(i, n):
            return u_dve, i * U_DVE + read_by(U_UNITS, u_reader, "dve", n) + START

        def u_by_act(i, n):
            return u_act, i * U_ACT + read_by(U_UNITS, u_reader, "act", n) + START

        def u_free(i, n):
            by = u_by_dve if u_reader(U_UNITS[n - 2]) == "dve" else u_by_act
            return by(i, max(n - 1, 0))

        def s_by_act(i, n):
            return s_done, i * NS + n + START

        def s_free(i, n):
            return s_by_act(i, max(n - 1, 0))

        r_rms = o_tmp[:, 0, :]

        with nc.Block() as block:

            @block.tensor
            def _(pe):
                mm = nc.tensor.matmul

                def products(out, pairs):
                    for k, (stationary, moving) in enumerate(pairs):
                        last = mm(out, stationary, moving, start=k == 0, stop=k == len(pairs) - 1)
                    return last

                def turn(i, schedule):
                    for kind, a, b in schedule:
                        if kind == "QK":
                            qk, hg = a // HG, a % HG
                            if a == 0:
                                pe.wait_ge(xt_split, 2 * (i + 1) + 2)
                            n = w_seq(i, kind, a)
                            if w_reused(i, n):
                                pe.wait_ge(*w_free(i, n))
                            products(w_unit(i, n), [
                                (w_qk[x][:, qk, c, P * hg:P * hg + P], x_t[y][:, c, :])
                                for c in range(DC) for x, y in PARTS]).then_inc(w_ready, 1)
                        elif kind == "VP":
                            n = w_seq(i, kind, a)
                            if w_reused(i, n):
                                pe.wait_ge(*w_free(i, n))
                            products(w_unit(i, n), [
                                (x_t[x][:, c, P * a:P * a + P], w_v[y][:, c, :])
                                for c in range(DC) for x, y in PARTS]).then_inc(w_ready, 1)
                        elif kind == "A":
                            if (a, b) == (0, 0):
                                pe.wait_ge(stack_first, 192 * (i + 1) + 192)
                            if (a, b) == (2, 0):
                                pe.wait_ge(stack_rest, 192 * i + 192)
                            n = w_seq(i, kind, a, b)
                            if w_reused(i, n):
                                pe.wait_ge(*w_free(i, n))
                            r, hg = 64 * (a % 2), a // 2
                            for h, qt, col in A_PIECES[b]:
                                keys = P * (qt + 1)
                                last = mm(w_unit(i, n)[:, col:col + keys],
                                          q_stack[r:r + 49, 4 * hg + h, P * qt:P * qt + P],
                                          k_stack[r:r + 49, 4 * hg + h, 0:keys], start=True, stop=True)
                            last.then_inc(w_ready, 1)
                        elif kind == "T":
                            n = w_seq(i, kind, a)
                            if w_reused(i, n):
                                pe.wait_ge(*w_free(i, n))
                            pe.wait_ge(*w_by_dve(i, 0 if a == 1 else w_seq(i, "A", a, 9) + 1))
                            nc.tensor.transpose(w_unit(i, n)[0:16, 0:P], m_col[:, a, :], ident[:])\
                                .then_inc(w_ready, 1)
                        elif kind == "B":
                            if b == 0:
                                pe.wait_ge(m_row_in[a % 2], 64 * i + 16 * (a // 2 + 1))
                            n = s_seq(kind, a, b)
                            pe.wait_ge(*s_free(i, n))
                            r, hg = 64 * (a % 2), a // 2
                            unit = s_unit(n)
                            pieces = ([(b, 1, 0, 0), (b, 3, 0, 384), (b, 0, 1, 0)] if b < 4 else
                                      [(h, 2, h // 2, 256 * (h % 2)) for h in range(4)])
                            for h, j, bank, col in pieces:
                                q0 = P * j
                                last = mm(unit[:, bank, col:col + N - q0],
                                          k_stack[r:r + 50, 4 * hg + h, q0:q0 + P],
                                          q_stack[r:r + 50, 4 * hg + h, q0:N], start=True, stop=True)
                            last.then_inc(s_ready, 1)
                        elif kind in ("PVS", "PVV"):
                            n = u_seq(kind, a, NT - 1)
                            if b == 0:
                                pe.wait_ge(masked, i * 5 * STEPS + 5 * (a + 1))
                                pe.wait_ge(*u_free(i, n))
                            hg = a // 2
                            for h in range(4):
                                unit, col = p_piece(h, b)
                                q0 = P * b
                                stationary = (ones[:] if kind == "PVS" else
                                              v_sb[:, b, DV * (4 * hg + h):DV * (4 * hg + h) + DV])
                                last = mm(u_bank(n)[DV * h:DV * h + DV, q0:N], stationary,
                                          p_sb[a % 2][:, unit, col:col + N - q0],
                                          start=b == 0, stop=b == NT - 1, skip_group_check=True)
                            if b == NT - 1:
                                last.then_inc(u_ready, 1)
                        elif kind == "MS":
                            n = w_seq(i, kind, a)
                            pe.wait_ge(*w_free(i, n))
                            pe.wait_ge(o_squared, i * HG + HG + START)
                            for hg in range(HG):
                                last = mm(w_unit(i, n)[DV * hg:DV * hg + DV, 0:N // 2], head_mean[:],
                                          o_sq[:, hg, N // 2 * a:N // 2 * a + N // 2],
                                          start=True, stop=True, skip_group_check=True)
                            last.then_inc(w_ready, 1)
                        elif kind == "MB":
                            n = w_seq(i, kind, a)
                            pe.wait_ge(*w_free(i, n))
                            pe.wait_ge(r_ready, 2 * i + 2)
                            rows = slice(DV * a, DV * a + DV)
                            mm(w_unit(i, n), head_rows[rows, :], r_rms[rows, :], start=True, stop=True)\
                                .then_inc(w_ready, 1)
                        elif kind == "WO":
                            n = w_seq(i, kind, a)
                            if w_reused(i, n):
                                pe.wait_ge(*w_free(i, n))
                            if a == 0:
                                pe.wait_ge(on_ready, i * HG + HG)
                            for k in range(2):
                                qt = 2 * a + k
                                last = products(w_unit(i, n)[:, D * k:D * k + D], [
                                    (on[x][:, hg, P * qt:P * qt + P], w_o[y][:, hg, :])
                                    for hg in range(HG) for x, y in PARTS])
                            last.then_inc(w_ready, 1)
                        elif kind == "XNT":
                            n = w_seq(i, kind, a)
                            if w_reused(i, n):
                                pe.wait_ge(*w_free(i, n))
                            pe.wait_ge(xn_ready, 2 * i + 1)
                            for k in range(NT):
                                last = nc.tensor.transpose(w_unit(i, n)[:, P * k:P * k + P],
                                                           xn_f[:, k, P * a:P * a + P], ident[:])
                            last.then_inc(w_ready, 1)
                        elif kind == "L2":
                            n = s_seq(kind, a)
                            pe.wait_ge(*s_free(i, n))
                            if a == 0:
                                pe.wait_ge(*w_by_dve(i, w_seq(i, "XNT", 1) + 1))
                            for k in range(2):
                                mt = 2 * a + k
                                last = products(s_unit(n)[:, k, :], [
                                    (sn_t[x][:, c, P * mt:P * mt + P], xn_t[y][:, c, :])
                                    for c in range(DC) for x, y in PARTS])
                            last.then_inc(s_ready, 1)
                        elif kind == "L1":
                            n = s_seq(kind, a)
                            pe.wait_ge(*s_free(i, n))
                            for k in range(2):
                                last = products(s_unit(n)[:, k, :], [
                                    (xn_t[x][:, c, P * a:P * a + P], sn_t[y][:, c, 512 * k:512 * k + 512])
                                    for c in range(DC) for x, y in PARTS])
                            last.then_inc(s_ready, 1)
                        elif kind == "TD":
                            n = w_seq(i, kind, a)
                            if w_reused(i, n):
                                pe.wait_ge(*w_free(i, n))
                            pe.wait_ge(ed_ready, i * E + a + 1)
                            for k in range(NT):
                                last = nc.tensor.transpose(w_unit(i, n)[:, P * k:P * k + P],
                                                           ed_t[:, a % 4, P * k:P * k + P], ident[:])
                            last.then_inc(w_ready, 1)
                        elif kind == "SL":
                            n = u_seq(kind, a, b)
                            pe.wait_ge(*u_free(i, n))
                            if b == 0:
                                pe.wait_ge(*w_by_dve(i, w_seq(i, "TD", 4 * a + 3) + 1))
                            if (a, b) == (0, 0):
                                pe.wait_ge(xn_ready, 2 * i + 2)
                            products(u_bank(n), [
                                (xn[x][:, k, P * b:P * b + P], disp[y][:, k, 512 * a:512 * a + 512])
                                for k in range(NT) for x, y in PARTS]).then_inc(u_ready, 1)

                turn(-1, FIRST)
                with pe.Fori(0, NB) as i:
                    turn(i, TURN)

            @block.sync
            def _(sp):
                def turn(i, schedule):
                    for kind, a, b in schedule:
                        if kind == "XL":
                            if not ahead(i):
                                sp.wait_ge(xt_split, 2 * (i + 1))
                                sp.nop(nofuse=True)
                            sp.dma_start(x_raw[:], t["x_t"][bass.ds(i + 1, 1)].rearrange(
                                "o (c p) n -> p (o c) n", p=P)).then_inc(xt_in, 16)
                            if not ahead(i):
                                sp.dma_start(x_res[:], t["x"][bass.ds(i, 1)].rearrange(
                                    "o (k p) d -> p (o k) d", p=P)).then_inc(xres_in, 16)
                        elif kind == "QK":
                            sp.wait_ge(*w_by_dve(i, w_seq(i, kind, a) + 1))
                            qk, hg, pos = a // HG, a % HG, QK_ORDER.index(a)
                            sp.dma_start(qk_scr[qk, :, P * hg:P * hg + P, :].rearrange("l p n -> p l n"),
                                         stage[pos % 3][:].bitcast(F32)).then_inc(stage_out[pos % 3], 16)
                            if pos in (1, 7):
                                for k in range(min(3, pos + 1)):
                                    sp.wait_ge(stage_out[k], 16 * ((i + 1) * STAGE_USES[k]
                                                                   + len(range(k, pos + 1, 3))))
                                    sp.nop(nofuse=True)
                                if not ahead(i):
                                    sp.wait_ge(s_ready, i * NS + s_seq("B", 1 if pos == 1 else 7, 4) + 1)
                                    sp.nop(nofuse=True)
                                loaded, g0, g1 = (stack_first, 0, 1) if pos == 1 else (stack_rest, 1, HG)
                                for q in range(2):
                                    view = qk_scr[q].rearrange("l (h m r) n -> l m r h n", m=2, r=DH)
                                    for m in range(2):
                                        for k, part in enumerate(STACK_PARTS[q]):
                                            r = 64 * m + DH * k
                                            sp.dma_start(
                                                stacks[q][r:r + DH, 4 * g0:4 * g1, :].bitcast(F32),
                                                view[part, m, :, 4 * g0:4 * g1]).then_inc(loaded, 16)
                        elif kind == "T":
                            n = w_seq(i, kind, a)
                            sp.wait_ge(*w_by_act(i, n + 1))
                            r = 64 * (a % 2) + 49
                            sp.dma_start(q_stack[r:r + 1, 4 * (a // 2):4 * (a // 2) + 4, :].bitcast(F32)
                                         .rearrange("p h (k n) -> p (h k) n", n=P),
                                         m_row[:, a % 2, :].bitcast(F32)).then_inc(m_row_in[a % 2], 16)
                        elif kind == "XNT" and a == 0:
                            sp.wait_ge(x_ready, i + 1)
                            sp.nop(nofuse=True)
                            sp.dma_start(x_scr[bass.ds(i, 1)].rearrange("o p k d -> p (o k) d"), x_res[:])\
                                .then_inc(x_out, 16)
                        elif kind == "SL":
                            sp.wait_ge(*u_by_act(i, u_seq(kind, a, b) + 1))
                            sp.nop(nofuse=True)
                            sp.dma_start(
                                sl_scr[4 * a:4 * a + 4, b, :, bass.ds(i, 1), :]
                                .rearrange("e p o s -> p (e o) s"),
                                slots[:, b, :].rearrange("p (e s) -> p e s", e=4)).then_inc(slots_out[b], 16)
                        elif kind == "L1":
                            sp.wait_ge(ec_ready, i * NT + a + 1)
                            sp.nop(nofuse=True)
                            sp.dma_start(ec_scr[bass.ds(i, 1), a].rearrange("o p m -> (o p) m"),
                                         e_c[a % 2][:]).then_inc(ec_out[a % 2], 16)
                    if ahead(i):
                        return
                    sp.wait_ge(xn_ready, 2 * i + 2)
                    sp.nop(nofuse=True)
                    for c in range(DC):
                        sp.wait_ge(slots_out[c], 32 * i + 32)
                        sp.nop(nofuse=True)
                    for k in range(2):
                        sp.wait_ge(ec_out[k], 32 * i + 32)
                        sp.nop(nofuse=True)
                    sp.wait_ge(x_out, 16 * i + 16)
                    sp.nop(nofuse=True)

                turn(-1, FIRST)
                with sp.Fori(0, NB) as i:
                    turn(i, TURN)
                sp.wait_ge(m_row_in[0], 64 * NB + 16)

            @block.scalar
            def _(act):
                ac = nc.scalar.activation
                def turn(i, schedule):
                    for kind, a, b in schedule:
                        if kind in W_READER:
                            n = w_seq(i, kind, a, b)
                        if kind == "QK":
                            pos = QK_ORDER.index(a)
                            if pos >= 3:
                                act.wait_ge(stage_out[pos % 3],
                                            16 * ((i + 1) * STAGE_USES[pos % 3] + pos // 3))
                            act.wait_ge(*w_made(i, n))
                            ac(stage[pos % 3][:, 0, :], w_unit(i, n), ACT.Copy).then_inc(qk_hi, 1)
                        elif kind == "VP":
                            act.wait_ge(*w_made(i, n))
                            ac(v_sb[:, a, :], w_unit(i, n), ACT.Copy).then_inc(w_act, 1)
                        elif kind == "T":
                            act.wait_ge(*w_made(i, n))
                            ac(m_row[:, a % 2, :], w_unit(i, n)[0:16, 0:P], ACT.Copy).then_inc(w_act, 1)
                        elif kind == "B":
                            n = s_seq(kind, a, b)
                            if b == 0 and a >= 2:
                                act.wait_ge(u_ready, i * NU + 2 * (a - 1))
                            act.wait_ge(s_ready, i * NS + n + 1)
                            ac(p_sb[a % 2][:, b, :], s_unit(n).rearrange("p k n -> p (k n)"), ACT.Exp,
                               scale=float(DH) ** -0.5).then_inc(s_done, 1)
                        elif kind in ("PVS", "PVV") and a % 2 == 0 and b == NT - 1:
                            n = u_seq(kind, a)
                            if kind == "PVS":
                                act.wait_ge(o_squared, i * HG + a // 2 + START)
                            act.wait_ge(u_ready, i * NU + n + 1)
                            ac(o_tmp[:, 0 if kind == "PVS" else 1, :], u_bank(n), ACT.Copy)\
                                .then_inc(u_act, 1)
                        elif kind == "SQ":
                            act.wait_ge(o_ready, i * HG + a + 1)
                            ac(o_sq[:, a, :], o_sq[:, a, :], ACT.Square, scale=EPS ** 0.5)
                            ac(o_tmp[:, 1, :], o_sb[:, a, :], ACT.Square).then_inc(squares, 1)
                        elif kind == "MS":
                            act.wait_ge(*w_made(i, n))
                            ac(r_rms[:, N // 2 * a:N // 2 * a + N // 2], w_unit(i, n)[:, 0:N // 2],
                               ACT.Sqrt).then_inc(w_act, 1)
                        elif kind == "XNT":
                            act.wait_ge(*w_made(i, n))
                            ac(xn_t[0][:, a, :], w_unit(i, n), ACT.Copy).then_inc(xnt_hi, 1)
                        elif kind == "L2":
                            n = s_seq(kind, a)
                            act.wait_ge(gneg_ready, i * 4 + a + 1)
                            for k in range(2):
                                mt = 2 * a + k
                                if mt >= 4:
                                    act.wait_ge(w_ready, i * NW + w_seq(i, "TD", mt - 4) + 1)
                                last = ac(ed_t[:, mt % 4, :], s_unit(n)[:, k, :], ACT.Exp,
                                          bias=small[:, 16 + mt:17 + mt],
                                          accum_out=small[:, 24 + mt:25 + mt])
                            last.then_inc(s_done, 1)
                        elif kind == "L1":
                            n = s_seq(kind, a)
                            act.wait_ge(cneg_ready, i * NT + a + 1)
                            if a >= 2:
                                act.wait_ge(ec_out[a % 2], 32 * i + 16)
                            ac(e_c[a % 2][:], s_unit(n).rearrange("p k n -> p (k n)"), ACT.Exp,
                               bias=small[:, 44 + a:45 + a],
                               accum_out=small[:, 48 + a:49 + a]).then_inc(s_done, 1)
                        elif kind == "TD":
                            if a == 0:
                                for k in range(3):
                                    act.wait_ge(stage_out[k], 16 * (i + 2) * STAGE_USES[k])
                            act.wait_ge(*w_made(i, n))
                            ac(disp[0][:, :, P * a:P * a + P], w_unit(i, n).rearrange("p (k m) -> p k m", m=P),
                               ACT.Copy).then_inc(td_hi, 1)
                        elif kind == "SL":
                            n = u_seq(kind, a, b)
                            if a:
                                act.wait_ge(slots_out[b], 32 * i + 16)
                            act.wait_ge(u_ready, i * NU + n + 1)
                            ac(slots[:, b, :], u_bank(n), ACT.Copy).then_inc(u_act, 1)

                for x in (s_done, u_act):
                    act.sem_inc(x, START)
                turn(-1, FIRST)
                with act.Fori(0, NB) as i:
                    turn(i, TURN)

            @block.gpsimd
            def _(pool):
                g = nc.gpsimd
                def turn(i, schedule):
                    for kind, a, b in schedule:
                        if kind == "B":
                            pool.wait_ge(*s_by_act(i, s_seq(kind, a, b) + 1))
                            pool.nop(nofuse=True)
                            unit = p_sb[a % 2][:, b, :]
                            if b < 4:
                                tiles = [unit[:, 0:P].rearrange("p (k n) -> p k n", n=P),
                                         unit[:, 384:384 + 2 * P].rearrange("p (k n) -> p k n", n=P)]
                            else:
                                tiles = [unit.rearrange("p (k n) -> p k n", k=4)[:, :, 0:P]]
                            for x in tiles:
                                last = g.affine_select(out=x, in_=x, compare_op=ALU.is_ge, fill=0.0, base=0,
                                                       pattern=[[0, x.shape[1]], [1, P]],
                                                       channel_multiplier=-1)
                            last.then_inc(masked, 1)
                        elif kind == "SQ":
                            pool.wait_ge(squares, i * HG + a + 1)
                            g.tensor_tensor(o_sq[:, a, :], o_sq[:, a, :], o_tmp[:, 1, :], ALU.add)\
                                .then_inc(o_squared, 1)
                        elif kind == "WO" and a == 1:
                            pool.wait_ge(stats_ready, i + 1)
                            pool.nop(nofuse=True)
                            g.tensor_scalar(small[:, 0:4], aggr[:, :, 1], EPS, None, ALU.add)\
                                .then_inc(chain_p, 1)
                            pool.wait_ge(chain_p, i + 1)
                            g.tensor_tensor(small[:, 4:8], small[:, 0:4], powers[:, 0:4], ALU.pow)\
                                .then_inc(rstd_ready, 1)
                            pool.wait_ge(sq_ready, i + 1)
                            g.tensor_tensor(small[:, 56:60], sumsq[:], powers[:, 4:8], ALU.pow)\
                                .then_inc(norm_ready, 1)

                pool.sem_inc(o_squared, START)
                turn(-1, FIRST)
                with pool.Fori(0, NB) as i:
                    turn(i, TURN)

            @block.vector
            def _(dve):
                v = nc.vector
                LINKS = 24
                def turn(i, schedule):
                    n_links = [0]

                    def link(ins):
                        n_links[0] += 1
                        ins.then_inc(chain_d, 1)
                        dve.wait_ge(chain_d, i * LINKS + n_links[0])

                    for kind, a, b in schedule:
                        if kind in W_READER:
                            n = w_seq(i, kind, a, b)
                        if kind == "XS":
                            if not ahead(i):
                                dve.wait_ge(u_ready, i * NU + u_seq("PVV", STEPS - 2) + 1)
                            dve.wait_ge(xt_in, 16 * (i + 1) + 16)
                            v.tensor_copy(x_t[0][:], x_raw[:]).then_inc(xt_split, 1)
                            dve.wait_ge(xt_split, 2 * (i + 1) + 1)
                            lo_part(v, x_t[1][:], x_raw[:], x_t[0][:]).then_inc(xt_split, 1)
                        elif kind == "QK":
                            pos = QK_ORDER.index(a)
                            dve.wait_ge(qk_hi, 8 * (i + 1) + pos + 1)
                            lo_part(v, stage[pos % 3][:, 1, :], w_unit(i, n), stage[pos % 3][:, 0, :])\
                                .then_inc(w_dve, 1)
                        elif kind == "A":
                            dve.wait_ge(*w_made(i, n))
                            dve.nop(nofuse=True)
                            for h, qt, col in A_PIECES[b]:
                                keys = P * (qt + 1)
                                last = v.tensor_tensor_reduce(
                                    out=w_unit(i, n)[:, col:col + keys], in0=w_unit(i, n)[:, col:col + keys],
                                    in1=mask_a[:, N - keys:N], scale=1.0, scalar=-3e38, op0=ALU.add,
                                    op1=ALU.max, accum_out=m_col[:, a, 4 * h + qt:4 * h + qt + 1])
                            last.then_inc(w_dve, 1)
                        elif kind == "PVS" and a % 2 and b == NT - 1:
                            n = u_seq(kind, a)
                            dve.wait_ge(*u_by_act(i, n))
                            dve.wait_ge(u_ready, i * NU + n + 1)
                            v.tensor_tensor(o_sq[:, a // 2, :], o_tmp[:, 0, :], u_bank(n), ALU.mult)
                            v.tensor_tensor(o_tmp[:, 1, :], o_tmp[:, 1, :], u_bank(n), ALU.mult)\
                                .then_inc(u_dve, 1)
                        elif kind == "PVV" and a % 2 and b == NT - 1:
                            n, hg = u_seq(kind, a), a // 2
                            dve.wait_ge(*u_by_dve(i, n))
                            dve.wait_ge(u_ready, i * NU + n + 1)
                            v.scalar_tensor_tensor(o_tmp[:, 0, :], u_bank(n), neg_lam[:, hg:hg + 1],
                                                   o_tmp[:, 0, :], ALU.mult, ALU.mult).then_inc(u_dve, 1)
                            dve.wait_ge(*u_by_dve(i, n + 1))
                            v.tensor_tensor(o_sb[:, hg, :], o_tmp[:, 0, :], o_tmp[:, 1, :], ALU.add)\
                                .then_inc(o_ready, 1)
                        elif kind == "MS":
                            dve.wait_ge(*w_by_act(i, n + 1))
                            half = r_rms[:, N // 2 * a:N // 2 * a + N // 2]
                            v.reciprocal(half, half).then_inc(r_ready, 1)
                        elif kind == "MB":
                            dve.wait_ge(*w_made(i, n))
                            v.tensor_tensor(o_sb[:, a, :], o_sb[:, a, :], w_unit(i, n), ALU.mult)\
                                .then_inc(w_dve, 1)
                            dve.wait_ge(*w_by_dve(i, n + 1))
                            link(v.tensor_copy(on[0][:, a, :], o_sb[:, a, :]))
                            lo_part(v, on[1][:, a, :], o_sb[:, a, :], on[0][:, a, :]).then_inc(on_ready, 1)
                        elif kind == "WO":
                            if a == 0:
                                dve.wait_ge(xres_in, 16 * i + 16)
                            dve.wait_ge(*w_made(i, n))
                            x2 = x_res[:, 2 * a:2 * a + 2, :]
                            v.tensor_tensor(x2, x2, w_unit(i, n).rearrange("p (k d) -> p k d", d=D), ALU.add)\
                                .then_inc(w_dve, 1)
                            dve.wait_ge(*w_by_dve(i, n + 1))
                            for k in range(2 * a, 2 * a + 2):
                                last = v.bn_stats(stat[:, k, :], x_res[:, k, :])
                            if a == 1:
                                link(last)
                                dve.nop(nofuse=True)
                                for k in range(NT):
                                    last = v.bn_aggr(aggr[:, k, :], stat[:, k, :])
                                last.then_inc(stats_ready, 1)
                        elif kind == "LN" and a == 0:
                            dve.wait_ge(rstd_ready, i + 1)
                            for k in range(NT):
                                last = v.tensor_scalar(x_res[:, k, :], x_res[:, k, :], aggr[:, k, 0:1],
                                                       small[:, 4 + k:5 + k], ALU.subtract, ALU.mult)
                            last.then_inc(x_ready, 1)
                            dve.wait_ge(x_ready, i + 1)
                            for k in range(NT):
                                last = v.tensor_tensor_reduce(
                                    out=xn_f[:, k, :], in0=x_res[:, k, :], in1=x_res[:, k, :], scale=1.0,
                                    scalar=0.0, op0=ALU.mult, op1=ALU.add, accum_out=sumsq[:, k:k + 1])
                            last.then_inc(sq_ready, 1)
                        elif kind == "LN" and a == 1:
                            dve.wait_ge(norm_ready, i + 1)
                            link(v.tensor_scalar(small[:, 56:60], small[:, 56:60], 1e-12,
                                                 float(D) ** -0.5, ALU.max, ALU.mult))
                            link(v.reciprocal(small[:, 0:4], small[:, 56:60]))
                            for k in range(NT):
                                last = v.scalar_tensor_tensor(xn_f[:, k, :], x_res[:, k, :],
                                                              small[:, k:k + 1], gamma[:],
                                                              ALU.mult, ALU.mult)
                            last.then_inc(xn_ready, 1)
                        elif kind == "LN":
                            dve.wait_ge(xn_ready, 2 * i + 1)
                            link(v.tensor_copy(xn[0][:], xn_f[:]))
                            lo_part(v, xn[1][:], xn_f[:], xn[0][:]).then_inc(xn_ready, 1)
                        elif kind == "XNT":
                            dve.wait_ge(xnt_hi, 2 * i + a + 1)
                            lo_part(v, xn_t[1][:, a, :], w_unit(i, n), xn_t[0][:, a, :]).then_inc(w_dve, 1)
                        elif kind == "L2":
                            n = s_seq(kind, a)
                            dve.wait_ge(s_ready, i * NS + n + 1)
                            link(v.reduce_max(small[:, 8 + 2 * a:10 + 2 * a], s_unit(n), AX.X))
                            v.tensor_scalar(small[:, 16 + 2 * a:18 + 2 * a], small[:, 8 + 2 * a:10 + 2 * a],
                                            -1.0, None, ALU.mult).then_inc(gneg_ready, 1)
                            dve.wait_ge(*s_by_act(i, n + 1))
                            link(v.reciprocal(small[:, 32 + 2 * a:34 + 2 * a],
                                              small[:, 24 + 2 * a:26 + 2 * a]))
                            for mt in (2 * a, 2 * a + 1):
                                v.tensor_scalar(ed_t[:, mt % 4, :], ed_t[:, mt % 4, :],
                                                small[:, 32 + mt:33 + mt], None, ALU.mult)\
                                    .then_inc(ed_ready, 1)
                        elif kind == "L1":
                            n = s_seq(kind, a)
                            dve.wait_ge(s_ready, i * NS + n + 1)
                            link(v.reduce_max(small[:, 40 + a:41 + a],
                                              s_unit(n).rearrange("p k n -> p (k n)"), AX.X))
                            v.tensor_scalar(small[:, 44 + a:45 + a], small[:, 40 + a:41 + a],
                                            -1.0, None, ALU.mult).then_inc(cneg_ready, 1)
                            dve.wait_ge(*s_by_act(i, n + 1))
                            link(v.reciprocal(small[:, 52 + a:53 + a], small[:, 48 + a:49 + a]))
                            v.tensor_scalar(e_c[a % 2][:], e_c[a % 2][:], small[:, 52 + a:53 + a], None,
                                            ALU.mult).then_inc(ec_ready, 1)
                        elif kind == "TD":
                            hi, lo = (disp[hl][:, :, P * a:P * a + P] for hl in range(2))
                            dve.wait_ge(td_hi, i * E + a + 1)
                            lo_part(v, lo, w_unit(i, n).rearrange("p (k m) -> p k m", m=P), hi)\
                                .then_inc(w_dve, 1)
                    assert ahead(i) or n_links[0] == LINKS, n_links[0]

                dve.sem_inc(u_dve, START)
                turn(-1, FIRST)
                with dve.Fori(0, NB) as i:
                    turn(i, TURN)

        if stop_after == 1:
            return

        at = base
        w1_raw, at = place("w1_raw", [P, DC, HID], F32, at)
        w2_raw, at = place("w2_raw", [P, HC, D], F32, at)
        sl_raw, at = place("sl_raw", [P, DC, NB * S], F32, at)
        w1_p, w2_p, sl_p, h_p, h_f, b1_sb, b2_sb, eo_sb = [[], []], [[], []], [[], []], [[], []], [], [], [], []
        for k in range(2):
            for hl in range(2):
                tensor, at = place(f"w1_p{k}{hl}", [P, DC, HID], F32R, at)
                w1_p[k].append(tensor)
                tensor, at = place(f"w2_p{k}{hl}", [P, HC, D], F32R, at)
                w2_p[k].append(tensor)
                tensor, at = place(f"sl_p{k}{hl}", [P, DC, NB * S], F32R, at)
                sl_p[k].append(tensor)
                tensor, at = place(f"h_p{k}{hl}", [P, HC, 512], F32R, at)
                h_p[k].append(tensor)
            tensor, at = place(f"h_f{k}", [P, 1024], F32, at)
            h_f.append(tensor)
            tensor, at = place(f"b1_sb{k}", [P, HC], F32, at)
            b1_sb.append(tensor)
            tensor, at = place(f"b2_sb{k}", [P, D], F32, at)
            b2_sb.append(tensor)
            tensor, at = place(f"eo_sb{k}", [P, 2, D], F32, at)
            eo_sb.append(tensor)
        assert at <= nc.sbuf_usable_end
        raw_split, split_link, h_ready, h_done, h_hi, h_split, eo_ready, eo_done = (
            sem(x) for x in ("raw_split split_link h_ready h_done h_hi h_split eo_ready "
                             "eo_done").split())
        raw_in = [sem(f"raw_in{q}") for q in range(3)]
        bias_in = [sem(f"bias_in{k}") for k in range(2)]
        eo_out = [sem(f"eo_out{k}") for k in range(2)]
        PAIRS = E // 2
        PAIR_ORDER = []
        for k in range(2):
            for hf in range(2):
                for u in range(4):
                    PAIR_ORDER.append(("H", k, hf, u))
                    if (hf, u) in ((0, 1), (0, 3), (1, 1)):
                        PAIR_ORDER.append(("SPLIT", k, 0, 2 * hf + u // 2))
            PAIR_ORDER += [("EO", k, hf, u) for hf in range(2) for u in range(2)]
        H_UNITS = [x for x in PAIR_ORDER if x[0] == "H"]
        EO_UNITS = [x for x in PAIR_ORDER if x[0] == "EO"]
        NH, NE = len(H_UNITS), len(EO_UNITS)
        raws = [(w1_raw, w1_p), (sl_raw, sl_p), (w2_raw, w2_p)]

        with nc.Block() as block:

            @block.sync
            def _(sp):
                def load(expert, k, biases_used=True):
                    one = bass.ds(expert, 1)
                    sources = [t["w1"][one].rearrange("o (c p) h -> p (o c) h", p=P),
                               sl_scr[one].rearrange("o c p b s -> p (o c) (b s)"),
                               t["w2"][one].rearrange("o (c p) d -> p (o c) d", p=P)]
                    for q, (raw, _) in enumerate(raws):
                        sp.wait_ge(raw_split, 3 * expert + q + START)
                        sp.nop(nofuse=True)
                        sp.dma_start(raw[:], sources[q]).then_inc(raw_in[q], 16)
                    if biases_used:
                        sp.wait_ge(eo_done, NE // 2 * (expert - 1) + START)
                        sp.nop(nofuse=True)
                    sp.dma_start(b1_sb[k][:], t["b1"][one].rearrange("o p c -> (o p) c"))\
                        .then_inc(bias_in[k], 16)
                    sp.dma_start(b2_sb[k][:], t["b2"][one].rearrange("o p d -> (o p) d"))\
                        .then_inc(bias_in[k], 16)

                load(0, 0, biases_used=False)
                with sp.Fori(0, PAIRS - 1) as i:
                    load(2 * i + 1, 1)
                    load(2 * i + 2, 0)
                load(E - 1, 1)

            @block.gpsimd
            def _(pool):
                for k in range(2):
                    pool.dma_start(start_scr[k], ident[0:16, 0:16]).then_inc(eo_out[k], 16 * START)
                with pool.Fori(0, PAIRS) as i:
                    for n, (_, k, hf, u) in enumerate(EO_UNITS):
                        pool.wait_ge(eo_done, i * NE + n + 1 + START)
                        pool.nop(nofuse=True)
                        b0 = 4 * hf + 2 * u
                        pool.dma_start(eo_scr[b0:b0 + 2, :, bass.ds(2 * i + k, 1), :]
                                       .rearrange("b s e d -> s (b e) d"), eo_sb[n % 2][:])\
                            .then_inc(eo_out[n % 2], 16)
                for k in range(2):
                    pool.wait_ge(eo_out[k], 16 * START + 16 * PAIRS * NE // 2)

            @block.tensor
            def _(pe):
                mm = nc.tensor.matmul

                def products(out, pairs):
                    for q, (stationary, moving) in enumerate(pairs):
                        last = mm(out, stationary, moving, start=q == 0, stop=q == len(pairs) - 1)
                    return last

                with pe.Fori(0, PAIRS) as i:
                    for kind, k, hf, u in PAIR_ORDER:
                        if kind == "H":
                            n = H_UNITS.index((kind, k, hf, u))
                            if (hf, u) == (0, 0):
                                pe.wait_ge(raw_split, 6 * i + 3 * k + 2 + START)
                            pe.wait_ge(h_done, i * NH + max(n - 1, 0) + START)
                            for q in range(2):
                                hc = 2 * u + q
                                last = products(s_unit(n)[:, q, :], [
                                    (w1_p[k][x][:, c, P * hc:P * hc + P],
                                     sl_p[k][y][:, c, 512 * hf:512 * hf + 512])
                                    for c in range(DC) for x, y in PARTS])
                            last.then_inc(h_ready, 1)
                        elif kind == "EO":
                            n = EO_UNITS.index((kind, k, hf, u))
                            if (hf, u) == (0, 0):
                                pe.wait_ge(raw_split, 6 * i + 3 * k + 3 + START)
                            pe.wait_ge(h_split, i * NH + 8 * k + 4 * hf + 4 + START)
                            pe.wait_ge(eo_done, i * NE + max(n - 1, 0) + START)
                            for q in range(2):
                                s0 = P * (2 * u + q)
                                last = products(w_bank(n)[:, D * q:D * q + D], [
                                    (h_p[hf][x][:, hc, s0:s0 + P], w2_p[k][y][:, hc, :])
                                    for hc in range(HC) for x, y in PARTS])
                            last.then_inc(eo_ready, 1)

            @block.scalar
            def _(act):
                act.sem_inc(h_done, START)
                with act.Fori(0, PAIRS) as i:
                    for n, (_, k, hf, u) in enumerate(H_UNITS):
                        if (hf, u) == (0, 0):
                            act.wait_ge(bias_in[k], 32 * i + 32)
                        act.wait_ge(h_split, i * NH + max(n - 1, 0) + START)
                        act.wait_ge(h_ready, i * NH + n + 1)
                        for q in range(2):
                            hc = 2 * u + q
                            last = nc.scalar.activation(h_f[n % 2][:, 512 * q:512 * q + 512],
                                                        s_unit(n)[:, q, :], ACT.Gelu,
                                                        bias=b1_sb[k][:, hc:hc + 1])
                        last.then_inc(h_done, 1)

            @block.vector
            def _(dve):
                v = nc.vector

                def split_raw(expert, k, q):
                    raw, parts = raws[q]
                    dve.wait_ge(raw_in[q], 16 * expert + 16)
                    v.tensor_copy(parts[k][0][:], raw[:]).then_inc(split_link, 1)
                    dve.wait_ge(split_link, 3 * expert + q + 1)
                    lo_part(v, parts[k][1][:], raw[:], parts[k][0][:]).then_inc(raw_split, 1)

                def turn(i, more):
                    for kind, k, hf, u in PAIR_ORDER:
                        if kind == "SPLIT":
                            if k == 0 or more:
                                split_raw(2 * i + k + 1, 1 - k, u)
                        elif kind == "H":
                            n = H_UNITS.index((kind, k, hf, u))
                            hi, lo = (h_p[hf][hl][:, 2 * u:2 * u + 2, :] for hl in range(2))
                            src = h_f[n % 2][:].rearrange("p (c n) -> p c n", c=2)
                            dve.wait_ge(h_done, i * NH + n + 1 + START)
                            v.tensor_copy(hi, src).then_inc(h_hi, 1)
                            dve.wait_ge(h_hi, i * NH + n + 1)
                            lo_part(v, lo, src, hi).then_inc(h_split, 1)
                        else:
                            n = EO_UNITS.index((kind, k, hf, u))
                            dve.wait_ge(eo_out[n % 2], 16 * (i * (NE // 2) + n // 2 + START))
                            dve.wait_ge(eo_ready, i * NE + n + 1)
                            for q in range(2):
                                last = v.tensor_tensor(eo_sb[n % 2][:, q, :],
                                                       w_bank(n)[:, D * q:D * q + D], b2_sb[k][:], ALU.add)
                            last.then_inc(eo_done, 1)

                for x in (raw_split, h_split, eo_done):
                    dve.sem_inc(x, START)
                for q in range(3):
                    split_raw(0, 0, q)
                with dve.Fori(0, PAIRS - 1) as i:
                    turn(i, True)
                turn(PAIRS - 1, False)

        if stop_after == 2:
            return

        at = base
        ec_in, eo_in, x_in, ec_p, eo_p = [], [], [], [[], []], [[], []]
        for k in range(2):
            tensor, at = place(f"ec_in{k}", [P, NT, M], F32, at)
            ec_in.append(tensor)
            tensor, at = place(f"eo_in{k}", [P, E, D], F32, at)
            eo_in.append(tensor)
            tensor, at = place(f"x_in{k}", [P, NT, D], F32, at)
            x_in.append(tensor)
            for hl in range(2):
                tensor, at = place(f"ec_p{k}{hl}", [P, E, N], F32R, at)
                ec_p[k].append(tensor)
                tensor, at = place(f"eo_p{k}{hl}", [P, E, D], F32R, at)
                eo_p[k].append(tensor)
        stat3, at = place("stat3", [P, 2, NT, 6], F32, at)
        aggr3, at = place("aggr3", [P, 2, NT, 2], F32, at)
        var3, at = place("var3", [P, 2, NT], F32, at)
        rstd3, at = place("rstd3", [P, 2, NT], F32, at)
        assert at <= nc.sbuf_usable_end
        (te_ready, te_hi, te_done, eo_hi, eo_split, y_ready, y_done, chain3, stats3_ready, rstd3_ready,
         chain3_p, ln_done) = (sem(x) for x in (
             "te_ready te_hi te_done eo_hi eo_split y_ready y_done chain3 stats3_ready rstd3_ready "
             "chain3_p ln_done").split())
        ec_loaded = [sem(f"ec_loaded{k}") for k in range(2)]
        eo_loaded = [sem(f"eo_loaded{k}") for k in range(2)]
        x_loaded = [sem(f"x_loaded{k}") for k in range(2)]
        out_stored = [sem(f"out_stored{k}") for k in range(2)]

        PREPARE3 = [("ES", 0, 0)] + [("TE", 0, u) for u in range(E)]
        ORDER3 = [("ES", 1, 0)]
        for u in range(NT):
            ORDER3 += [("Y", 0, u), ("TE", 1, 2 * u), ("TE", 1, 2 * u + 1)]
        ORDER3 += [("LN", 0, 0)]

        def batches(fori, work):
            work(-1, 1, -1, [(kind, 1, u) for kind, _, u in PREPARE3])
            with fori(0, NB // 2 - 1) as i:
                for k in range(2):
                    work(2 * i + k, k, i, ORDER3)
            work(NB - 2, 0, NB // 2 - 1, ORDER3)
            work(NB - 1, 1, NB // 2 - 1, [x for x in ORDER3 if x[1] == 0])

        with nc.Block() as block:

            @block.sync
            def _(sp):
                def load(batch, k, pair, reused=True):
                    one = bass.ds(batch, 1)
                    if reused:
                        sp.wait_ge(te_done, E * (batch - 1) + START)
                        sp.nop(nofuse=True)
                    sp.dma_start(ec_in[k][:], ec_scr[one].rearrange("o k p m -> p (o k) m"))\
                        .then_inc(ec_loaded[k], 16)
                    if reused:
                        sp.wait_ge(eo_split, batch - 1)
                        sp.nop(nofuse=True)
                    sp.dma_start(eo_in[k][:], eo_scr[one].rearrange("o s e d -> (o s) e d"))\
                        .then_inc(eo_loaded[k], 16)
                    if reused:
                        sp.wait_ge(out_stored[k], 16 * pair)
                        sp.nop(nofuse=True)
                    sp.dma_start(x_in[k][:], x_scr[one].rearrange("o p k d -> p (o k) d"))\
                        .then_inc(x_loaded[k], 16)

                for k in range(2):
                    load(k, k, 0, reused=False)
                with sp.Fori(0, NB // 2 - 1) as i:
                    for k in range(2):
                        load(2 * i + 2 + k, k, i + 1)

            @block.gpsimd
            def _(pool):
                g = nc.gpsimd
                with pool.Fori(0, NB // 2) as i:
                    for k in range(2):
                        pool.wait_ge(stats3_ready, 2 * i + k + 1)
                        pool.nop(nofuse=True)
                        g.tensor_scalar(var3[:, k, :], aggr3[:, k, :, 1], EPS, None, ALU.add)\
                            .then_inc(chain3_p, 1)
                        pool.wait_ge(chain3_p, 2 * i + k + 1)
                        g.tensor_tensor(rstd3[:, k, :], var3[:, k, :], powers[:, 0:4], ALU.pow)\
                            .then_inc(rstd3_ready, 1)
                        pool.wait_ge(ln_done, 2 * i + k + 1)
                        pool.nop(nofuse=True)
                        pool.dma_start(out[bass.ds(2 * i + k, 1)].rearrange("o (k p) d -> p (o k) d", p=P),
                                       x_in[k][:]).then_inc(out_stored[k], 16)
                for k in range(2):
                    pool.wait_ge(out_stored[k], 16 * NB // 2)

            @block.tensor
            def _(pe):
                mm = nc.tensor.matmul

                def work(batch, k, pair, order):
                    for kind, ahead_by, u in order:
                        if kind == "TE":
                            b, kb, pb = batch + 1, 1 - k, pair + k
                            if u == 0:
                                pe.wait_ge(ec_loaded[kb], 16 * pb + 16)
                            pe.wait_ge(te_done, E * b + max(u - 1, 0) + START)
                            for q in range(NT):
                                last = nc.tensor.transpose(w_bank(u)[:, P * q:P * q + P],
                                                           ec_in[kb][:, q, P * u:P * u + P], ident[:])
                            last.then_inc(te_ready, 1)
                        elif kind == "Y":
                            if u == 0:
                                pe.wait_ge(te_done, E * batch + E + START)
                                pe.wait_ge(eo_split, batch + 1)
                            pe.wait_ge(y_done, NT * batch + max(u - 1, 0) + START)
                            pairs = [(ec_p[k][x][:, j, P * u:P * u + P], eo_p[k][y][:, j, :])
                                     for j in range(E) for x, y in PARTS]
                            for q, (stationary, moving) in enumerate(pairs):
                                last = mm(u_bank(u)[:, 0:D], stationary, moving, start=q == 0,
                                          stop=q == len(pairs) - 1)
                            last.then_inc(y_ready, 1)

                batches(pe.Fori, work)

            @block.scalar
            def _(act):
                def work(batch, k, pair, order):
                    for kind, ahead_by, u in order:
                        b, kb, pb = batch + 1, 1 - k, pair + k
                        if kind == "ES":
                            act.wait_ge(eo_loaded[kb], 16 * pb + 16)
                            nc.scalar.activation(eo_p[kb][0][:], eo_in[kb][:], ACT.Copy).then_inc(eo_hi, 1)
                        elif kind == "TE":
                            act.wait_ge(te_ready, E * b + u + 1)
                            nc.scalar.activation(ec_p[kb][0][:, u, :], w_bank(u), ACT.Copy)\
                                .then_inc(te_hi, 1)

                batches(act.Fori, work)

            @block.vector
            def _(dve):
                v = nc.vector
                for x in (te_done, y_done):
                    dve.sem_inc(x, START)

                def work(batch, k, pair, order):
                    for kind, ahead_by, u in order:
                        b, kb, pb = batch + 1, 1 - k, pair + k
                        if kind == "ES":
                            dve.wait_ge(eo_hi, b + 1)
                            lo_part(v, eo_p[kb][1][:], eo_in[kb][:], eo_p[kb][0][:]).then_inc(eo_split, 1)
                        elif kind == "TE":
                            dve.wait_ge(te_hi, E * b + u + 1)
                            lo_part(v, ec_p[kb][1][:, u, :], w_bank(u), ec_p[kb][0][:, u, :])\
                                .then_inc(te_done, 1)
                        elif kind == "Y":
                            x = x_in[k][:, u, :]
                            if u == 0:
                                dve.wait_ge(x_loaded[k], 16 * pair + 16)
                            dve.wait_ge(y_ready, NT * batch + u + 1)
                            v.tensor_tensor(x, x, u_bank(u)[:, 0:D], ALU.add).then_inc(y_done, 1)
                            dve.wait_ge(y_done, NT * batch + u + 1 + START)
                            last = v.bn_stats(stat3[:, k, u, :], x)
                            if u == NT - 1:
                                last.then_inc(chain3, 1)
                                dve.wait_ge(chain3, batch + 1)
                                dve.nop(nofuse=True)
                                for q in range(NT):
                                    last = v.bn_aggr(aggr3[:, k, q, :], stat3[:, k, q, :])
                                last.then_inc(stats3_ready, 1)
                        else:
                            dve.wait_ge(rstd3_ready, batch + 1)
                            for q in range(NT):
                                last = v.tensor_scalar(x_in[k][:, q, :], x_in[k][:, q, :],
                                                       aggr3[:, k, q, 0:1], rstd3[:, k, q:q + 1],
                                                       ALU.subtract, ALU.mult)
                            last.then_inc(ln_done, 1)

                batches(dve.Fori, work)


def layouts(L0_attn_X, L0_attn_Wq, L0_attn_Wk, L0_attn_Wv, L0_attn_Wo, L0_attn_lq1, L0_attn_lk1,
            L0_attn_lq2, L0_attn_lk2, L0_attn_rms_scale, L0_ffn_norm_gamma, L0_ffn_slot_norm_gamma,
            L0_ffn_slot_embeds, L0_ffn_w1, L0_ffn_b1, L0_ffn_w2, L0_ffn_b2):
    def tiled(w):
        return w.reshape(-1, P, w.shape[1]).transpose(1, 0, 2)

    def per_head(x):
        return np.repeat(x.reshape(HG, 4, DH).transpose(1, 0, 2), DV, axis=0)

    rows = np.arange(P)
    arrays = {
        "x": L0_attn_X,
        "x_t": L0_attn_X.transpose(0, 2, 1)[list(range(NB)) + [0]],
        "w_qk": np.stack([tiled(L0_attn_Wq.T), tiled(L0_attn_Wk.T)], axis=1),
        "w_v": tiled(L0_attn_Wv.T), "w_o": tiled(L0_attn_Wo.T),
        "lam_in": np.stack([per_head(x) for x in (L0_attn_lq1, L0_attn_lq2, L0_attn_lk1, L0_attn_lk2)], 1),
        "rms_col": np.tile(L0_attn_rms_scale, 4)[:, None],
        "gamma": np.broadcast_to(L0_ffn_norm_gamma, (P, D)),
        "slot_gamma": np.broadcast_to(L0_ffn_slot_norm_gamma, (P, D)),
        "slot": L0_ffn_slot_embeds.transpose(1, 0, 2),
        "w1": L0_ffn_w1, "w2": L0_ffn_w2,
        "b1": L0_ffn_b1.reshape(E, HC, P).transpose(0, 2, 1),
        "b2": np.broadcast_to(L0_ffn_b2[:, None, :], (E, P, D)),
        "ident": np.eye(P, dtype=np.float32),
        "head_mean": np.kron(np.eye(4), np.full((DV, DV // 4), 1 / DV)).astype(np.float32),
        "head_rows": np.tile(np.kron(np.eye(4), np.eye(DV // 4, 1) @ np.ones((1, DV))), (HG, 1))
        .astype(np.float32),
        "mask_a": np.concatenate([np.zeros((P, N - P)), np.where(rows[None] > rows[:, None], NEG, 0.0)],
                                 axis=1).astype(np.float32),
    }
    return {k: np.ascontiguousarray(v) for k, v in arrays.items()}


def kernel(**inputs):
    import concourse.bacc as bacc
    from concourse.bass_utils import run_bass_kernel_spmd

    nc = bacc.Bacc("TRN2", target_bir_lowering=False, num_devices=1)
    arrays = layouts(**{k: np.asarray(v) for k, v in inputs.items()})
    t = {k: nc.dram_tensor("in_" + k, v.shape, F32, kind="ExternalInput").ap() for k, v in arrays.items()}
    out = nc.dram_tensor("out", (NB, N, D), F32, kind="ExternalOutput").ap()
    layer(nc, t, out)
    result = run_bass_kernel_spmd(nc, [{"in_" + k: v for k, v in arrays.items()}], core_ids=[0])
    return result.results[0]["out"]
```

```python
import numpy as np
import concourse.bass as bass
from concourse import mybir
from contextlib import ExitStack

F32 = mybir.dt.float32
F32R = mybir.dt.float32r
ALU = mybir.AluOpType
ACT = mybir.ActivationFunctionType
AX = mybir.AxisListType

NB, N, D = 8, 512, 256
H, DH, DV = 16, 16, 32
E, S, HID = 8, 128, 1024
M = E * S
HD = H * DV
P = 128
NT, DC, HG = N // P, D // P, HD // P
STEPS = 2 * HG
HC = HID // P
LAMBDA_INIT = 0.8
EPS = 1e-5
NEG = -1e30
S_START = 3
START = 1
PARTS = ((0, 0), (0, 1), (1, 0))


STEP_ORDER = "BBaBapaaBaaBpTaBppBapaaBBBpaSpp"
LAST_ORDER = ("pppppBpppBBBXBqqBBBBBqppppppppqSmqqvmmmqmqwwfnfvnffxnxvf2rf2"
              "f2frrDfD21rvc2Df2frD1rsfD1c2rft2rfDscfDDf1scfsfffffff")


QK_ORDER = [k for hg in range(HG) for k in (hg, HG + hg)]


B_UNITS = 10


def woven(order, queues):
    queues = {letter: list(units) for letter, units in queues.items()}
    out = [queues[letter].pop(0) for letter in order if queues[letter]]
    assert not any(queues.values()), queues
    return out


def phase1_schedules():
    def score(s):
        return [("A", s, u) for u in range(10)]

    def exponentials(s):
        return [("B", s, u) for u in range(B_UNITS)]

    def values(s):
        return [(kind, s, j) for kind in ("PVS", "PVV") for j in range(NT)] if s >= 0 else []

    def units(kind, count):
        return [(kind, k, 0) for k in range(count)]

    x_split, projections, v_units = [("XS", 0, 0)], [("QK", k, 0) for k in QK_ORDER], units("VP", NT)
    first = [("XL", 0, 0)] + x_split + woven("qqvvqqvvqqqq", {"q": projections, "v": v_units})
    first += score(0) + [("T", 0, 0)] + score(1)
    turn = [("XL", 0, 0)]
    for s in range(STEPS - 1):
        turn += woven(STEP_ORDER, {
            "p": values(s - 1), "B": exponentials(s), "a": score(s + 2) if s + 2 < STEPS else [],
            "T": [("T", s + 1, 0)], "S": [("SQ", s // 2 - 1, 0)] if s and s % 2 == 0 else []})
    last = STEPS - 1
    turn += woven(LAST_ORDER, {
        "p": values(last - 1) + values(last), "B": exponentials(last), "S": [("SQ", HG - 1, 0)],
        "X": x_split, "t": [("T", 0, 0)], "q": projections, "v": v_units, "f": score(0) + score(1),
        "m": units("MS", 1) + units("MB", HG), "n": units("LN", 3), "w": units("WO", 2),
        "x": units("XNT", DC), "2": units("L2", E), "r": units("DN", E), "1": units("L1", NT),
        "c": units("CN", NT), "D": units("TD", E),
        "s": [("SL", a, b) for a in range(2) for b in range(DC)]})
    ahead = x_split + projections + v_units + score(0) + score(1) + [("T", 0, 0)]
    return first, turn, [x for x in turn if x not in ahead]


FIRST, TURN, LAST = phase1_schedules()
W_READER = {"QK": "dve", "VP": "act", "A": "dve", "T": "act", "MS": "act", "MB": "dve",
            "WO": "dve", "XNT": "dve", "TD": "dve"}
W_FIRST, W_UNITS, W_LAST = ([x for x in units if x[0] in W_READER] for units in (FIRST, TURN, LAST))
S_UNITS = [(kind, a, b + half) for kind, a, b in TURN if kind in ("B", "L2", "L1")
           for half in range(2 if kind == "L1" else 1)]
U_UNITS = [x for x in TURN if x[0] == "SL" or (x[0] in ("PVS", "PVV") and x[2] == NT - 1)]
NW, NS, NU = len(W_UNITS), len(S_UNITS), len(U_UNITS)
assert NW % 3 == 0 and NS % 3 == 0 and NU % 2 == 0
assert W_FIRST[-3:] == W_UNITS[-3:]


def w_reader(unit):
    return W_READER[unit[0]]


def u_reader(unit):
    return "act" if unit[0] == "SL" or unit[1] % 2 == 0 else "dve"


def read_by(units, reader, who, upto):
    return sum(reader(x) == who for x in units[:upto])


W_DVE, W_ACT = (read_by(W_UNITS, w_reader, w, NW) for w in ("dve", "act"))
U_DVE, U_ACT = (read_by(U_UNITS, u_reader, w, NU) for w in ("dve", "act"))


def p_piece(a, j):
    return {0: (a, 512), 1: (a, 0), 3: (a, 384), 2: (4, 256 * a)}[j]


A_PIECES = []
for _a in range(4):
    A_PIECES += [[(_a, 3, 0)], [(_a, 2, 0), (_a, 0, 384)]]
A_PIECES += [[(0, 1, 0), (1, 1, 256)], [(2, 1, 0), (3, 1, 256)]]


def b_pieces(u):
    if u < 8:
        return [(u // 2, 0, 0)] if u % 2 else [(u // 2, 1, 0), (u // 2, 3, 384)]
    return [(2 * (u - 8) + k, 2, 256 * k) for k in range(2)]


def layer(nc, t, out, stop_after=3):
    ctx = ExitStack()
    with ctx:

        def sem(name):
            return ctx.enter_context(nc.semaphore(name))

        top = [(nc.sbuf_base + 63) // 64 * 64]

        def place(name, shape, dt, at):
            size = 4 * int(np.prod(shape[1:]))
            return nc.alloc_sbuf_tensor_at(name, shape, dt, offset=at), at + (size + 31) // 32 * 32

        def keep(name, shape, dt=F32):
            tensor, top[0] = place(name, shape, dt, top[0])
            return tensor

        ident = keep("ident", [P, P])
        powers = keep("powers", [P, 8])
        base = top[0]
        ones = keep("ones", [P, DV])
        mask_a = keep("mask_a", [P, N])
        head_mean = keep("head_mean", [P, DV])
        head_rows = keep("head_rows", [P, P])
        neg_lam = keep("neg_lam", [P, HG])
        w_qk = [keep(f"w_qk{hl}", [P, 2, DC, HD], F32R) for hl in range(2)]
        w_v = [keep(f"w_v{hl}", [P, DC, HD], F32R) for hl in range(2)]
        w_o = [keep(f"w_o{hl}", [P, HG, D], F32R) for hl in range(2)]
        sn_t = [keep(f"sn_t{hl}", [P, DC, M], F32R) for hl in range(2)]
        gamma = keep("gamma", [P, D])
        q_stack = keep("q_stack", [P, H, N], F32R)
        k_stack = keep("k_stack", [P, H, N], F32R)
        v_sb = keep("v_sb", [P, NT, HD])
        xn_t = [keep(f"xn_t{hl}", [P, DC, N], F32R) for hl in range(2)]
        x_raw = keep("x_raw", [P, DC, N])
        x_res = keep("x_res", [P, NT, D])
        m_col = keep("m_col", [P, STEPS, 16])
        m_row = keep("m_row", [16, 2, P], F32R)
        stat = keep("stat", [P, NT, 6])
        aggr = keep("aggr", [P, NT, 2])
        small = keep("small", [P, 80])
        sumsq = keep("sumsq", [P, NT])
        p_at = top[0]
        p_sb = [keep(f"p_sb{k}", [P, 5, 1024]) for k in range(2)]
        at = p_at
        x_t, stage, on, disp, e_c, xn = [], [], [], [], [], []
        for hl in range(2):
            tensor, at = place(f"x_t{hl}", [P, DC, N], F32R, at)
            x_t.append(tensor)
        for k in range(3):
            tensor, at = place(f"stage{k}", [P, 2, N], F32R, at)
            stage.append(tensor)
        for hl in range(2):
            tensor, at = place(f"on{hl}", [P, HG, N], F32R, at)
            on.append(tensor)
        assert at <= top[0]
        at = p_at
        for hl in range(2):
            tensor, at = place(f"disp{hl}", [P, NT, M], F32R, at)
            disp.append(tensor)
        for k in range(2):
            tensor, at = place(f"e_c{k}", [P, M], F32, at)
            e_c.append(tensor)
        assert at <= top[0]
        r_at = top[0]
        o_sb, a2 = place("o_sb", [P, HG, N], F32, r_at)
        o_tmp, a2 = place("o_tmp", [P, 2, N], F32, a2)
        o_sq, a2 = place("o_sq", [P, HG, N], F32, a2)
        xn_f, a3 = place("xn_f", [P, NT, D], F32, r_at)
        slots = nc.alloc_sbuf_tensor_at("slots", [P, DC, 512], F32, offset=r_at)
        for hl in range(2):
            tensor, a3 = place(f"xn{hl}", [P, NT, D], F32R, a3)
            xn.append(tensor)
        ed_t, a3 = place("ed_t", [P, 4, N], F32, a3)
        assert max(a2, a3) <= nc.sbuf_usable_end, (max(a2, a3), nc.sbuf_usable_end)
        raw_at = p_at
        w_qk_raw, raw_at = place("w_qk_raw", [P, 2, DC, HD], F32, raw_at)
        w_v_raw, raw_at = place("w_v_raw", [P, DC, HD], F32, raw_at)
        w_o_raw, raw_at = place("w_o_raw", [P, HG, D], F32, raw_at)
        slot_raw, raw_at = place("slot_raw", [P, E, D], F32, raw_at)
        slot_n, raw_at = place("slot_n", [P, E, D], F32, raw_at)
        slot_gamma, raw_at = place("slot_gamma", [P, D], F32, raw_at)
        rms_col, raw_at = place("rms_col", [P, 1], F32, raw_at)
        lam_in, raw_at = place("lam_in", [P, 4, HG, DH], F32, raw_at)
        lam_sum, raw_at = place("lam_sum", [P, 2, HG], F32, raw_at)
        assert raw_at <= nc.sbuf_usable_end

        psum = ctx.enter_context(nc.psum_tensor("psum", [P, 8, 512], F32))

        qk_scr = nc.dram_tensor("qk_scr", [2, 2, HD, N], F32).ap()
        x_scr = nc.dram_tensor("x_scr", [NB, P, NT, D], F32).ap()
        ec_scr = nc.dram_tensor("ec_scr", [NB, NT, P, M], F32).ap()
        sl_scr = nc.dram_tensor("sl_scr", [E, DC, P, NB, S], F32).ap()
        eo_scr = nc.dram_tensor("eo_scr", [NB, S, E, D], F32).ap()
        start_scr = nc.dram_tensor("start_scr", [2, 16, 16], F32).ap()

        def lo_part(eng, lo, src, hi):
            return eng.tensor_tensor(lo, src, hi.bitcast(F32), ALU.subtract)

        slot_in, const_in, pro_dve, pro_pool, pro_const, pro_act, pro_pe = (
            sem(x) for x in ("slot_in", "const_in", "pro_dve", "pro_pool", "pro_const", "pro_act", "pro_pe"))
        slot_loads = [(slot_raw, t["slot"]), (slot_gamma, t["slot_gamma"]), (ident, t["ident"])]
        const_loads = [(w_qk_raw, t["w_qk"]), (w_v_raw, t["w_v"]), (lam_in, t["lam_in"]),
                       (w_o_raw, t["w_o"]), (rms_col, t["rms_col"]), (mask_a, t["mask_a"]),
                       (head_mean, t["head_mean"]), (head_rows, t["head_rows"]), (gamma, t["gamma"])]
        SN_UNITS = [(c, g) for c in range(DC) for g in range(2)]

        def sn_bank(n):
            return psum[:, n, :]

        squares_ready, slot_ready, dots_ready = 1, 4, 6

        with nc.Block() as block:

            @block.sync
            def _(sp):
                for dst, src in slot_loads:
                    sp.dma_start(dst[:], src).then_inc(slot_in, 16)
                for dst, src in const_loads:
                    sp.dma_start(dst[:], src).then_inc(const_in, 16)
                sp.wait_ge(pro_pool, 3)
                sp.wait_ge(slot_in, 16 * len(slot_loads))
                sp.wait_ge(const_in, 16 * len(const_loads))

            @block.vector
            def _(dve):
                v = nc.vector
                n = [0]

                def link(ins):
                    n[0] += 1
                    ins.then_inc(pro_dve, 1)
                    dve.wait_ge(pro_dve, n[0])

                v.memset(ones[:], 1.0)
                dve.wait_ge(slot_in, 16 * len(slot_loads))
                for e in range(E):
                    ins = v.tensor_tensor_reduce(
                        out=slot_n[:, e], in0=slot_raw[:, e], in1=slot_raw[:, e], scale=1.0, scalar=0.0,
                        op0=ALU.mult, op1=ALU.add, accum_out=small[:, e:e + 1])
                link(ins)
                assert n[0] == squares_ready
                dve.wait_ge(pro_pool, 1)
                link(v.tensor_scalar(small[:, 8:16], small[:, 8:16], 1e-12, float(D) ** -0.5,
                                     ALU.max, ALU.mult))
                link(v.reciprocal(small[:, 16:24], small[:, 8:16]))
                for e in range(E):
                    ins = v.scalar_tensor_tensor(slot_n[:, e], slot_raw[:, e], small[:, 16 + e:17 + e],
                                                 slot_gamma[:], ALU.mult, ALU.mult)
                link(ins)
                assert n[0] == slot_ready
                dve.wait_ge(const_in, 16 * len(const_loads))
                link(v.tensor_tensor(lam_in[:, 0:2], lam_in[:, 0:2], lam_in[:, 2:4], ALU.mult))
                link(v.reduce_sum(lam_sum[:], lam_in[:, 0:2], AX.X))
                assert n[0] == dots_ready
                v.tensor_copy(w_qk[0][:], w_qk_raw[:])
                link(v.tensor_copy(w_v[0][:], w_v_raw[:]))
                lo_part(v, w_qk[1][:], w_qk_raw[:], w_qk[0][:])
                lo_part(v, w_v[1][:], w_v_raw[:], w_v[0][:])
                link(v.tensor_scalar(w_o_raw[:], w_o_raw[:], rms_col[:, 0:1], 1.0 - LAMBDA_INIT,
                                     ALU.mult, ALU.mult))
                link(v.tensor_copy(w_o[0][:], w_o_raw[:]))
                lo_part(v, w_o[1][:], w_o_raw[:], w_o[0][:])
                for k, (c, g) in enumerate(SN_UNITS):
                    dve.wait_ge(pro_act, 1 + k)
                    lo_part(v, sn_t[1][:, c, 512 * g:512 * g + 512], sn_bank(k),
                            sn_t[0][:, c, 512 * g:512 * g + 512])
                dve.wait_ge(pro_act, len(SN_UNITS) + 1)
                link(v.tensor_tensor(neg_lam[:], lam_sum[:, 1, :], lam_sum[:, 0, :], ALU.subtract))
                link(v.tensor_scalar(neg_lam[:], neg_lam[:], -LAMBDA_INIT, None, ALU.add))

            @block.gpsimd
            def _(pool):
                g = nc.gpsimd
                g.memset(powers[:, 0:4], -0.5)
                g.memset(powers[:, 4:8], 0.5)
                g.memset(small[:, 40:48], 0.5).then_inc(pro_const, 1)
                pool.wait_ge(pro_const, 1)
                pool.wait_ge(pro_dve, squares_ready)
                g.tensor_tensor(small[:, 8:16], small[:, 0:8], small[:, 40:48], ALU.pow)\
                    .then_inc(pro_pool, 1)
                g.memset(q_stack[:].bitcast(F32), 0.0).then_inc(pro_pool, 1)
                g.memset(k_stack[:].bitcast(F32), -1.0).then_inc(pro_pool, 1)

            @block.scalar
            def _(act):
                for k, (c, g) in enumerate(SN_UNITS):
                    act.wait_ge(pro_pe, k + 1)
                    nc.scalar.activation(sn_t[0][:, c, 512 * g:512 * g + 512], sn_bank(k), ACT.Copy)\
                        .then_inc(pro_act, 1)
                act.wait_ge(pro_dve, dots_ready)
                nc.scalar.activation(lam_sum[:], lam_sum[:], ACT.Exp).then_inc(pro_act, 1)

            @block.tensor
            def _(pe):
                pe.wait_ge(pro_dve, slot_ready)
                for k, (c, g) in enumerate(SN_UNITS):
                    for e in range(4):
                        last = nc.tensor.transpose(sn_bank(k)[:, P * e:P * e + P],
                                                   slot_n[:, 4 * g + e, P * c:P * c + P], ident[:])
                    last.then_inc(pro_pe, 1)

        (w_ready, w_dve, w_act, s_ready, s_done, u_ready, u_dve, u_act, xt_in, xt_split, qk_hi, stack_first, stack_rest,
         xres_in, masked, o_ready, squares, o_squared, r_ready, on_ready, stats_ready, rstd_ready, x_ready,
         sq_ready, norm_ready, xn_ready, xnt_hi, gneg_ready, ed_ready, td_hi, cneg_ready,
         ec_ready, x_out, chain_d, chain_p) = (sem(x) for x in (
             "w_ready w_dve w_act s_ready s_done u_ready u_dve u_act xt_in xt_split qk_hi stack_first stack_rest "
             "xres_in masked o_ready squares o_squared r_ready on_ready stats_ready rstd_ready x_ready "
             "sq_ready norm_ready xn_ready xnt_hi gneg_ready ed_ready td_hi cneg_ready "
             "ec_ready x_out chain_d chain_p").split())
        stage_out = [sem(f"stage_out{k}") for k in range(3)]
        m_row_in = [sem(f"m_row_in{k}") for k in range(2)]
        slots_out = [sem(f"slots_out{k}") for k in range(DC)]
        ec_out = [sem(f"ec_out{k}") for k in range(2)]
        STAGE_USES = [len(range(k, 8, 3)) for k in range(3)]
        stacks = (q_stack, k_stack)
        STACK_PARTS = ((0, 0, 1), (0, 1, 0))

        def last_turn(i):
            return isinstance(i, int) and i == NB - 1

        def ahead(i):
            return isinstance(i, int) and i < 0

        def w_units(i):
            return W_FIRST if ahead(i) else W_LAST if last_turn(i) else W_UNITS

        def w_seq(i, kind, a, b=0):
            return w_units(i).index((kind, a, b))

        def s_seq(kind, a, b=0):
            return S_UNITS.index((kind, a, b))

        def u_seq(kind, a, b=NT - 1):
            return U_UNITS.index((kind, a, b))

        def w_bank(n):
            return psum[:, n % 2, :]

        def w_unit(i, n):
            return psum[:, (n if ahead(i) else n + len(W_FIRST)) % 3, :]

        def s_bank(n):
            return psum[:, 3 + n % 3, :]

        def s_unit(n):
            return psum[:, 2 + 2 * (n % 2):4 + 2 * (n % 2), :]

        def u_bank(n):
            return psum[:, 6 + n % 2, :]

        def w_made(i, n):
            return w_ready, n + 1 if ahead(i) else len(W_FIRST) + i * NW + n + 1

        def w_by(i, n, who, done, per_turn):
            if ahead(i):
                return done, read_by(W_FIRST, w_reader, who, n)
            units = w_units(i)
            if n < 0:
                i, n, units = i - 1, NW + n, W_UNITS
            return done, (read_by(W_FIRST, w_reader, who, len(W_FIRST)) + i * per_turn
                          + read_by(units, w_reader, who, n))

        def w_by_dve(i, n):
            return w_by(i, n, "dve", w_dve, W_DVE)

        def w_by_act(i, n):
            return w_by(i, n, "act", w_act, W_ACT)

        def w_reused(i, n):
            return n >= 3 or not ahead(i)

        def w_free(i, n):
            before = w_units(i)[n - 3] if n >= 3 else W_UNITS[n - 3]
            by = w_by_dve if w_reader(before) == "dve" else w_by_act
            return by(i, n - 2)

        def u_by_dve(i, n):
            return u_dve, i * U_DVE + read_by(U_UNITS, u_reader, "dve", n) + START

        def u_by_act(i, n):
            return u_act, i * U_ACT + read_by(U_UNITS, u_reader, "act", n) + START

        def u_free(i, n):
            by = u_by_dve if u_reader(U_UNITS[n - 2]) == "dve" else u_by_act
            return by(i, max(n - 1, 0))

        def s_by_act(i, n):
            return s_done, i * NS + n + S_START

        def s_free(i, n):
            return s_by_act(i, n - 2)

        r_rms = o_tmp[:, 0, :]

        with nc.Block() as block:

            @block.tensor
            def _(pe):
                mm = nc.tensor.matmul

                def products(out, pairs):
                    for k, (stationary, moving) in enumerate(pairs):
                        last = mm(out, stationary, moving, start=k == 0, stop=k == len(pairs) - 1)
                    return last

                def turn(i, schedule):
                    for kind, a, b in schedule:
                        if kind == "QK":
                            qk, hg = a // HG, a % HG
                            if a == 0:
                                pe.wait_ge(xt_split, 2 * (i + 1) + 2)
                            n = w_seq(i, kind, a)
                            if w_reused(i, n):
                                pe.wait_ge(*w_free(i, n))
                            products(w_unit(i, n), [
                                (w_qk[x][:, qk, c, P * hg:P * hg + P], x_t[y][:, c, :])
                                for c in range(DC) for x, y in PARTS]).then_inc(w_ready, 1)
                        elif kind == "VP":
                            n = w_seq(i, kind, a)
                            if w_reused(i, n):
                                pe.wait_ge(*w_free(i, n))
                            products(w_unit(i, n), [
                                (x_t[x][:, c, P * a:P * a + P], w_v[y][:, c, :])
                                for c in range(DC) for x, y in PARTS]).then_inc(w_ready, 1)
                        elif kind == "A":
                            if (a, b) == (0, 0):
                                pe.wait_ge(stack_first, 192 * (i + 1) + 192)
                            if (a, b) == (2, 0):
                                pe.wait_ge(stack_rest, 192 * i + 192)
                            n = w_seq(i, kind, a, b)
                            if w_reused(i, n):
                                pe.wait_ge(*w_free(i, n))
                            r, hg = 64 * (a % 2), a // 2
                            for h, qt, col in A_PIECES[b]:
                                keys = P * (qt + 1)
                                last = mm(w_unit(i, n)[:, col:col + keys],
                                          q_stack[r:r + 49, 4 * hg + h, P * qt:P * qt + P],
                                          k_stack[r:r + 49, 4 * hg + h, 0:keys], start=True, stop=True)
                            last.then_inc(w_ready, 1)
                        elif kind == "T":
                            n = w_seq(i, kind, a)
                            if w_reused(i, n):
                                pe.wait_ge(*w_free(i, n))
                            pe.wait_ge(*w_by_dve(i, 0 if a == 1 else w_seq(i, "A", a, 9) + 1))
                            nc.tensor.transpose(w_unit(i, n)[0:16, 0:P], m_col[:, a, :], ident[:])\
                                .then_inc(w_ready, 1)
                        elif kind == "B":
                            if b == 0:
                                pe.wait_ge(m_row_in[a % 2], 64 * i + 16 * (a // 2 + 1))
                            n = s_seq(kind, a, b)
                            pe.wait_ge(*s_free(i, n))
                            r, hg = 64 * (a % 2), a // 2
                            for h, j, col in b_pieces(b):
                                q0 = P * j
                                last = mm(s_bank(n)[:, col:col + N - q0],
                                          k_stack[r:r + 50, 4 * hg + h, q0:q0 + P],
                                          q_stack[r:r + 50, 4 * hg + h, q0:N], start=True, stop=True)
                            last.then_inc(s_ready, 1)
                        elif kind in ("PVS", "PVV"):
                            n = u_seq(kind, a, NT - 1)
                            if b == 0:
                                pe.wait_ge(masked, i * B_UNITS * STEPS + B_UNITS * (a + 1))
                                pe.wait_ge(*u_free(i, n))
                            hg = a // 2
                            for h in range(4):
                                unit, col = p_piece(h, b)
                                q0 = P * b
                                stationary = (ones[:] if kind == "PVS" else
                                              v_sb[:, b, DV * (4 * hg + h):DV * (4 * hg + h) + DV])
                                last = mm(u_bank(n)[DV * h:DV * h + DV, q0:N], stationary,
                                          p_sb[a % 2][:, unit, col:col + N - q0],
                                          start=b == 0, stop=b == NT - 1, skip_group_check=True)
                            if b == NT - 1:
                                last.then_inc(u_ready, 1)
                        elif kind == "MS":
                            n = w_seq(i, kind, a)
                            pe.wait_ge(*w_free(i, n))
                            pe.wait_ge(o_squared, i * HG + HG + START)
                            for hg in range(HG):
                                last = mm(w_unit(i, n)[DV * hg:DV * hg + DV, :], head_mean[:],
                                          o_sq[:, hg, :], start=True, stop=True, skip_group_check=True)
                            last.then_inc(w_ready, 1)
                        elif kind == "MB":
                            n = w_seq(i, kind, a)
                            pe.wait_ge(*w_free(i, n))
                            pe.wait_ge(r_ready, i + 1)
                            rows = slice(DV * a, DV * a + DV)
                            mm(w_unit(i, n), head_rows[rows, :], r_rms[rows, :], start=True, stop=True)\
                                .then_inc(w_ready, 1)
                        elif kind == "WO":
                            n = w_seq(i, kind, a)
                            if w_reused(i, n):
                                pe.wait_ge(*w_free(i, n))
                            if a == 0:
                                pe.wait_ge(on_ready, i * HG + HG)
                            for k in range(2):
                                qt = 2 * a + k
                                last = products(w_unit(i, n)[:, D * k:D * k + D], [
                                    (on[x][:, hg, P * qt:P * qt + P], w_o[y][:, hg, :])
                                    for hg in range(HG) for x, y in PARTS])
                            last.then_inc(w_ready, 1)
                        elif kind == "XNT":
                            n = w_seq(i, kind, a)
                            if w_reused(i, n):
                                pe.wait_ge(*w_free(i, n))
                            pe.wait_ge(xn_ready, 2 * i + 1)
                            for k in range(NT):
                                last = nc.tensor.transpose(w_unit(i, n)[:, P * k:P * k + P],
                                                           xn_f[:, k, P * a:P * a + P], ident[:])
                            last.then_inc(w_ready, 1)
                        elif kind == "L2":
                            n = s_seq(kind, a)
                            pe.wait_ge(*s_free(i, n))
                            if a == 0:
                                pe.wait_ge(*w_by_dve(i, w_seq(i, "XNT", 1) + 1))
                            products(s_bank(n), [
                                (sn_t[x][:, c, P * a:P * a + P], xn_t[y][:, c, :])
                                for c in range(DC) for x, y in PARTS]).then_inc(s_ready, 1)
                        elif kind == "L1":
                            for k in range(2):
                                n = s_seq(kind, a, k)
                                pe.wait_ge(*s_free(i, n))
                                products(s_bank(n), [
                                    (xn_t[x][:, c, P * a:P * a + P], sn_t[y][:, c, 512 * k:512 * k + 512])
                                    for c in range(DC) for x, y in PARTS]).then_inc(s_ready, 1)
                        elif kind == "TD":
                            n = w_seq(i, kind, a)
                            if w_reused(i, n):
                                pe.wait_ge(*w_free(i, n))
                            pe.wait_ge(ed_ready, i * E + a + 1)
                            for k in range(NT):
                                last = nc.tensor.transpose(w_unit(i, n)[:, P * k:P * k + P],
                                                           ed_t[:, a % 4, P * k:P * k + P], ident[:])
                            last.then_inc(w_ready, 1)
                        elif kind == "SL":
                            n = u_seq(kind, a, b)
                            pe.wait_ge(*u_free(i, n))
                            if b == 0:
                                pe.wait_ge(*w_by_dve(i, w_seq(i, "TD", 4 * a + 3) + 1))
                            if (a, b) == (0, 0):
                                pe.wait_ge(xn_ready, 2 * i + 2)
                            products(u_bank(n), [
                                (xn[x][:, k, P * b:P * b + P], disp[y][:, k, 512 * a:512 * a + 512])
                                for k in range(NT) for x, y in PARTS]).then_inc(u_ready, 1)

                turn(-1, FIRST)
                with pe.Fori(0, NB - 1) as i:
                    turn(i, TURN)
                turn(NB - 1, LAST)

            @block.sync
            def _(sp):
                def turn(i, schedule):
                    for kind, a, b in schedule:
                        if kind == "XL":
                            if not ahead(i):
                                sp.wait_ge(xt_split, 2 * (i + 1))
                                sp.nop(nofuse=True)
                            if not last_turn(i):
                                sp.dma_start(x_raw[:], t["x_t"][bass.ds(i + 1, 1)].rearrange(
                                    "o (c p) n -> p (o c) n", p=P)).then_inc(xt_in, 16)
                            if not ahead(i):
                                sp.dma_start(x_res[:], t["x"][bass.ds(i, 1)].rearrange(
                                    "o (k p) d -> p (o k) d", p=P)).then_inc(xres_in, 16)
                        elif kind == "QK":
                            sp.wait_ge(*w_by_dve(i, w_seq(i, kind, a) + 1))
                            qk, hg, pos = a // HG, a % HG, QK_ORDER.index(a)
                            sp.dma_start(qk_scr[qk, :, P * hg:P * hg + P, :].rearrange("l p n -> p l n"),
                                         stage[pos % 3][:].bitcast(F32)).then_inc(stage_out[pos % 3], 16)
                            if pos in (1, 7):
                                for k in range(min(3, pos + 1)):
                                    sp.wait_ge(stage_out[k], 16 * ((i + 1) * STAGE_USES[k]
                                                                   + len(range(k, pos + 1, 3))))
                                    sp.nop(nofuse=True)
                                if not ahead(i):
                                    sp.wait_ge(s_ready, i * NS + s_seq("B", 1 if pos == 1 else 7, B_UNITS - 1) + 1)
                                    sp.nop(nofuse=True)
                                loaded, g0, g1 = (stack_first, 0, 1) if pos == 1 else (stack_rest, 1, HG)
                                for q in range(2):
                                    view = qk_scr[q].rearrange("l (h m r) n -> l m r h n", m=2, r=DH)
                                    for m in range(2):
                                        for k, part in enumerate(STACK_PARTS[q]):
                                            r = 64 * m + DH * k
                                            sp.dma_start(
                                                stacks[q][r:r + DH, 4 * g0:4 * g1, :].bitcast(F32),
                                                view[part, m, :, 4 * g0:4 * g1]).then_inc(loaded, 16)
                        elif kind == "T":
                            n = w_seq(i, kind, a)
                            sp.wait_ge(*w_by_act(i, n + 1))
                            r = 64 * (a % 2) + 49
                            sp.dma_start(q_stack[r:r + 1, 4 * (a // 2):4 * (a // 2) + 4, :].bitcast(F32)
                                         .rearrange("p h (k n) -> p (h k) n", n=P),
                                         m_row[:, a % 2, :].bitcast(F32)).then_inc(m_row_in[a % 2], 16)
                        elif kind == "XNT" and a == 0:
                            sp.wait_ge(x_ready, i + 1)
                            sp.nop(nofuse=True)
                            sp.dma_start(x_scr[bass.ds(i, 1)].rearrange("o p k d -> p (o k) d"), x_res[:])\
                                .then_inc(x_out, 16)
                        elif kind == "SL":
                            sp.wait_ge(*u_by_act(i, u_seq(kind, a, b) + 1))
                            sp.nop(nofuse=True)
                            sp.dma_start(
                                sl_scr[4 * a:4 * a + 4, b, :, bass.ds(i, 1), :]
                                .rearrange("e p o s -> p (e o) s"),
                                slots[:, b, :].rearrange("p (e s) -> p e s", e=4)).then_inc(slots_out[b], 16)
                        elif kind == "CN":
                            sp.wait_ge(ec_ready, i * NT + a + 1)
                            sp.nop(nofuse=True)
                            sp.dma_start(ec_scr[bass.ds(i, 1), a].rearrange("o p m -> (o p) m"),
                                         e_c[a % 2][:]).then_inc(ec_out[a % 2], 16)
                    if ahead(i):
                        return
                    sp.wait_ge(xn_ready, 2 * i + 2)
                    sp.nop(nofuse=True)
                    for c in range(DC):
                        sp.wait_ge(slots_out[c], 32 * i + 32)
                        sp.nop(nofuse=True)
                    for k in range(2):
                        sp.wait_ge(ec_out[k], 32 * i + 32)
                        sp.nop(nofuse=True)
                    sp.wait_ge(x_out, 16 * i + 16)
                    sp.nop(nofuse=True)

                turn(-1, FIRST)
                with sp.Fori(0, NB - 1) as i:
                    turn(i, TURN)
                turn(NB - 1, LAST)

            @block.scalar
            def _(act):
                ac = nc.scalar.activation
                def turn(i, schedule):
                    for kind, a, b in schedule:
                        if kind in W_READER:
                            n = w_seq(i, kind, a, b)
                        if kind == "QK":
                            pos = QK_ORDER.index(a)
                            if pos >= 3:
                                act.wait_ge(stage_out[pos % 3],
                                            16 * ((i + 1) * STAGE_USES[pos % 3] + pos // 3))
                            act.wait_ge(*w_made(i, n))
                            ac(stage[pos % 3][:, 0, :], w_unit(i, n), ACT.Copy).then_inc(qk_hi, 1)
                        elif kind == "VP":
                            act.wait_ge(*w_made(i, n))
                            ac(v_sb[:, a, :], w_unit(i, n), ACT.Copy).then_inc(w_act, 1)
                        elif kind == "T":
                            act.wait_ge(*w_made(i, n))
                            ac(m_row[:, a % 2, :], w_unit(i, n)[0:16, 0:P], ACT.Copy).then_inc(w_act, 1)
                        elif kind == "B":
                            n = s_seq(kind, a, b)
                            if b == 0 and a >= 2:
                                act.wait_ge(u_ready, i * NU + 2 * (a - 1))
                            act.wait_ge(s_ready, i * NS + n + 1)
                            ac(p_sb[a % 2][:, b // 2, 512 * (b % 2):512 * (b % 2) + 512], s_bank(n),
                               ACT.Exp, scale=float(DH) ** -0.5).then_inc(s_done, 1)
                        elif kind in ("PVS", "PVV") and a % 2 == 0 and b == NT - 1:
                            n = u_seq(kind, a)
                            if kind == "PVS":
                                act.wait_ge(o_squared, i * HG + a // 2 + START)
                            act.wait_ge(u_ready, i * NU + n + 1)
                            ac(o_tmp[:, 0 if kind == "PVS" else 1, :], u_bank(n), ACT.Copy)\
                                .then_inc(u_act, 1)
                        elif kind == "SQ":
                            act.wait_ge(o_ready, i * HG + a + 1)
                            ac(o_sq[:, a, :], o_sq[:, a, :], ACT.Square, scale=EPS ** 0.5)
                            ac(o_tmp[:, 1, :], o_sb[:, a, :], ACT.Square).then_inc(squares, 1)
                        elif kind == "MS":
                            act.wait_ge(*w_made(i, n))
                            ac(r_rms, w_unit(i, n), ACT.Sqrt).then_inc(w_act, 1)
                        elif kind == "XNT":
                            act.wait_ge(*w_made(i, n))
                            ac(xn_t[0][:, a, :], w_unit(i, n), ACT.Copy).then_inc(xnt_hi, 1)
                        elif kind == "L2":
                            n = s_seq(kind, a)
                            if a >= 4:
                                act.wait_ge(*w_made(i, w_seq(i, "TD", a - 4)))
                            act.wait_ge(gneg_ready, i * E + a + 1)
                            ac(ed_t[:, a % 4, :], s_bank(n), ACT.Exp, bias=small[:, 16 + a:17 + a],
                               accum_out=small[:, 24 + a:25 + a]).then_inc(s_done, 1)
                        elif kind == "L1":
                            if a >= 2:
                                act.wait_ge(ec_out[a % 2], 32 * i + 16)
                            act.wait_ge(cneg_ready, i * NT + a + 1)
                            for k in range(2):
                                ac(e_c[a % 2][:, 512 * k:512 * k + 512], s_bank(s_seq(kind, a, k)), ACT.Exp,
                                   bias=small[:, 44 + a:45 + a],
                                   accum_out=small[:, 68 + 2 * a + k:69 + 2 * a + k]).then_inc(s_done, 1)
                        elif kind == "TD":
                            if a == 0 and not last_turn(i):
                                for k in range(3):
                                    act.wait_ge(stage_out[k], 16 * (i + 2) * STAGE_USES[k])
                            act.wait_ge(*w_made(i, n))
                            ac(disp[0][:, :, P * a:P * a + P], w_unit(i, n).rearrange("p (k m) -> p k m", m=P),
                               ACT.Copy).then_inc(td_hi, 1)
                        elif kind == "SL":
                            n = u_seq(kind, a, b)
                            if a:
                                act.wait_ge(slots_out[b], 32 * i + 16)
                            act.wait_ge(u_ready, i * NU + n + 1)
                            ac(slots[:, b, :], u_bank(n), ACT.Copy).then_inc(u_act, 1)

                act.sem_inc(s_done, S_START)
                act.sem_inc(u_act, START)
                turn(-1, FIRST)
                with act.Fori(0, NB - 1) as i:
                    turn(i, TURN)
                turn(NB - 1, LAST)

            @block.gpsimd
            def _(pool):
                g = nc.gpsimd
                def turn(i, schedule):
                    for kind, a, b in schedule:
                        if kind == "B":
                            pool.wait_ge(*s_by_act(i, s_seq(kind, a, b) + 1))
                            pool.nop(nofuse=True)
                            unit = p_sb[a % 2][:, b // 2, 512 * (b % 2):512 * (b % 2) + 512]
                            firsts = [col // P for _, _, col in b_pieces(b)]
                            tiles = unit.rearrange("p (k n) -> p k n", n=P)[
                                :, 0::(firsts[-1] or NT), :]
                            g.affine_select(out=tiles, in_=tiles, compare_op=ALU.is_ge, fill=0.0, base=0,
                                            pattern=[[0, tiles.shape[1]], [1, P]],
                                            channel_multiplier=-1).then_inc(masked, 1)
                        elif kind == "SQ":
                            pool.wait_ge(squares, i * HG + a + 1)
                            g.tensor_tensor(o_sq[:, a, :], o_sq[:, a, :], o_tmp[:, 1, :], ALU.add)\
                                .then_inc(o_squared, 1)
                        elif kind == "WO" and a == 1:
                            pool.wait_ge(stats_ready, i + 1)
                            pool.nop(nofuse=True)
                            g.tensor_scalar(small[:, 0:4], aggr[:, :, 1], EPS, None, ALU.add)\
                                .then_inc(chain_p, 1)
                            pool.wait_ge(chain_p, i + 1)
                            g.tensor_tensor(small[:, 4:8], small[:, 0:4], powers[:, 0:4], ALU.pow)\
                                .then_inc(rstd_ready, 1)
                            pool.wait_ge(sq_ready, i + 1)
                            g.tensor_tensor(small[:, 56:60], sumsq[:], powers[:, 4:8], ALU.pow)\
                                .then_inc(norm_ready, 1)

                pool.sem_inc(o_squared, START)
                turn(-1, FIRST)
                with pool.Fori(0, NB - 1) as i:
                    turn(i, TURN)
                turn(NB - 1, LAST)

            @block.vector
            def _(dve):
                v = nc.vector
                LINKS = 28
                def turn(i, schedule):
                    n_links = [0]

                    def link(ins):
                        n_links[0] += 1
                        ins.then_inc(chain_d, 1)
                        dve.wait_ge(chain_d, i * LINKS + n_links[0])

                    for kind, a, b in schedule:
                        if kind in W_READER:
                            n = w_seq(i, kind, a, b)
                        if kind == "XS":
                            if not ahead(i):
                                dve.wait_ge(u_ready, i * NU + u_seq("PVV", STEPS - 2) + 1)
                            dve.wait_ge(xt_in, 16 * (i + 1) + 16)
                            v.tensor_copy(x_t[0][:], x_raw[:]).then_inc(xt_split, 1)
                            dve.wait_ge(xt_split, 2 * (i + 1) + 1)
                            lo_part(v, x_t[1][:], x_raw[:], x_t[0][:]).then_inc(xt_split, 1)
                        elif kind == "QK":
                            pos = QK_ORDER.index(a)
                            dve.wait_ge(qk_hi, 8 * (i + 1) + pos + 1)
                            lo_part(v, stage[pos % 3][:, 1, :], w_unit(i, n), stage[pos % 3][:, 0, :])\
                                .then_inc(w_dve, 1)
                        elif kind == "A":
                            dve.wait_ge(*w_made(i, n))
                            dve.nop(nofuse=True)
                            for h, qt, col in A_PIECES[b]:
                                keys = P * (qt + 1)
                                last = v.tensor_tensor_reduce(
                                    out=w_unit(i, n)[:, col:col + keys], in0=w_unit(i, n)[:, col:col + keys],
                                    in1=mask_a[:, N - keys:N], scale=1.0, scalar=-3e38, op0=ALU.add,
                                    op1=ALU.max, accum_out=m_col[:, a, 4 * h + qt:4 * h + qt + 1])
                            last.then_inc(w_dve, 1)
                        elif kind == "PVS" and a % 2 and b == NT - 1:
                            n = u_seq(kind, a)
                            dve.wait_ge(*u_by_act(i, n))
                            dve.wait_ge(u_ready, i * NU + n + 1)
                            v.tensor_tensor(o_sq[:, a // 2, :], o_tmp[:, 0, :], u_bank(n), ALU.mult)
                            v.tensor_tensor(o_tmp[:, 1, :], o_tmp[:, 1, :], u_bank(n), ALU.mult)\
                                .then_inc(u_dve, 1)
                        elif kind == "PVV" and a % 2 and b == NT - 1:
                            n, hg = u_seq(kind, a), a // 2
                            dve.wait_ge(*u_by_dve(i, n))
                            dve.wait_ge(u_ready, i * NU + n + 1)
                            v.scalar_tensor_tensor(o_tmp[:, 0, :], u_bank(n), neg_lam[:, hg:hg + 1],
                                                   o_tmp[:, 0, :], ALU.mult, ALU.mult).then_inc(u_dve, 1)
                            dve.wait_ge(*u_by_dve(i, n + 1))
                            v.tensor_tensor(o_sb[:, hg, :], o_tmp[:, 0, :], o_tmp[:, 1, :], ALU.add)\
                                .then_inc(o_ready, 1)
                        elif kind == "MS":
                            dve.wait_ge(*w_by_act(i, n + 1))
                            v.reciprocal(r_rms, r_rms).then_inc(r_ready, 1)
                        elif kind == "MB":
                            dve.wait_ge(*w_made(i, n))
                            v.tensor_tensor(o_sb[:, a, :], o_sb[:, a, :], w_unit(i, n), ALU.mult)\
                                .then_inc(w_dve, 1)
                            dve.wait_ge(*w_by_dve(i, n + 1))
                            link(v.tensor_copy(on[0][:, a, :], o_sb[:, a, :]))
                            lo_part(v, on[1][:, a, :], o_sb[:, a, :], on[0][:, a, :]).then_inc(on_ready, 1)
                        elif kind == "WO":
                            if a == 0:
                                dve.wait_ge(xres_in, 16 * i + 16)
                            dve.wait_ge(*w_made(i, n))
                            x2 = x_res[:, 2 * a:2 * a + 2, :]
                            v.tensor_tensor(x2, x2, w_unit(i, n).rearrange("p (k d) -> p k d", d=D), ALU.add)\
                                .then_inc(w_dve, 1)
                            dve.wait_ge(*w_by_dve(i, n + 1))
                            for k in range(2 * a, 2 * a + 2):
                                last = v.bn_stats(stat[:, k, :], x_res[:, k, :])
                            if a == 1:
                                link(last)
                                dve.nop(nofuse=True)
                                for k in range(NT):
                                    last = v.bn_aggr(aggr[:, k, :], stat[:, k, :])
                                last.then_inc(stats_ready, 1)
                        elif kind == "LN" and a == 0:
                            dve.wait_ge(rstd_ready, i + 1)
                            for k in range(NT):
                                last = v.tensor_scalar(x_res[:, k, :], x_res[:, k, :], aggr[:, k, 0:1],
                                                       small[:, 4 + k:5 + k], ALU.subtract, ALU.mult)
                            last.then_inc(x_ready, 1)
                            dve.wait_ge(x_ready, i + 1)
                            for k in range(NT):
                                last = v.tensor_tensor_reduce(
                                    out=xn_f[:, k, :], in0=x_res[:, k, :], in1=x_res[:, k, :], scale=1.0,
                                    scalar=0.0, op0=ALU.mult, op1=ALU.add, accum_out=sumsq[:, k:k + 1])
                            last.then_inc(sq_ready, 1)
                        elif kind == "LN" and a == 1:
                            dve.wait_ge(norm_ready, i + 1)
                            link(v.tensor_scalar(small[:, 56:60], small[:, 56:60], 1e-12,
                                                 float(D) ** -0.5, ALU.max, ALU.mult))
                            link(v.reciprocal(small[:, 0:4], small[:, 56:60]))
                            for k in range(NT):
                                last = v.scalar_tensor_tensor(xn_f[:, k, :], x_res[:, k, :],
                                                              small[:, k:k + 1], gamma[:],
                                                              ALU.mult, ALU.mult)
                            last.then_inc(xn_ready, 1)
                        elif kind == "LN":
                            dve.wait_ge(xn_ready, 2 * i + 1)
                            link(v.tensor_copy(xn[0][:], xn_f[:]))
                            lo_part(v, xn[1][:], xn_f[:], xn[0][:]).then_inc(xn_ready, 1)
                        elif kind == "XNT":
                            dve.wait_ge(xnt_hi, 2 * i + a + 1)
                            lo_part(v, xn_t[1][:, a, :], w_unit(i, n), xn_t[0][:, a, :]).then_inc(w_dve, 1)
                        elif kind == "L2":
                            dve.wait_ge(s_ready, i * NS + s_seq(kind, a) + 1)
                            v.reduce_max(small[:, 16 + a:17 + a], s_bank(s_seq(kind, a)), AX.X,
                                         negate=True).then_inc(gneg_ready, 1)
                        elif kind == "DN":
                            dve.wait_ge(*s_by_act(i, s_seq("L2", a) + 1))
                            link(v.reciprocal(small[:, 32 + a:33 + a], small[:, 24 + a:25 + a]))
                            v.tensor_scalar(ed_t[:, a % 4, :], ed_t[:, a % 4, :], small[:, 32 + a:33 + a],
                                            None, ALU.mult).then_inc(ed_ready, 1)
                        elif kind == "L1":
                            for k in range(2):
                                n, col = s_seq(kind, a, k), 60 + 2 * a + k
                                dve.wait_ge(s_ready, i * NS + n + 1)
                                last = v.reduce_max(small[:, col:col + 1], s_bank(n), AX.X)
                            link(last)
                            v.reduce_max(small[:, 44 + a:45 + a], small[:, 60 + 2 * a:62 + 2 * a], AX.X,
                                         negate=True).then_inc(cneg_ready, 1)
                        elif kind == "CN":
                            dve.wait_ge(*s_by_act(i, s_seq("L1", a, 1) + 1))
                            link(v.reduce_sum(small[:, 48 + a:49 + a], small[:, 68 + 2 * a:70 + 2 * a], AX.X))
                            link(v.reciprocal(small[:, 52 + a:53 + a], small[:, 48 + a:49 + a]))
                            v.tensor_scalar(e_c[a % 2][:], e_c[a % 2][:], small[:, 52 + a:53 + a], None,
                                            ALU.mult).then_inc(ec_ready, 1)
                        elif kind == "TD":
                            hi, lo = (disp[hl][:, :, P * a:P * a + P] for hl in range(2))
                            dve.wait_ge(td_hi, i * E + a + 1)
                            lo_part(v, lo, w_unit(i, n).rearrange("p (k m) -> p k m", m=P), hi)\
                                .then_inc(w_dve, 1)
                    assert ahead(i) or n_links[0] == LINKS, n_links[0]

                dve.sem_inc(u_dve, START)
                turn(-1, FIRST)
                with dve.Fori(0, NB - 1) as i:
                    turn(i, TURN)
                turn(NB - 1, LAST)

        if stop_after == 1:
            return

        at = base
        w1_raw, at = place("w1_raw", [P, DC, HID], F32, at)
        w2_raw, at = place("w2_raw", [P, HC, D], F32, at)
        sl_raw, at = place("sl_raw", [P, DC, NB * S], F32, at)
        w1_p, w2_p, sl_p, h_p, h_f, b1_sb, b2_sb, eo_sb = [[], []], [[], []], [[], []], [[], []], [], [], [], []
        for k in range(2):
            for hl in range(2):
                tensor, at = place(f"w1_p{k}{hl}", [P, DC, HID], F32R, at)
                w1_p[k].append(tensor)
                tensor, at = place(f"w2_p{k}{hl}", [P, HC, D], F32R, at)
                w2_p[k].append(tensor)
                tensor, at = place(f"sl_p{k}{hl}", [P, DC, NB * S], F32R, at)
                sl_p[k].append(tensor)
                tensor, at = place(f"h_p{k}{hl}", [P, HC, 512], F32R, at)
                h_p[k].append(tensor)
            tensor, at = place(f"h_f{k}", [P, 1024], F32, at)
            h_f.append(tensor)
            tensor, at = place(f"b1_sb{k}", [P, HC], F32, at)
            b1_sb.append(tensor)
            tensor, at = place(f"b2_sb{k}", [P, D], F32, at)
            b2_sb.append(tensor)
            tensor, at = place(f"eo_sb{k}", [P, 2, D], F32, at)
            eo_sb.append(tensor)
        assert at <= nc.sbuf_usable_end
        raw_split, split_link, h_ready, h_done, h_hi, h_split, eo_ready, eo_done = (
            sem(x) for x in ("raw_split split_link h_ready h_done h_hi h_split eo_ready "
                             "eo_done").split())
        raw_in = [sem(f"raw_in{q}") for q in range(3)]
        bias_in = [sem(f"bias_in{k}") for k in range(2)]
        eo_out = [sem(f"eo_out{k}") for k in range(2)]
        PAIRS = E // 2
        PAIR_ORDER = []
        for k in range(2):
            for hf in range(2):
                for u in range(4):
                    PAIR_ORDER.append(("H", k, hf, u))
                    if (hf, u) in ((0, 1), (0, 3)):
                        PAIR_ORDER.append(("SPLIT", k, 0, u // 2))
            PAIR_ORDER += [("EO", k, 0, 0), ("EO", k, 0, 1), ("SPLIT", k, 0, 2),
                           ("EO", k, 1, 0), ("EO", k, 1, 1)]
        H_UNITS = [x for x in PAIR_ORDER if x[0] == "H"]
        EO_UNITS = [x for x in PAIR_ORDER if x[0] == "EO"]
        NH, NE = len(H_UNITS), len(EO_UNITS)
        raws = [(w1_raw, w1_p), (sl_raw, sl_p), (w2_raw, w2_p)]

        with nc.Block() as block:

            @block.sync
            def _(sp):
                def load(expert, k, biases_used=True):
                    one = bass.ds(expert, 1)
                    sources = [t["w1"][one].rearrange("o (c p) h -> p (o c) h", p=P),
                               sl_scr[one].rearrange("o c p b s -> p (o c) (b s)"),
                               t["w2"][one].rearrange("o (c p) d -> p (o c) d", p=P)]
                    for q, (raw, _) in enumerate(raws):
                        sp.wait_ge(raw_split, 3 * expert + q + START)
                        sp.nop(nofuse=True)
                        sp.dma_start(raw[:], sources[q]).then_inc(raw_in[q], 16)
                    if biases_used:
                        sp.wait_ge(eo_done, NE // 2 * (expert - 1) + START)
                        sp.nop(nofuse=True)
                    sp.dma_start(b1_sb[k][:], t["b1"][one].rearrange("o p c -> (o p) c"))\
                        .then_inc(bias_in[k], 16)
                    sp.dma_start(b2_sb[k][:], t["b2"][one].rearrange("o p d -> (o p) d"))\
                        .then_inc(bias_in[k], 16)

                load(0, 0, biases_used=False)
                with sp.Fori(0, PAIRS - 1) as i:
                    load(2 * i + 1, 1)
                    load(2 * i + 2, 0)
                load(E - 1, 1)

            @block.gpsimd
            def _(pool):
                for k in range(2):
                    pool.dma_start(start_scr[k], ident[0:16, 0:16]).then_inc(eo_out[k], 16 * START)
                with pool.Fori(0, PAIRS) as i:
                    for n, (_, k, hf, u) in enumerate(EO_UNITS):
                        pool.wait_ge(eo_done, i * NE + n + 1 + START)
                        pool.nop(nofuse=True)
                        b0 = 4 * hf + 2 * u
                        pool.dma_start(eo_scr[b0:b0 + 2, :, bass.ds(2 * i + k, 1), :]
                                       .rearrange("b s e d -> s (b e) d"), eo_sb[n % 2][:])\
                            .then_inc(eo_out[n % 2], 16)
                for k in range(2):
                    pool.wait_ge(eo_out[k], 16 * START + 16 * PAIRS * NE // 2)

            @block.tensor
            def _(pe):
                mm = nc.tensor.matmul

                def products(out, pairs):
                    for q, (stationary, moving) in enumerate(pairs):
                        last = mm(out, stationary, moving, start=q == 0, stop=q == len(pairs) - 1)
                    return last

                with pe.Fori(0, PAIRS) as i:
                    for kind, k, hf, u in PAIR_ORDER:
                        if kind == "H":
                            n = H_UNITS.index((kind, k, hf, u))
                            if (hf, u) == (0, 0):
                                pe.wait_ge(raw_split, 6 * i + 3 * k + 2 + START)
                            pe.wait_ge(h_done, i * NH + max(n - 1, 0) + START)
                            for q in range(2):
                                hc = 2 * u + q
                                last = products(s_unit(n)[:, q, :], [
                                    (w1_p[k][x][:, c, P * hc:P * hc + P],
                                     sl_p[k][y][:, c, 512 * hf:512 * hf + 512])
                                    for c in range(DC) for x, y in PARTS])
                            last.then_inc(h_ready, 1)
                        elif kind == "EO":
                            n = EO_UNITS.index((kind, k, hf, u))
                            if (hf, u) == (0, 0):
                                pe.wait_ge(raw_split, 6 * i + 3 * k + 3 + START)
                            pe.wait_ge(h_split, i * NH + 8 * k + 4 * hf + 4 + START)
                            pe.wait_ge(eo_done, i * NE + max(n - 1, 0) + START)
                            for q in range(2):
                                s0 = P * (2 * u + q)
                                last = products(w_bank(n)[:, D * q:D * q + D], [
                                    (h_p[hf][x][:, hc, s0:s0 + P], w2_p[k][y][:, hc, :])
                                    for hc in range(HC) for x, y in PARTS])
                            last.then_inc(eo_ready, 1)

            @block.scalar
            def _(act):
                act.sem_inc(h_done, START)
                with act.Fori(0, PAIRS) as i:
                    for n, (_, k, hf, u) in enumerate(H_UNITS):
                        if (hf, u) == (0, 0):
                            act.wait_ge(bias_in[k], 32 * i + 32)
                        act.wait_ge(h_split, i * NH + max(n - 1, 0) + START)
                        act.wait_ge(h_ready, i * NH + n + 1)
                        for q in range(2):
                            hc = 2 * u + q
                            last = nc.scalar.activation(h_f[n % 2][:, 512 * q:512 * q + 512],
                                                        s_unit(n)[:, q, :], ACT.Gelu,
                                                        bias=b1_sb[k][:, hc:hc + 1])
                        last.then_inc(h_done, 1)

            @block.vector
            def _(dve):
                v = nc.vector

                def split_raw(expert, k, q):
                    raw, parts = raws[q]
                    dve.wait_ge(raw_in[q], 16 * expert + 16)
                    v.tensor_copy(parts[k][0][:], raw[:]).then_inc(split_link, 1)
                    dve.wait_ge(split_link, 3 * expert + q + 1)
                    lo_part(v, parts[k][1][:], raw[:], parts[k][0][:]).then_inc(raw_split, 1)

                def turn(i, more):
                    for kind, k, hf, u in PAIR_ORDER:
                        if kind == "SPLIT":
                            if k == 0 or more:
                                split_raw(2 * i + k + 1, 1 - k, u)
                        elif kind == "H":
                            n = H_UNITS.index((kind, k, hf, u))
                            hi, lo = (h_p[hf][hl][:, 2 * u:2 * u + 2, :] for hl in range(2))
                            src = h_f[n % 2][:].rearrange("p (c n) -> p c n", c=2)
                            dve.wait_ge(h_done, i * NH + n + 1 + START)
                            v.tensor_copy(hi, src).then_inc(h_hi, 1)
                            dve.wait_ge(h_hi, i * NH + n + 1)
                            lo_part(v, lo, src, hi).then_inc(h_split, 1)
                        else:
                            n = EO_UNITS.index((kind, k, hf, u))
                            dve.wait_ge(eo_out[n % 2], 16 * (i * (NE // 2) + n // 2 + START))
                            dve.wait_ge(eo_ready, i * NE + n + 1)
                            for q in range(2):
                                last = v.tensor_tensor(eo_sb[n % 2][:, q, :],
                                                       w_bank(n)[:, D * q:D * q + D], b2_sb[k][:], ALU.add)
                            last.then_inc(eo_done, 1)

                for x in (raw_split, h_split, eo_done):
                    dve.sem_inc(x, START)
                for q in range(3):
                    split_raw(0, 0, q)
                with dve.Fori(0, PAIRS - 1) as i:
                    turn(i, True)
                turn(PAIRS - 1, False)

        if stop_after == 2:
            return

        at = base
        ec_in, eo_in, x_in, ec_p, eo_p = [], [], [], [[], []], [[], []]
        for k in range(2):
            tensor, at = place(f"ec_in{k}", [P, NT, M], F32, at)
            ec_in.append(tensor)
            tensor, at = place(f"eo_in{k}", [P, E, D], F32, at)
            eo_in.append(tensor)
            tensor, at = place(f"x_in{k}", [P, NT, D], F32, at)
            x_in.append(tensor)
            for hl in range(2):
                tensor, at = place(f"ec_p{k}{hl}", [P, E, N], F32R, at)
                ec_p[k].append(tensor)
                tensor, at = place(f"eo_p{k}{hl}", [P, E, D], F32R, at)
                eo_p[k].append(tensor)
        stat3, at = place("stat3", [P, 2, NT, 6], F32, at)
        aggr3, at = place("aggr3", [P, 2, NT, 2], F32, at)
        var3, at = place("var3", [P, 2, NT], F32, at)
        rstd3, at = place("rstd3", [P, 2, NT], F32, at)
        assert at <= nc.sbuf_usable_end
        (te_ready, te_hi, te_done, eo_hi, eo_split, y_ready, y_done, chain3, stats3_ready, rstd3_ready,
         chain3_p, ln_done) = (sem(x) for x in (
             "te_ready te_hi te_done eo_hi eo_split y_ready y_done chain3 stats3_ready rstd3_ready "
             "chain3_p ln_done").split())
        ec_loaded = [sem(f"ec_loaded{k}") for k in range(2)]
        eo_loaded = [sem(f"eo_loaded{k}") for k in range(2)]
        x_loaded = [sem(f"x_loaded{k}") for k in range(2)]
        out_stored = [sem(f"out_stored{k}") for k in range(2)]

        PREPARE3 = [("ES", 0, 0)] + [("TE", 0, u) for u in range(E)]
        ORDER3 = woven("YTTYETTYTTYTT", {"Y": [("Y", 0, u) for u in range(NT)], "E": [("ES", 1, 0)],
                                         "T": [("TE", 1, u) for u in range(E)]})
        ORDER3 += [("LN", 0, 0)]

        def batches(fori, work):
            work(-1, 1, -1, [(kind, 1, u) for kind, _, u in PREPARE3])
            with fori(0, NB // 2 - 1) as i:
                for k in range(2):
                    work(2 * i + k, k, i, ORDER3)
            work(NB - 2, 0, NB // 2 - 1, ORDER3)
            work(NB - 1, 1, NB // 2 - 1, [x for x in ORDER3 if x[1] == 0])

        with nc.Block() as block:

            @block.sync
            def _(sp):
                def load(batch, k, pair, reused=True):
                    one = bass.ds(batch, 1)
                    if reused:
                        sp.wait_ge(te_done, E * (batch - 1) + START)
                        sp.nop(nofuse=True)
                    sp.dma_start(ec_in[k][:], ec_scr[one].rearrange("o k p m -> p (o k) m"))\
                        .then_inc(ec_loaded[k], 16)
                    if reused:
                        sp.wait_ge(eo_split, batch - 1)
                        sp.nop(nofuse=True)
                    sp.dma_start(eo_in[k][:], eo_scr[one].rearrange("o s e d -> (o s) e d"))\
                        .then_inc(eo_loaded[k], 16)
                    if reused:
                        sp.wait_ge(out_stored[k], 16 * pair)
                        sp.nop(nofuse=True)
                    sp.dma_start(x_in[k][:], x_scr[one].rearrange("o p k d -> p (o k) d"))\
                        .then_inc(x_loaded[k], 16)

                for k in range(2):
                    load(k, k, 0, reused=False)
                with sp.Fori(0, NB // 2 - 1) as i:
                    for k in range(2):
                        load(2 * i + 2 + k, k, i + 1)

            @block.gpsimd
            def _(pool):
                g = nc.gpsimd
                with pool.Fori(0, NB // 2) as i:
                    for k in range(2):
                        pool.wait_ge(stats3_ready, 2 * i + k + 1)
                        pool.nop(nofuse=True)
                        g.tensor_scalar(var3[:, k, :], aggr3[:, k, :, 1], EPS, None, ALU.add)\
                            .then_inc(chain3_p, 1)
                        pool.wait_ge(chain3_p, 2 * i + k + 1)
                        g.tensor_tensor(rstd3[:, k, :], var3[:, k, :], powers[:, 0:4], ALU.pow)\
                            .then_inc(rstd3_ready, 1)
                        pool.wait_ge(ln_done, 2 * i + k + 1)
                        pool.nop(nofuse=True)
                        pool.dma_start(out[bass.ds(2 * i + k, 1)].rearrange("o (k p) d -> p (o k) d", p=P),
                                       x_in[k][:]).then_inc(out_stored[k], 16)
                for k in range(2):
                    pool.wait_ge(out_stored[k], 16 * NB // 2)

            @block.tensor
            def _(pe):
                mm = nc.tensor.matmul

                def work(batch, k, pair, order):
                    for kind, ahead_by, u in order:
                        if kind == "TE":
                            b, kb, pb = batch + 1, 1 - k, pair + k
                            if u == 0:
                                pe.wait_ge(ec_loaded[kb], 16 * pb + 16)
                            pe.wait_ge(te_done, E * b + max(u - 1, 0) + START)
                            for q in range(NT):
                                last = nc.tensor.transpose(w_bank(u)[:, P * q:P * q + P],
                                                           ec_in[kb][:, q, P * u:P * u + P], ident[:])
                            last.then_inc(te_ready, 1)
                        elif kind == "Y":
                            if u == 0:
                                pe.wait_ge(te_done, E * batch + E + START)
                                pe.wait_ge(eo_split, batch + 1)
                            pe.wait_ge(y_done, NT * batch + max(u - 1, 0) + START)
                            pairs = [(ec_p[k][x][:, j, P * u:P * u + P], eo_p[k][y][:, j, :])
                                     for j in range(E) for x, y in PARTS]
                            for q, (stationary, moving) in enumerate(pairs):
                                last = mm(u_bank(u)[:, 0:D], stationary, moving, start=q == 0,
                                          stop=q == len(pairs) - 1)
                            last.then_inc(y_ready, 1)

                batches(pe.Fori, work)

            @block.scalar
            def _(act):
                def work(batch, k, pair, order):
                    for kind, ahead_by, u in order:
                        b, kb, pb = batch + 1, 1 - k, pair + k
                        if kind == "ES":
                            if order is ORDER3:
                                act.wait_ge(y_ready, NT * batch + 1)
                            act.wait_ge(eo_loaded[kb], 16 * pb + 16)
                            nc.scalar.activation(eo_p[kb][0][:], eo_in[kb][:], ACT.Copy).then_inc(eo_hi, 1)
                        elif kind == "TE":
                            act.wait_ge(te_ready, E * b + u + 1)
                            nc.scalar.activation(ec_p[kb][0][:, u, :], w_bank(u), ACT.Copy)\
                                .then_inc(te_hi, 1)

                batches(act.Fori, work)

            @block.vector
            def _(dve):
                v = nc.vector
                for x in (te_done, y_done):
                    dve.sem_inc(x, START)

                def work(batch, k, pair, order):
                    for kind, ahead_by, u in order:
                        b, kb, pb = batch + 1, 1 - k, pair + k
                        if kind == "ES":
                            dve.wait_ge(eo_hi, b + 1)
                            lo_part(v, eo_p[kb][1][:], eo_in[kb][:], eo_p[kb][0][:]).then_inc(eo_split, 1)
                        elif kind == "TE":
                            dve.wait_ge(te_hi, E * b + u + 1)
                            lo_part(v, ec_p[kb][1][:, u, :], w_bank(u), ec_p[kb][0][:, u, :])\
                                .then_inc(te_done, 1)
                        elif kind == "Y":
                            x = x_in[k][:, u, :]
                            if u == 0:
                                dve.wait_ge(x_loaded[k], 16 * pair + 16)
                            dve.wait_ge(y_ready, NT * batch + u + 1)
                            v.tensor_tensor(x, x, u_bank(u)[:, 0:D], ALU.add).then_inc(y_done, 1)
                            dve.wait_ge(y_done, NT * batch + u + 1 + START)
                            last = v.bn_stats(stat3[:, k, u, :], x)
                            if u == NT - 1:
                                last.then_inc(chain3, 1)
                                dve.wait_ge(chain3, batch + 1)
                                dve.nop(nofuse=True)
                                for q in range(NT):
                                    last = v.bn_aggr(aggr3[:, k, q, :], stat3[:, k, q, :])
                                last.then_inc(stats3_ready, 1)
                        else:
                            dve.wait_ge(rstd3_ready, batch + 1)
                            for q in range(NT):
                                last = v.tensor_scalar(x_in[k][:, q, :], x_in[k][:, q, :],
                                                       aggr3[:, k, q, 0:1], rstd3[:, k, q:q + 1],
                                                       ALU.subtract, ALU.mult)
                            last.then_inc(ln_done, 1)

                batches(dve.Fori, work)


def layouts(L0_attn_X, L0_attn_Wq, L0_attn_Wk, L0_attn_Wv, L0_attn_Wo, L0_attn_lq1, L0_attn_lk1,
            L0_attn_lq2, L0_attn_lk2, L0_attn_rms_scale, L0_ffn_norm_gamma, L0_ffn_slot_norm_gamma,
            L0_ffn_slot_embeds, L0_ffn_w1, L0_ffn_b1, L0_ffn_w2, L0_ffn_b2):
    def tiled(w):
        return w.reshape(-1, P, w.shape[1]).transpose(1, 0, 2)

    def per_head(x):
        return np.repeat(x.reshape(HG, 4, DH).transpose(1, 0, 2), DV, axis=0)

    rows = np.arange(P)
    arrays = {
        "x": L0_attn_X, "x_t": L0_attn_X.transpose(0, 2, 1),
        "w_qk": np.stack([tiled(L0_attn_Wq.T), tiled(L0_attn_Wk.T)], axis=1),
        "w_v": tiled(L0_attn_Wv.T), "w_o": tiled(L0_attn_Wo.T),
        "lam_in": np.stack([per_head(x) for x in (L0_attn_lq1, L0_attn_lq2, L0_attn_lk1, L0_attn_lk2)], 1),
        "rms_col": np.tile(L0_attn_rms_scale, 4)[:, None],
        "gamma": np.broadcast_to(L0_ffn_norm_gamma, (P, D)),
        "slot_gamma": np.broadcast_to(L0_ffn_slot_norm_gamma, (P, D)),
        "slot": L0_ffn_slot_embeds.transpose(1, 0, 2),
        "w1": L0_ffn_w1, "w2": L0_ffn_w2,
        "b1": L0_ffn_b1.reshape(E, HC, P).transpose(0, 2, 1),
        "b2": np.broadcast_to(L0_ffn_b2[:, None, :], (E, P, D)),
        "ident": np.eye(P, dtype=np.float32),
        "head_mean": np.kron(np.eye(4), np.full((DV, DV // 4), 1 / DV)).astype(np.float32),
        "head_rows": np.tile(np.kron(np.eye(4), np.eye(DV // 4, 1) @ np.ones((1, DV))), (HG, 1))
        .astype(np.float32),
        "mask_a": np.concatenate([np.zeros((P, N - P)), np.where(rows[None] > rows[:, None], NEG, 0.0)],
                                 axis=1).astype(np.float32),
    }
    return {k: np.ascontiguousarray(v) for k, v in arrays.items()}


def kernel(**inputs):
    import concourse.bacc as bacc
    from concourse.bass_utils import run_bass_kernel_spmd

    nc = bacc.Bacc("TRN2", target_bir_lowering=False, num_devices=1)
    arrays = layouts(**{k: np.asarray(v) for k, v in inputs.items()})
    t = {k: nc.dram_tensor("in_" + k, v.shape, F32, kind="ExternalInput").ap() for k, v in arrays.items()}
    out = nc.dram_tensor("out", (NB, N, D), F32, kind="ExternalOutput").ap()
    layer(nc, t, out)
    result = run_bass_kernel_spmd(nc, [{"in_" + k: v for k, v in arrays.items()}], core_ids=[0])
    return result.results[0]["out"]
```
